# Optimizing a Trainium2 kernel written in Bass

```python
import numpy as np
import jax
import jax.numpy as jnp

def _softmax(x, axis=-1):
    return jax.nn.softmax(x, axis=axis)

def _gelu(x):
    return jax.nn.gelu(x, approximate=True)

def _silu(x):
    return jax.nn.silu(x)

def _sigmoid(x):
    return jax.nn.sigmoid(x)

def _layernorm(x, axis=-1, eps=1e-05):
    m = jnp.mean(x, axis=axis, keepdims=True)
    v = jnp.var(x, axis=axis, keepdims=True)
    return (x - m) / jnp.sqrt(v + eps)

def _scatter_add(tgt, idx, src, axis=0):
    return tgt.at[idx].add(src)

def _segment_sum(src, seg, n):
    return jax.ops.segment_sum(src, seg, n)
kernel_name = 'mk_adaln_attn_ffn_d2_seqx_r8_3396ed'

def setup_inputs(seed: int=0):
    np.random.seed(seed)
    _w = jnp.asarray

    def _rec_inputs():
        import jax
        import jax.numpy as jnp
        _rk = jax.random.key(seed)
        x = -0.000125 + 0.9999 * jax.random.normal(jax.random.fold_in(_rk, 1), (32, 128, 128), jnp.float32)
        _lenS = 128 - jax.random.randint(jax.random.fold_in(_rk, 7), (32,), 0, max(1, 128 // 4) + 1, jnp.int32)
        _lenS2 = 128 - jax.random.randint(jax.random.fold_in(_rk, 8), (32,), 0, max(1, 128 // 4) + 1, jnp.int32)
        cond_256 = -0.0209273 + 1.04763 * jax.random.normal(jax.random.fold_in(_rk, 11), (32, 32), jnp.float32)
        cond_64 = 0.0223021 + 1.01123 * jax.random.normal(jax.random.fold_in(_rk, 12), (32, 64), jnp.float32)
        return (x, cond_256, cond_64)
    x, cond_256, cond_64 = _rec_inputs()

    def _L0_cond_setup():
        import math
        import jax, jax.numpy as jnp
        import numpy as np
        from jax.scipy.linalg import cholesky, solve_triangular
        B, S, D, O, K, R = (4, 1024, 128, 128, 32, 64)

        def build_dct_basis(dim: int, num_bases: int) -> np.ndarray:
            num_bases = min(num_bases, dim)
            positions = np.arange(dim, dtype=np.float32)[None, :]
            modes = np.arange(num_bases, dtype=np.float32)[:, None]
            basis = np.cos(math.pi / float(dim) * (positions + 0.5) * modes)
            basis[0] = basis[0] / math.sqrt(2.0)
            basis = basis * math.sqrt(2.0 / float(dim))
            return basis.astype(np.float32)

        def _orthogonalize_mode_to_rank(raw: jnp.ndarray) -> jnp.ndarray:
            raw = raw.astype(jnp.float32)
            gram = raw.T @ raw
            eye = jnp.eye(raw.shape[1], dtype=jnp.float32)
            chol = cholesky(gram + 0.0001 * eye, lower=True)
            inv_chol = solve_triangular(chol, eye, lower=True)
            q = raw @ inv_chol.T
            signs = jnp.sign(jnp.sum(q * raw, axis=0, keepdims=True))
            signs = jnp.where(signs == 0, jnp.ones_like(signs), signs)
            return q * signs
        key = jax.random.key(seed)
        k1, k2, k3, k4, k5 = jax.random.split(key, 5)
        x = jax.random.normal(k1, (B, S, D), dtype=jnp.float32)
        spectral_coeff = jax.random.normal(k2, (B, K), dtype=jnp.float32)
        rank_coeff = jax.random.normal(k3, (B, R), dtype=jnp.float32)
        input_basis = jnp.asarray(build_dct_basis(D, K))
        diag = min(K, R)
        mode_to_rank = 0.02 * jax.random.normal(k4, (K, R), dtype=jnp.float32)
        mode_to_rank = mode_to_rank.at[:diag, :diag].add(jnp.eye(diag, dtype=jnp.float32))
        output_basis = 0.02 * jax.random.normal(k5, (R, O), dtype=jnp.float32)
        return {'x': x, 'spectral_coeff': spectral_coeff, 'rank_coeff': rank_coeff, 'input_basis': input_basis, 'mode_to_rank': mode_to_rank, 'output_basis': output_basis}
    _L0_cond_all = _L0_cond_setup()
    _L0_cond_in = {k: v for k, v in _L0_cond_all.items() if k in ('input_basis', 'mode_to_rank', 'output_basis')}
    del _L0_cond_all

    def _L0_attn_setup():
        import jax, jax.numpy as jnp
        import numpy as np
        D_MODEL = 128
        N_HEADS = 16
        D_HEAD = D_MODEL // N_HEADS
        B, T = (2, 256)
        EPS = 1e-05
        key = jax.random.key(seed)
        ks = jax.random.split(key, 5)
        s = 1.0 / np.sqrt(D_MODEL)
        return {'x': jax.random.normal(ks[0], (B, T, D_MODEL), dtype=jnp.float32), 'W_q': jax.random.normal(ks[1], (D_MODEL, D_MODEL), dtype=jnp.float32) * s, 'W_k': jax.random.normal(ks[2], (D_MODEL, D_MODEL), dtype=jnp.float32) * s, 'W_v': jax.random.normal(ks[3], (D_MODEL, D_MODEL), dtype=jnp.float32) * s, 'W_o': jax.random.normal(ks[4], (D_MODEL, D_MODEL), dtype=jnp.float32) * s, 'gn_weight': jnp.ones((D_MODEL,), dtype=jnp.float32), 'gn_bias': jnp.zeros((D_MODEL,), dtype=jnp.float32)}
    _L0_attn_all = _L0_attn_setup()
    _L0_attn_in = {k: v for k, v in _L0_attn_all.items() if k in ('W_q', 'W_k', 'W_v', 'W_o', 'gn_weight', 'gn_bias')}
    del _L0_attn_all

    def _L0_cond2_setup():
        import jax, jax.numpy as jnp
        import numpy as np
        TOP_K = 2
        EPS = 1e-06
        B, S, H, G, E, M = (2, 256, 128, 32, 8, 256)
        key = jax.random.key(seed)
        ks = jax.random.split(key, 16)
        s_h = 1.0 / np.sqrt(H)
        s_g = 1.0 / np.sqrt(G)
        s_m = 1.0 / np.sqrt(M)
        return {'x': jax.random.normal(ks[0], (B, S, H), jnp.float32), 'genre_embed': jax.random.normal(ks[1], (B, 1, G), jnp.float32), 'rms_w': jnp.ones((H,), jnp.float32), 'wg_W': jax.random.normal(ks[2], (H, E), jnp.float32) * s_h, 'wg_b': jnp.zeros((E,), jnp.float32), 'gg_W': jax.random.normal(ks[3], (G, E), jnp.float32) * s_g, 'gg_b': jnp.zeros((E,), jnp.float32), 'W1': jax.random.normal(ks[4], (E, H, M), jnp.float32) * s_h, 'b1': jnp.zeros((E, M), jnp.float32), 'W2': jax.random.normal(ks[5], (E, M, M), jnp.float32) * s_m, 'b2': jnp.zeros((E, M), jnp.float32), 'W3': jax.random.normal(ks[6], (E, M, H), jnp.float32) * s_m, 'b3': jnp.zeros((E, H), jnp.float32)}
    _L0_cond2_all = _L0_cond2_setup()
    _L0_cond2_in = {k: v for k, v in _L0_cond2_all.items() if k in ('rms_w', 'wg_W', 'wg_b', 'gg_W', 'gg_b', 'W1', 'b1', 'W2', 'b2', 'W3', 'b3')}
    del _L0_cond2_all

    def _L0_ffn_setup():
        import jax, jax.numpy as jnp
        import numpy as np
        D_MODEL = 128
        N_EXPERTS = 8
        TOP_K = 2
        FFN_HIDDEN = 4 * D_MODEL
        key = jax.random.key(seed)
        ks = jax.random.split(key, 6)

        def xavier(k, shape):
            fan_in, fan_out = (shape[-2], shape[-1])
            lim = jnp.sqrt(6.0 / (fan_in + fan_out))
            return jax.random.uniform(k, shape, jnp.float32, -lim, lim)
        x = jax.random.normal(ks[0], (4, 256, D_MODEL), jnp.float32)
        w_gate = xavier(ks[1], (N_EXPERTS, D_MODEL))
        W1 = xavier(ks[2], (N_EXPERTS, D_MODEL, FFN_HIDDEN))
        b1 = jnp.zeros((N_EXPERTS, FFN_HIDDEN), jnp.float32)
        W2 = xavier(ks[3], (N_EXPERTS, FFN_HIDDEN, D_MODEL))
        b2 = jnp.zeros((N_EXPERTS, D_MODEL), jnp.float32)
        return {'x': x, 'w_gate': w_gate, 'W1': W1, 'b1': b1, 'W2': W2, 'b2': b2}
    _L0_ffn_all = _L0_ffn_setup()
    _L0_ffn_in = {k: v for k, v in _L0_ffn_all.items() if k in ('w_gate', 'W1', 'b1', 'W2', 'b2')}
    del _L0_ffn_all

    def _L1_cond_setup():
        import jax, jax.numpy as jnp
        import numpy as np
        B, S, E, H, CD = (4, 128, 128, 16, 32)
        HD = E // H
        FIELD_COHERENCE = 0.7
        COH_THRESHOLD = 0.5
        FIELD_COUPLING = 0.3

        def _layernorm(x, g, b, eps=1e-05):
            mu = x.mean(-1, keepdims=True)
            var = ((x - mu) ** 2).mean(-1, keepdims=True)
            return (x - mu) * jax.lax.rsqrt(var + eps) * g + b
        key = jax.random.key(seed)
        ks = jax.random.split(key, 10)
        s = 0.02
        f32 = jnp.float32
        return {'x': jax.random.normal(ks[0], (B, S, E), f32), 'consciousness_state': jax.random.normal(ks[1], (B, CD), f32), 'Wqkv': jax.random.normal(ks[2], (3 * E, E), f32) * s, 'bqkv': jnp.zeros((3 * E,), f32), 'Wout': jax.random.normal(ks[3], (E, E), f32) * s, 'bout': jnp.zeros((E,), f32), 'Wc1': jax.random.normal(ks[4], (E, E + CD), f32) * s, 'bc1': jnp.zeros((E,), f32), 'Wc2': jax.random.normal(ks[5], (H, E), f32) * s, 'bc2': jnp.zeros((H,), f32), 'We1': jax.random.normal(ks[6], (E, CD), f32) * s, 'be1': jnp.zeros((E,), f32), 'We2': jax.random.normal(ks[7], (E, E), f32) * s, 'be2': jnp.zeros((E,), f32), 'ln_g': jnp.ones((E,), f32), 'ln_b': jnp.zeros((E,), f32)}
    _L1_cond_all = _L1_cond_setup()
    _L1_cond_in = {k: v for k, v in _L1_cond_all.items() if k in ('Wqkv', 'bqkv', 'Wout', 'bout', 'Wc1', 'bc1', 'Wc2', 'bc2', 'We1', 'be1', 'We2', 'be2', 'ln_g', 'ln_b')}
    del _L1_cond_all

    def _L1_attn_setup():
        import jax, jax.numpy as jnp
        import numpy as np
        from functools import partial
        B, S, D, H, DK, DV, DFF = (4, 256, 128, 8, 128, 128, 512)
        EPS = 1e-06

        def rms_norm(x):
            return x * jax.lax.rsqrt(jnp.mean(x * x, axis=-1, keepdims=True) + EPS)

        def l2norm(x):
            return x * jax.lax.rsqrt(jnp.sum(x * x, axis=-1, keepdims=True) + EPS)

        def gated_delta_net(h, Wq, Wk, Wv, Wb, Wa, A_log, dt_bias, Wg, o_norm_w, Wo):
            b, s, _ = h.shape
            q = l2norm(jax.nn.silu(h @ Wq).reshape(b, s, H, DK))
            k = l2norm(jax.nn.silu(h @ Wk).reshape(b, s, H, DK))
            v = jax.nn.silu(h @ Wv).reshape(b, s, H, DV)
            beta = jax.nn.sigmoid(h @ Wb)
            g = -jnp.exp(A_log) * jax.nn.softplus(h @ Wa + dt_bias)
            alpha = jnp.exp(g)
            scale = DK ** (-0.5)
            tm = lambda a: jnp.moveaxis(a, 1, 0)
            qs, ks_, vs, als, bts = (tm(q), tm(k), tm(v), tm(alpha), tm(beta))

            def step(Sst, inp):
                q_t, k_t, v_t, a_t, b_t = inp
                Sst = Sst * a_t[..., None, None]
                kv = jnp.einsum('bhd,bhde->bhe', k_t, Sst)
                delta = (v_t - kv) * b_t[..., None]
                Sst = Sst + jnp.einsum('bhd,bhe->bhde', k_t, delta)
                o_t = jnp.einsum('bhd,bhde->bhe', q_t, Sst) * scale
                return (Sst, o_t)
            S0 = jnp.zeros((b, H, DK, DV), dtype=h.dtype)
            _, o = jax.lax.scan(step, S0, (qs, ks_, vs, als, bts))
            o = jnp.moveaxis(o, 0, 1)
            gate = (h @ Wg).reshape(b, s, H, DV)
            o = rms_norm(o) * o_norm_w * jax.nn.silu(gate)
            return o.reshape(b, s, H * DV) @ Wo
        key = jax.random.key(seed)
        ks = jax.random.split(key, 16)
        w = lambda k, shp: jax.random.normal(k, shp, dtype=jnp.float32) * 0.02
        return {'x': jax.random.normal(ks[0], (B, S, D), dtype=jnp.float32), 'Wq': w(ks[1], (D, H * DK)), 'Wk': w(ks[2], (D, H * DK)), 'Wv': w(ks[3], (D, H * DV)), 'Wb': w(ks[4], (D, H)), 'Wa': w(ks[5], (D, H)), 'A_log': jnp.log(jnp.linspace(1.0, 8.0, H).astype(jnp.float32)), 'dt_bias': jax.random.normal(ks[6], (H,), dtype=jnp.float32) * 0.1, 'Wg': w(ks[7], (D, H * DV)), 'o_norm_w': jnp.ones((DV,), dtype=jnp.float32), 'Wo': w(ks[8], (H * DV, D)), 'W_fc': w(ks[9], (D, DFF)), 'W_proj': w(ks[10], (DFF, D))}
    _L1_attn_all = _L1_attn_setup()
    _L1_attn_in = {k: v for k, v in _L1_attn_all.items() if k in ('Wq', 'Wk', 'Wv', 'Wb', 'Wa', 'A_log', 'dt_bias', 'Wg', 'o_norm_w', 'Wo', 'W_fc', 'W_proj')}
    del _L1_attn_all

    def _L1_cond2_setup():
        import jax, jax.numpy as jnp
        import numpy as np
        EPS = 1e-08

        def hamilton(q1, q2):
            w1, x1, y1, z1 = (q1[..., i, :] for i in range(4))
            w2, x2, y2, z2 = (q2[..., i, :] for i in range(4))
            w = w1 * w2 - x1 * x2 - y1 * y2 - z1 * z2
            x = w1 * x2 + x1 * w2 + y1 * z2 - z1 * y2
            y = w1 * y2 - x1 * z2 + y1 * w2 + z1 * x2
            z = w1 * z2 + x1 * y2 - y1 * x2 + z1 * w2
            return jnp.stack([w, x, y, z], axis=-2)

        def _normalize(q):
            return q / jnp.sqrt(jnp.sum(q * q, axis=0, keepdims=True) + EPS)
        key = jax.random.key(seed)
        k1, k2, k3, k4 = jax.random.split(key, 4)
        B, T, d_model = (4, 512, 128)
        quat_dim = d_model // 4
        x = jax.random.normal(k1, (B, T, d_model), dtype=jnp.float32)
        q_left = jax.random.normal(k2, (4, quat_dim), dtype=jnp.float32)
        q_right = jax.random.normal(k3, (4, quat_dim), dtype=jnp.float32)
        spectral_gate = jax.random.uniform(k4, (1, 1, 1, quat_dim), dtype=jnp.float32)
        return {'x': x, 'q_left': q_left, 'q_right': q_right, 'spectral_gate': spectral_gate}
    _L1_cond2_all = _L1_cond2_setup()
    _L1_cond2_in = {k: v for k, v in _L1_cond2_all.items() if k in ('q_right', 'spectral_gate')}
    del _L1_cond2_all

    def _L1_ffn_setup():
        import jax, jax.numpy as jnp
        import numpy as np

        def _ste(w, w_q):
            return w + jax.lax.stop_gradient(w_q - w)

        def quantize_w8_per(w, axis):
            amax = jnp.clip(jnp.max(jnp.abs(w), axis=axis, keepdims=True), 1e-08, None)
            scale = 127.0 / amax
            w_q = jnp.clip(jnp.round(w * scale), -128.0, 127.0) / scale
            return _ste(w, w_q)

        def quantize_a16(x):
            amax = jnp.clip(jnp.max(jnp.abs(x)), 1e-08, None)
            scale = 32767.0 / amax
            x_q = jnp.clip(jnp.round(x * scale), -32768.0, 32767.0) / scale
            return _ste(x, x_q)
        key = jax.random.key(seed)
        k1, k2, k3 = jax.random.split(key, 3)
        d_model, d_ff = (128, 512)
        x = jax.random.normal(k1, (4, 256, d_model), dtype=jnp.float32)
        W_in = jax.random.normal(k2, (d_model, d_ff), dtype=jnp.float32) / np.sqrt(d_model)
        b_in = jnp.zeros((d_ff,), dtype=jnp.float32)
        W_out = jax.random.normal(k3, (d_ff, d_model), dtype=jnp.float32) / np.sqrt(d_ff)
        b_out = jnp.zeros((d_model,), dtype=jnp.float32)
        return {'x': x, 'W_in': W_in, 'b_in': b_in, 'W_out': W_out, 'b_out': b_out}
    _L1_ffn_all = _L1_ffn_setup()
    _L1_ffn_in = {k: v for k, v in _L1_ffn_all.items() if k in ('W_in', 'b_in', 'W_out', 'b_out')}
    del _L1_ffn_all
    return {'x': x, 'cond_256': cond_256, 'cond_64': cond_64, 'L0_cond_input_basis': _L0_cond_in['input_basis'], 'L0_cond_mode_to_rank': _L0_cond_in['mode_to_rank'], 'L0_cond_output_basis': _L0_cond_in['output_basis'], 'L0_attn_W_q': _L0_attn_in['W_q'], 'L0_attn_W_k': _L0_attn_in['W_k'], 'L0_attn_W_v': _L0_attn_in['W_v'], 'L0_attn_W_o': _L0_attn_in['W_o'], 'L0_attn_gn_weight': _L0_attn_in['gn_weight'], 'L0_attn_gn_bias': _L0_attn_in['gn_bias'], 'L0_cond2_rms_w': _L0_cond2_in['rms_w'], 'L0_cond2_wg_W': _L0_cond2_in['wg_W'], 'L0_cond2_wg_b': _L0_cond2_in['wg_b'], 'L0_cond2_gg_W': _L0_cond2_in['gg_W'], 'L0_cond2_gg_b': _L0_cond2_in['gg_b'], 'L0_cond2_W1': _L0_cond2_in['W1'], 'L0_cond2_b1': _L0_cond2_in['b1'], 'L0_cond2_W2': _L0_cond2_in['W2'], 'L0_cond2_b2': _L0_cond2_in['b2'], 'L0_cond2_W3': _L0_cond2_in['W3'], 'L0_cond2_b3': _L0_cond2_in['b3'], 'L0_ffn_w_gate': _L0_ffn_in['w_gate'], 'L0_ffn_W1': _L0_ffn_in['W1'], 'L0_ffn_b1': _L0_ffn_in['b1'], 'L0_ffn_W2': _L0_ffn_in['W2'], 'L0_ffn_b2': _L0_ffn_in['b2'], 'L1_cond_Wqkv': _L1_cond_in['Wqkv'], 'L1_cond_bqkv': _L1_cond_in['bqkv'], 'L1_cond_Wout': _L1_cond_in['Wout'], 'L1_cond_bout': _L1_cond_in['bout'], 'L1_cond_Wc1': _L1_cond_in['Wc1'], 'L1_cond_bc1': _L1_cond_in['bc1'], 'L1_cond_Wc2': _L1_cond_in['Wc2'], 'L1_cond_bc2': _L1_cond_in['bc2'], 'L1_cond_We1': _L1_cond_in['We1'], 'L1_cond_be1': _L1_cond_in['be1'], 'L1_cond_We2': _L1_cond_in['We2'], 'L1_cond_be2': _L1_cond_in['be2'], 'L1_cond_ln_g': _L1_cond_in['ln_g'], 'L1_cond_ln_b': _L1_cond_in['ln_b'], 'L1_attn_Wq': _L1_attn_in['Wq'], 'L1_attn_Wk': _L1_attn_in['Wk'], 'L1_attn_Wv': _L1_attn_in['Wv'], 'L1_attn_Wb': _L1_attn_in['Wb'], 'L1_attn_Wa': _L1_attn_in['Wa'], 'L1_attn_A_log': _L1_attn_in['A_log'], 'L1_attn_dt_bias': _L1_attn_in['dt_bias'], 'L1_attn_Wg': _L1_attn_in['Wg'], 'L1_attn_o_norm_w': _L1_attn_in['o_norm_w'], 'L1_attn_Wo': _L1_attn_in['Wo'], 'L1_attn_W_fc': _L1_attn_in['W_fc'], 'L1_attn_W_proj': _L1_attn_in['W_proj'], 'L1_cond2_q_right': _L1_cond2_in['q_right'], 'L1_cond2_spectral_gate': _L1_cond2_in['spectral_gate'], 'L1_ffn_W_in': _L1_ffn_in['W_in'], 'L1_ffn_b_in': _L1_ffn_in['b_in'], 'L1_ffn_W_out': _L1_ffn_in['W_out'], 'L1_ffn_b_out': _L1_ffn_in['b_out']}

def reference(x, cond_256, cond_64, L0_cond_input_basis, L0_cond_mode_to_rank, L0_cond_output_basis, L0_attn_W_q, L0_attn_W_k, L0_attn_W_v, L0_attn_W_o, L0_attn_gn_weight, L0_attn_gn_bias, L0_cond2_rms_w, L0_cond2_wg_W, L0_cond2_wg_b, L0_cond2_gg_W, L0_cond2_gg_b, L0_cond2_W1, L0_cond2_b1, L0_cond2_W2, L0_cond2_b2, L0_cond2_W3, L0_cond2_b3, L0_ffn_w_gate, L0_ffn_W1, L0_ffn_b1, L0_ffn_W2, L0_ffn_b2, L1_cond_Wqkv, L1_cond_bqkv, L1_cond_Wout, L1_cond_bout, L1_cond_Wc1, L1_cond_bc1, L1_cond_Wc2, L1_cond_bc2, L1_cond_We1, L1_cond_be1, L1_cond_We2, L1_cond_be2, L1_cond_ln_g, L1_cond_ln_b, L1_attn_Wq, L1_attn_Wk, L1_attn_Wv, L1_attn_Wb, L1_attn_Wa, L1_attn_A_log, L1_attn_dt_bias, L1_attn_Wg, L1_attn_o_norm_w, L1_attn_Wo, L1_attn_W_fc, L1_attn_W_proj, L1_cond2_q_right, L1_cond2_spectral_gate, L1_ffn_W_in, L1_ffn_b_in, L1_ffn_W_out, L1_ffn_b_out):
    import jax
    import jax.numpy as jnp

    def _L0_cond_ref(x, spectral_coeff, rank_coeff, input_basis, mode_to_rank, output_basis):
        import math
        import jax, jax.numpy as jnp
        import numpy as np
        from jax.scipy.linalg import cholesky, solve_triangular
        B, S, D, O, K, R = (4, 1024, 128, 128, 32, 64)

        def build_dct_basis(dim: int, num_bases: int) -> np.ndarray:
            num_bases = min(num_bases, dim)
            positions = np.arange(dim, dtype=np.float32)[None, :]
            modes = np.arange(num_bases, dtype=np.float32)[:, None]
            basis = np.cos(math.pi / float(dim) * (positions + 0.5) * modes)
            basis[0] = basis[0] / math.sqrt(2.0)
            basis = basis * math.sqrt(2.0 / float(dim))
            return basis.astype(np.float32)

        def _orthogonalize_mode_to_rank(raw: jnp.ndarray) -> jnp.ndarray:
            raw = raw.astype(jnp.float32)
            gram = raw.T @ raw
            eye = jnp.eye(raw.shape[1], dtype=jnp.float32)
            chol = cholesky(gram + 0.0001 * eye, lower=True)
            inv_chol = solve_triangular(chol, eye, lower=True)
            q = raw @ inv_chol.T
            signs = jnp.sign(jnp.sum(q * raw, axis=0, keepdims=True))
            signs = jnp.where(signs == 0, jnp.ones_like(signs), signs)
            return q * signs
        mtr = _orthogonalize_mode_to_rank(mode_to_rank).astype(x.dtype)
        proj = jnp.einsum('bsd,kd->bsk', x, input_basis.astype(x.dtype))
        proj = proj * spectral_coeff[:, None, :]
        hidden = jnp.einsum('bsk,kr->bsr', proj, mtr)
        hidden = hidden * rank_coeff[:, None, :]
        out = jnp.einsum('bsr,ro->bso', hidden, output_basis.astype(x.dtype))
        return out

    def _L0_attn_ref(x, W_q, W_k, W_v, W_o, gn_weight, gn_bias):
        import jax, jax.numpy as jnp
        import numpy as np
        D_MODEL = 128
        N_HEADS = 16
        D_HEAD = D_MODEL // N_HEADS
        B, T = (2, 256)
        EPS = 1e-05
        b, t, dm = x.shape
        h, dh = (N_HEADS, D_HEAD)
        gammas = 1.0 - 2.0 ** (-5.0 - jnp.arange(h, dtype=jnp.float32))
        q = (x @ W_q.T).reshape(b, t, h, dh)
        k = (x @ W_k.T).reshape(b, t, h, dh)
        v = (x @ W_v.T).reshape(b, t, h, dh)
        idx = jnp.arange(t)
        diff = idx[:, None] - idx[None, :]
        pow_ = jnp.maximum(diff, 0).astype(jnp.float32)
        decay = jnp.where(diff >= 0, gammas[:, None, None] ** pow_, 0.0)
        scale = jnp.sqrt(jnp.float32(dh))
        attn = jnp.einsum('bihd,bjhd->bhij', q, k) * decay[None] / scale
        y = jnp.einsum('bhij,bjhd->bihd', attn, v)
        mean = y.mean(axis=(1, 3), keepdims=True)
        var = y.var(axis=(1, 3), keepdims=True)
        yn = (y - mean) / jnp.sqrt(var + EPS)
        yn = yn.reshape(b, t, dm) * gn_weight + gn_bias
        return yn @ W_o.T

    def _L0_cond2_ref(x, genre_embed, rms_w, wg_W, wg_b, gg_W, gg_b, W1, b1, W2, b2, W3, b3):
        import jax, jax.numpy as jnp
        import numpy as np
        TOP_K = 2
        EPS = 1e-06
        E = W1.shape[0]
        var = jnp.mean(x * x, axis=-1, keepdims=True)
        xn = rms_w * (x * jax.lax.rsqrt(var + EPS))
        gate = xn @ wg_W + wg_b + (genre_embed @ gg_W + gg_b)
        gate_w = jax.nn.softmax(gate, axis=-1)
        topk_w, topk_i = jax.lax.top_k(gate_w, TOP_K)
        cw = jnp.sum(jax.nn.one_hot(topk_i, E, dtype=x.dtype) * topk_w[..., None], axis=-2)
        h1 = jax.nn.relu(jnp.einsum('bsh,ehm->bsem', x, W1) + b1)
        h2 = jax.nn.relu(jnp.einsum('bsem,emn->bsen', h1, W2) + b2)
        out_e = jnp.einsum('bsen,enh->bseh', h2, W3) + b3
        return jnp.einsum('bseh,bse->bsh', out_e, cw)

    def _L0_ffn_ref(x, w_gate, W1, b1, W2, b2):
        import jax, jax.numpy as jnp
        import numpy as np
        D_MODEL = 128
        N_EXPERTS = 8
        TOP_K = 2
        FFN_HIDDEN = 4 * D_MODEL
        B, S, D = x.shape
        flat_x = x.reshape(-1, D)
        gate = jax.nn.softmax(flat_x @ w_gate.T, axis=-1)
        topk_scores, topk_idx = jax.lax.top_k(gate, TOP_K)
        cw = (jax.nn.one_hot(topk_idx, N_EXPERTS, dtype=flat_x.dtype) * topk_scores[..., None]).sum(axis=1)
        h = jax.nn.gelu(jnp.einsum('td,edh->teh', flat_x, W1) + b1, approximate=False)
        y = jnp.einsum('teh,ehd->ted', h, W2) + b2
        out = jnp.einsum('ted,te->td', y, cw)
        return out.reshape(B, S, D)

    def _L1_cond_ref(x, consciousness_state, Wqkv, bqkv, Wout, bout, Wc1, bc1, Wc2, bc2, We1, be1, We2, be2, ln_g, ln_b):
        import jax, jax.numpy as jnp
        import numpy as np
        B, S, E, H, CD = (4, 128, 128, 16, 32)
        HD = E // H
        FIELD_COHERENCE = 0.7
        COH_THRESHOLD = 0.5
        FIELD_COUPLING = 0.3

        def _layernorm(x, g, b, eps=1e-05):
            mu = x.mean(-1, keepdims=True)
            var = ((x - mu) ** 2).mean(-1, keepdims=True)
            return (x - mu) * jax.lax.rsqrt(var + eps) * g + b
        Bb, Ss, Ee = x.shape
        qkv = (x @ Wqkv.T + bqkv).reshape(Bb, Ss, 3, H, HD).transpose(2, 0, 3, 1, 4)
        q, k, v = (qkv[0], qkv[1], qkv[2])
        attn = jax.nn.softmax(jnp.einsum('bhid,bhjd->bhij', q, k) / jnp.sqrt(jnp.float32(HD)), axis=-1)
        cs_exp = jnp.broadcast_to(consciousness_state[:, None, :], (Bb, Ss, CD))
        comb = jnp.concatenate([x, cs_exp], axis=-1)
        coh = jax.nn.sigmoid(jnp.tanh(comb @ Wc1.T + bc1) @ Wc2.T + bc2).transpose(0, 2, 1)
        mod = attn * coh[..., None]
        mod = mod / (mod.sum(-1, keepdims=True) + 1e-08)
        fp = _layernorm(jax.nn.relu(consciousness_state @ We1.T + be1) @ We2.T + be2, ln_g, ln_b)
        pos = jnp.arange(Ss, dtype=jnp.float32)
        inv = 10000.0 ** jnp.repeat(jnp.arange(0, Ee, 2, dtype=jnp.float32) / Ee, 2)
        pe = jnp.sin(pos[:, None] / inv[None, :])
        fa = jax.nn.softmax(jnp.einsum('be,se->bs', fp, pe), axis=-1)
        fi = FIELD_COUPLING * FIELD_COHERENCE
        mod = (1.0 - fi) * mod + fi * fa[:, None, :, None]
        out = jnp.einsum('bhij,bhjd->bhid', mod, v).transpose(0, 2, 1, 3).reshape(Bb, Ss, Ee)
        return out @ Wout.T + bout

    def _L1_attn_ref(x, Wq, Wk, Wv, Wb, Wa, A_log, dt_bias, Wg, o_norm_w, Wo, W_fc, W_proj):
        import jax, jax.numpy as jnp
        import numpy as np
        from functools import partial
        B, S, D, H, DK, DV, DFF = (4, 256, 128, 8, 128, 128, 512)
        EPS = 1e-06

        def rms_norm(x):
            return x * jax.lax.rsqrt(jnp.mean(x * x, axis=-1, keepdims=True) + EPS)

        def l2norm(x):
            return x * jax.lax.rsqrt(jnp.sum(x * x, axis=-1, keepdims=True) + EPS)

        def gated_delta_net(h, Wq, Wk, Wv, Wb, Wa, A_log, dt_bias, Wg, o_norm_w, Wo):
            b, s, _ = h.shape
            q = l2norm(jax.nn.silu(h @ Wq).reshape(b, s, H, DK))
            k = l2norm(jax.nn.silu(h @ Wk).reshape(b, s, H, DK))
            v = jax.nn.silu(h @ Wv).reshape(b, s, H, DV)
            beta = jax.nn.sigmoid(h @ Wb)
            g = -jnp.exp(A_log) * jax.nn.softplus(h @ Wa + dt_bias)
            alpha = jnp.exp(g)
            scale = DK ** (-0.5)
            tm = lambda a: jnp.moveaxis(a, 1, 0)
            qs, ks_, vs, als, bts = (tm(q), tm(k), tm(v), tm(alpha), tm(beta))

            def step(Sst, inp):
                q_t, k_t, v_t, a_t, b_t = inp
                Sst = Sst * a_t[..., None, None]
                kv = jnp.einsum('bhd,bhde->bhe', k_t, Sst)
                delta = (v_t - kv) * b_t[..., None]
                Sst = Sst + jnp.einsum('bhd,bhe->bhde', k_t, delta)
                o_t = jnp.einsum('bhd,bhde->bhe', q_t, Sst) * scale
                return (Sst, o_t)
            S0 = jnp.zeros((b, H, DK, DV), dtype=h.dtype)
            _, o = jax.lax.scan(step, S0, (qs, ks_, vs, als, bts))
            o = jnp.moveaxis(o, 0, 1)
            gate = (h @ Wg).reshape(b, s, H, DV)
            o = rms_norm(o) * o_norm_w * jax.nn.silu(gate)
            return o.reshape(b, s, H * DV) @ Wo
        ln_scale = 1.0
        h = gated_delta_net(ln_scale * rms_norm(x), Wq, Wk, Wv, Wb, Wa, A_log, dt_bias, Wg, o_norm_w, Wo)
        x = x + h
        m = ln_scale * rms_norm(x)
        y = jnp.square(jax.nn.relu(m @ W_fc)) @ W_proj
        return x + y

    def _L1_cond2_ref(x, q_left, q_right, spectral_gate):
        import jax, jax.numpy as jnp
        import numpy as np
        EPS = 1e-08

        def hamilton(q1, q2):
            w1, x1, y1, z1 = (q1[..., i, :] for i in range(4))
            w2, x2, y2, z2 = (q2[..., i, :] for i in range(4))
            w = w1 * w2 - x1 * x2 - y1 * y2 - z1 * z2
            x = w1 * x2 + x1 * w2 + y1 * z2 - z1 * y2
            y = w1 * y2 - x1 * z2 + y1 * w2 + z1 * x2
            z = w1 * z2 + x1 * y2 - y1 * x2 + z1 * w2
            return jnp.stack([w, x, y, z], axis=-2)

        def _normalize(q):
            return q / jnp.sqrt(jnp.sum(q * q, axis=0, keepdims=True) + EPS)
        B, T, d_model = x.shape
        quat_dim = d_model // 4
        x_quat = x.reshape(B, T, 4, quat_dim)
        x_spectral = jnp.fft.fft(x_quat, axis=1)
        x_filtered = jnp.fft.ifft(x_spectral * spectral_gate, axis=1).real.astype(x.dtype)
        q_left_n = _normalize(q_left)
        q_right_n = _normalize(q_right)
        conj_sign = jnp.array([1.0, -1.0, -1.0, -1.0], dtype=x.dtype)[:, None]
        q_right_conj = q_right_n * conj_sign
        x_right = hamilton(x_filtered, q_right_conj)
        x_rotated = hamilton(q_left_n, x_right)
        return x_rotated.reshape(B, T, d_model)

    def _L1_ffn_ref(x, W_in, b_in, W_out, b_out):
        import jax, jax.numpy as jnp
        import numpy as np

        def _ste(w, w_q):
            return w + jax.lax.stop_gradient(w_q - w)

        def quantize_w8_per(w, axis):
            amax = jnp.clip(jnp.max(jnp.abs(w), axis=axis, keepdims=True), 1e-08, None)
            scale = 127.0 / amax
            w_q = jnp.clip(jnp.round(w * scale), -128.0, 127.0) / scale
            return _ste(w, w_q)

        def quantize_a16(x):
            amax = jnp.clip(jnp.max(jnp.abs(x)), 1e-08, None)
            scale = 32767.0 / amax
            x_q = jnp.clip(jnp.round(x * scale), -32768.0, 32767.0) / scale
            return _ste(x, x_q)
        W_in_sim = quantize_w8_per(W_in, axis=0)
        W_out_sim = quantize_w8_per(W_out, axis=1)
        x_sim = quantize_a16(x)
        hidden = jax.nn.gelu(x_sim @ W_in_sim + b_in, approximate=False)
        hidden_sim = quantize_a16(hidden)
        out = hidden_sim @ W_out_sim + b_out
        return out
    x = x + _L0_attn_ref(_L0_cond_ref(x, cond_256, cond_64, L0_cond_input_basis, L0_cond_mode_to_rank, L0_cond_output_basis), L0_attn_W_q, L0_attn_W_k, L0_attn_W_v, L0_attn_W_o, L0_attn_gn_weight, L0_attn_gn_bias)
    x = x + _L0_ffn_ref(_L0_cond2_ref(x, cond_256[:, None, :], L0_cond2_rms_w, L0_cond2_wg_W, L0_cond2_wg_b, L0_cond2_gg_W, L0_cond2_gg_b, L0_cond2_W1, L0_cond2_b1, L0_cond2_W2, L0_cond2_b2, L0_cond2_W3, L0_cond2_b3), L0_ffn_w_gate, L0_ffn_W1, L0_ffn_b1, L0_ffn_W2, L0_ffn_b2)
    x = x + _L1_attn_ref(_L1_cond_ref(x, cond_256, L1_cond_Wqkv, L1_cond_bqkv, L1_cond_Wout, L1_cond_bout, L1_cond_Wc1, L1_cond_bc1, L1_cond_Wc2, L1_cond_bc2, L1_cond_We1, L1_cond_be1, L1_cond_We2, L1_cond_be2, L1_cond_ln_g, L1_cond_ln_b), L1_attn_Wq, L1_attn_Wk, L1_attn_Wv, L1_attn_Wb, L1_attn_Wa, L1_attn_A_log, L1_attn_dt_bias, L1_attn_Wg, L1_attn_o_norm_w, L1_attn_Wo, L1_attn_W_fc, L1_attn_W_proj)
    x = x + _L1_ffn_ref(_L1_cond2_ref(x, cond_256, L1_cond2_q_right, L1_cond2_spectral_gate), L1_ffn_W_in, L1_ffn_b_in, L1_ffn_W_out, L1_ffn_b_out)
    return x

_drawn_inputs = setup_inputs


def setup_inputs(seed=0):
    import zlib

    import numpy as np

    out = dict(_drawn_inputs(seed))
    spreads = {'L0_attn_gn_weight': (1.0, 0.2),
     'L0_attn_gn_bias': (0.0, 0.1),
     'L0_cond2_rms_w': (1.0, 0.6),
     'L0_cond2_wg_b': (0.0, 0.8),
     'L0_cond2_gg_b': (0.0, 0.67),
     'L0_cond2_b1': (0.0, 0.8),
     'L0_cond2_b2': (0.0, 0.594),
     'L0_cond2_b3': (0.0, 0.492),
     'L0_ffn_b1': (0.0, 0.586),
     'L0_ffn_b2': (0.0, 0.402),
     'L1_cond_bqkv': (0.0, 0.389),
     'L1_cond_bout': (0.0, 0.1),
     'L1_cond_bc1': (0.0, 2.0),
     'L1_cond_bc2': (0.0, 2.0),
     'L1_cond_be1': (0.0, 0.8),
     'L1_cond_be2': (0.0, 0.421),
     'L1_cond_ln_g': (1.0, 0.6),
     'L1_cond_ln_b': (0.0, 0.8),
     'L1_attn_o_norm_w': (1.0, 0.6),
     'L1_ffn_b_in': (0.0, 0.407),
     'L1_ffn_b_out': (0.0, 0.1)}
    factors = {'L1_cond_Wqkv': 7.017,
     'L1_cond_Wc1': 64.0,
     'L1_cond_Wc2': 64.0,
     'L1_cond_We1': 8.0,
     'L1_cond_We2': 4.646,
     'L1_attn_Wk': 3.551,
     'L1_attn_Wv': 5.517,
     'L1_attn_Wb': 8.0,
     'L1_attn_Wa': 8.0,
     'L1_attn_A_log': 8.0,
     'L1_attn_dt_bias': 8.0,
     'L1_attn_Wg': 4.783,
     'L1_attn_Wo': 4.826,
     'L1_attn_W_fc': 3.375,
     'L1_attn_W_proj': 3.605}
    for name, (base, spread) in spreads.items():
        noise = np.random.default_rng([zlib.crc32(name.encode()), seed]).standard_normal(out[name].shape)
        drawn = base * np.exp(spread * noise) if base else spread * noise
        out[name] = jnp.asarray(drawn.astype(out[name].dtype))
    for name, factor in factors.items():
        out[name] = (out[name] * factor).astype(out[name].dtype)
    return out
```

```python
from contextlib import ExitStack

import concourse.bass as bass
import numpy as np
from concourse import mybir

B = 32
T = 128
D = 128
GB = 4
GROUPS = B // GB
GT = GB * T
NE = 8
HALVES = 2
TURNS = GROUPS // HALVES
F32 = mybir.dt.float32
BF16 = mybir.dt.bfloat16
ACT = mybir.ActivationFunctionType
ALU = mybir.AluOpType
AX = mybir.AxisListType


class Chain:

    def __init__(self, eng, sem):
        self.eng, self.sem, self.base, self.n = eng, sem, 0, 0

    def turn(self, it, per_turn, before=0):
        self.base, self.n = it * per_turn + before, 0

    def link(self, ins):
        ins.then_inc(self.sem, 1)
        self.n += 1
        self.eng.wait_ge(self.sem, self.base + self.n)


class Memory:

    def __init__(self, nc, ctx, stage):
        self.nc, self.ctx, self.stage, self.sems = nc, ctx, stage, []
        ctx.callback(self.release)

    def release(self):
        self.nc.clear_and_free_semaphores(self.sems)
        self.nc.all_engine_barrier()

    def sb(self, name, shape, dt=F32):
        return self.ctx.enter_context(self.nc.sbuf_tensor(f"{self.stage}_{name}", shape, dt))

    def ps(self, name, shape, dt=F32):
        return self.ctx.enter_context(self.nc.psum_tensor(f"{self.stage}_{name}", shape, dt))

    def sem(self, name):
        self.sems.append(self.nc.alloc_semaphore(f"{self.stage}_{name}"))
        return self.sems[-1]


def over_experts(ap):
    return ap.unsqueeze(2).to_broadcast([128, GB, NE])


def gate_shift(nc, ch, g):
    ch.link(nc.vector.tensor_reduce(g["mx"][:], g["lg"][:], AX.X, ALU.max))
    nc.vector.tensor_tensor(g["lg"][:], g["lg"][:], over_experts(g["mx"][:]),
                            ALU.subtract).then_inc(g["shifted"], 1)


def gate_pick(nc, ch, g):
    p = g["p"][:, :, 0:NE]
    ch.link(nc.vector.tensor_reduce(g["mx"][:], p, AX.X, ALU.add))
    ch.link(nc.vector.reciprocal(g["mx"][:], g["mx"][:]))
    ch.link(nc.vector.tensor_tensor(p, p, over_experts(g["mx"][:]), ALU.mult))
    nc.vector.memset(g["carry"][:], 0.0)
    for b in range(GB):
        last = nc.vector.max(g["t8"][:, b, :], g["p"][:, b, :])
    ch.link(last)
    ch.link(nc.vector.memset(g["t8"][:, :, 2:8], -1.0))
    nc.vector.memset(g["carry"][:], 0.0)
    for b in range(GB):
        last = nc.vector.match_replace(g["rest"][:, b, :], g["t8"][:, b, :], g["p"][:, b, :], 0.0)
    ch.link(last)
    nc.vector.tensor_tensor(g["cw"][:].rearrange("p e b -> p b e"), p, g["rest"][:, :, 0:NE],
                            ALU.subtract).then_inc(g["picked"], 1)


GATE_LINKS = 7


def gate_memory(m):
    g = {"lg": m.sb("gate_logits", [128, GB, NE]), "p": m.sb("gate_weights", [128, GB, 2 * NE]),
         "mx": m.sb("gate_max", [128, GB]), "t8": m.sb("gate_top", [128, GB, 8]),
         "carry": m.sb("gate_carry", [128, 1]),
         "rest": m.sb("gate_rest", [128, GB, 2 * NE]), "cw": m.sb("gate_kept", [128, NE, GB]),
         "cwT": m.sb("gate_keptT", [NE * GB, T])}
    for s in ("logits", "shifted", "exp", "picked", "turned", "out", "stored"):
        g[s] = m.sem("gate_" + s)
    return g


def mixing_basis(nc, w, c):
    K, R = 32, 64
    with ExitStack() as ctx:
        m = Memory(nc, ctx, "basis")
        a = m.sb("a", [R + K, R])
        cols = m.sb("cols", [R + K, R])
        diag = m.sb("diag", [R, R])
        rp = m.sb("rp", [R + K, 1])
        fac = m.sb("fac", [R + K, 1])
        qs = m.sb("qs", [R + K, R])
        q0 = m.sb("q0", [K, R])
        prod = m.sb("prod", [K, R])
        sgn = m.sb("sgn", [K, R])
        gg = m.sb("gg", [K, B, NE])
        bias = m.sb("bias", [1, NE])
        brow = m.sb("brow", [1, B, NE])
        gram_ps = m.ps("gramp", [R, R])
        row_ps = m.ps("rowp", [R + K, R])
        obw_ps = m.ps("obwp", [R, 3 * D])
        sum_ps = m.ps("sump", [K, R])
        gb_ps = m.ps("gbp", [128, B * NE])
        gram, folded, picked, spread, moved, products, sums, gate_rows, gate_bias, roots, chain, done = (
            m.sem(s) for s in ("gram", "folded", "picked", "spread", "moved", "products", "sums",
                               "gate_rows", "gate_bias", "roots", "chain", "done"))
        LINKS = 4

        with nc.Block() as block:
            @block.sync
            def _(sp):
                sp.dma_start(a[R:R + K, :], w["raw_dram"]).then_inc(moved, 16)
                sp.wait_ge(done, 1)
                sp.dma_start(q0[:], qs[R:R + K, :]).then_inc(moved, 16)

            @block.scalar
            def _(act):
                act.wait_ge(spread, R + 1)
                nc.scalar.activation(qs[:], row_ps[:], ACT.Sqrt).then_inc(roots, 1)

            @block.tensor
            def _(pe):
                nc.tensor.matmul(gram_ps[:], w["raw"][:], w["raw"][:], start=True, stop=True).then_inc(gram, 1)
                nc.tensor.matmul(obw_ps[:], w["OBT"][:], w["WqkvT"][:], start=True, stop=True).then_inc(folded, 1)
                pe.wait_ge(gate_rows, 1)
                nc.tensor.matmul(gb_ps[:], w["ones"][0:K, :], gg[:].rearrange("p b e -> p (b e)"), start=True, stop=False)
                nc.tensor.matmul(gb_ps[:], w["ones"][0:1, :], brow[:].rearrange("p b e -> p (b e)"),
                                 start=False, stop=True).then_inc(gate_bias, 1)
                with pe.Fori(0, R + 1) as n:
                    pe.wait_ge(picked, n + 1)
                    nc.tensor.matmul(row_ps[:], w["ones"][0:R, 0:R + K], diag[:], start=True, stop=True).then_inc(spread, 1)
                pe.wait_ge(products, 1)
                nc.tensor.matmul(sum_ps[:], w["ones"][0:K, 0:K], prod[:], start=True, stop=True).then_inc(sums, 1)

            @block.vector
            def _(dve):
                ch = Chain(dve, chain)
                nc.vector.tensor_scalar(c["wg1"][:], w["wg1"][:], w["rms_w"][:], None, ALU.mult)
                ch.link(nc.vector.tensor_tensor(bias[:], w["wgb"][:], w["ggb"][:], ALU.add))
                nc.vector.tensor_copy(brow[:], bias[:].unsqueeze(1).to_broadcast([1, B, NE]))
                nc.vector.tensor_tensor(gg[:], w["condT"][:].unsqueeze(2).to_broadcast([K, B, NE]),
                                        w["ggW"][:].unsqueeze(1).to_broadcast([K, B, NE]), ALU.mult).then_inc(gate_rows, 1)
                dve.wait_ge(gram, 1)
                ch.link(nc.vector.scalar_tensor_tensor(a[0:R, :], w["ident"][0:R, 0:R], 1e-4, gram_ps[:], ALU.mult, ALU.add))
                dve.wait_ge(folded, 1)
                nc.vector.tensor_copy(c["obw"][:], obw_ps[:])
                nc.vector.memset(c["gball"][:, 0:GB, :], 0.0)
                dve.wait_ge(gate_bias, 1)
                nc.vector.tensor_copy(c["gball"][:, GB:, :].rearrange("p b e -> p (b e)"), gb_ps[:])
                dve.wait_ge(moved, 16)
                before = ch.n
                with dve.Fori(0, R) as n:
                    ch.turn(n, LINKS, before)
                    nc.vector.tensor_scalar(diag[:], w["ident"][0:R, 0:R], a[0:R, bass.ds(n, 1)],
                                            w["below"][:, bass.ds(n, 1)], ALU.mult, ALU.mult).then_inc(picked, 1)
                    ch.link(nc.vector.tensor_copy(cols[:, bass.ds(n, 1)], a[:, bass.ds(n, 1)]))
                    dve.wait_ge(spread, n + 1)
                    ch.link(nc.vector.reciprocal(rp[:], row_ps[:, bass.ds(n, 1)]))
                    ch.link(nc.vector.scalar_tensor_tensor(fac[:], cols[:, bass.ds(n, 1)], -1.0, rp[:], ALU.mult, ALU.mult))
                    ch.link(nc.vector.scalar_tensor_tensor(a[:], row_ps[:], fac[:], a[:], ALU.mult, ALU.add))
                ch.turn(0, 0, before + R * LINKS)
                nc.vector.tensor_tensor(diag[:], w["ident"][0:R, 0:R], cols[0:R, :], ALU.mult).then_inc(picked, 1)
                dve.wait_ge(roots, 1)
                ch.link(nc.vector.reciprocal(qs[:], qs[:]))
                nc.vector.tensor_tensor(qs[:], qs[:], cols[:], ALU.mult).then_inc(done, 1)
                dve.wait_ge(moved, 32)
                nc.vector.tensor_tensor(prod[:], q0[:], w["raw"][:], ALU.mult).then_inc(products, 1)
                dve.wait_ge(sums, 1)
                ch.link(nc.vector.tensor_scalar(sgn[:], sum_ps[:], 0.0, 2.0, ALU.is_ge, ALU.mult))
                ch.link(nc.vector.tensor_scalar(sgn[:], sgn[:], -1.0, None, ALU.add))
                nc.vector.tensor_tensor(c["mtr"][:], sgn[:], q0[:], ALU.mult).then_inc(done, 1)


def retention(nc, w, c, dram):
    NH, HQ = 16, 4
    K, R = 32, 64
    EPS_GN, EPS_RMS = 1e-5, 1e-6
    with ExitStack() as ctx:
        m = Memory(nc, ctx, "ret")
        xT = m.sb("xT", [128, 2, GT])
        xres = m.sb("xres", [128, 2, GT])
        proj = m.sb("proj", [K, GT])
        hid = m.sb("hid", [R, GT])
        qT = m.sb("qT", [128, 2, GT])
        kT = m.sb("kT", [128, 2, GT])
        vm = m.sb("vm", [128, 2, GB, HQ, D])
        qm = m.sb("qm", [128, 2, NH, T])
        pT = m.sb("pT", [128, 2, NH, T])
        bn = m.sb("bn", [128, GB, 6])
        mv = m.sb("mv", [128, GB, 2])
        dev = m.sb("dev", [128, GB])
        spread = m.sb("spread", [128, GB])
        gmean = m.sb("gmean", [128, GB])
        scale = m.sb("scale", [128, GB])
        shift = m.sb("shift", [128, GB])
        yn = m.sb("yn", [128, GT])
        x1T = m.sb("x1T", [128, 2, GT])
        sq = m.sb("sq", [128, GT])
        rms = m.sb("rms", [128, GB])
        g = gate_memory(m)
        s_ps = [m.ps(f"sp{i}", [128, HQ, T]) for i in range(HQ)]
        y_ps = [m.ps(f"yp{i}", [128, GT]) for i in range(2)]
        xa = m.ps("xa", [128, GT])
        tb = m.ps("tb", [128, GT])
        x_in = [m.sem(f"x_in{i}") for i in range(2)]
        res_in = [m.sem(f"res_in{i}") for i in range(2)]
        x1_stored = [m.sem(f"x1_stored{i}") for i in range(2)]
        (primed, proj_made, proj_kept, hid_made, hid_kept, q_made, q_kept, k_made, k_kept, v_made, v_kept, qm_made,
         s_made, p_made, y_made, means, mean_made, spreads, var_made, affine, yn_kept, o_made, x1_kept, sq_kept,
         gn_var, gn_root, rms_var, rms_root, chain) = (m.sem(s) for s in (
             "primed", "proj_made", "proj_kept", "hid_made", "hid_kept", "q_made", "q_kept", "k_made", "k_kept",
             "v_made", "v_kept", "qm_made", "s_made", "p_made", "y_made", "means", "mean_made", "spreads",
             "var_made", "affine", "yn_kept", "o_made", "x1_kept", "sq_kept", "gn_var", "gn_root", "rms_var", "rms_root",
             "chain"))
        FREE = 2 * HQ
        LINKS = 1 + 3 + 3 + 3 + GATE_LINKS

        def of_group(ap, u):
            return ap[:, bass.ds(u * GB, GB)].unsqueeze(2)

        with nc.Block() as block:
            @block.sync
            def _(sp):
                for half in range(2):
                    sp.dma_start(xT[:, half, :], dram["xT"][half, :, :]).then_inc(x_in[half], 16)
                sp.dma_start(xres[:, 0, :], dram["xT"][0, :, :]).then_inc(res_in[0], 16)
                sp.dma_start(xres[:, 1, :], dram["xT"][0, :, :]).then_inc(res_in[1], 16)
                sp.wait_ge(primed, 2)
                for half in range(2):
                    sp.dma_start(dram["x1T"][GROUPS + 1 + half, :, :], x1T[:, half, :]).then_inc(x1_stored[half], 16)
                sp.dma_start(dram["cw1"][GROUPS + 1, :, :].rearrange("e (b t) -> (e b) t", t=T),
                             g["cwT"][:]).then_inc(g["stored"], 16)
                with sp.Fori(0, TURNS) as it:
                    for half in range(2):
                        u = it * 2 + half
                        sp.wait_ge(proj_made, u + 1)
                        sp.dma_start(xT[:, half, :], dram["xT"][bass.ds(u + 2, 1), :, :].squeeze(0)).then_inc(x_in[half], 16)
                        sp.wait_ge(x1_kept, u + 1)
                        sp.dma_start(xres[:, 1 - half, :], dram["xT"][bass.ds(u + 1, 1), :, :].squeeze(0)).then_inc(res_in[1 - half], 16)
                        sp.dma_start(dram["x1T"][bass.ds(u, 1), :, :].squeeze(0), x1T[:, 1 - half, :]).then_inc(x1_stored[1 - half], 16)
                        sp.wait_ge(g["out"], u + 1)
                        sp.dma_start(dram["cw1"][bass.ds(u, 1), :, :].rearrange("u e (b t) -> (u e b) t", t=T),
                                     g["cwT"][:]).then_inc(g["stored"], 16)
                sp.wait_ge(x1_kept, GROUPS + 1)
                sp.dma_start(dram["x1T"][GROUPS, :, :], x1T[:, 1, :]).then_inc(x1_stored[1], 16)
                sp.wait_ge(g["out"], GROUPS + 1)
                sp.dma_start(dram["cw1"][GROUPS, :, :].rearrange("e (b t) -> (e b) t", t=T),
                             g["cwT"][:]).then_inc(g["stored"], 16)
                sp.wait_ge(g["stored"], 16 * (GROUPS + 2))
                sp.wait_ge(x1_stored[0], 16 * (TURNS + 1))
                sp.wait_ge(x1_stored[1], 16 * (TURNS + 2))
                for half in range(2):
                    sp.wait_ge(x_in[half], 16 * (TURNS + 1))
                    sp.wait_ge(res_in[half], 16 * (TURNS + 1))

            @block.gpsimd
            def _(pool):
                with pool.Fori(0, TURNS) as it:
                    for half in range(2):
                        u = it * 2 + half
                        pool.wait_ge(q_kept, u + 1)
                        for b in range(GB):
                            pool.wait_ge(p_made, u * GB * HQ + b * HQ + HQ)
                            nc.gpsimd.tensor_tensor(
                                qm[:, b % 2, :, :], qT[:, half, b * T:(b + 1) * T].unsqueeze(1).to_broadcast([128, NH, T]),
                                w["headmask"][:].unsqueeze(2).to_broadcast([128, NH, T]), ALU.mult).then_inc(qm_made, 1)

            @block.tensor
            def _(pe):
                def project_1(v, h, load):
                    pe.wait_ge(x_in[h], load)
                    nc.tensor.matmul(xa[0:K, :], w["ibT"][:], xT[:, h, :], start=True, stop=True).then_inc(proj_made, 1)

                def project_2(v):
                    pe.wait_ge(proj_kept, v + 1)
                    nc.tensor.matmul(xa[0:R, :], c["mtr"][:], proj[:], start=True, stop=True).then_inc(hid_made, 1)

                def project_3(v, h):
                    pe.wait_ge(hid_kept, v + 1)
                    nc.tensor.matmul(xa[:], c["obw"][:, 0:D], hid[:], start=True, stop=True).then_inc(q_made, 1)
                    nc.tensor.matmul(y_ps[h][:], c["obw"][:, D:2 * D], hid[:], start=True, stop=True).then_inc(k_made, 1)
                    pe.wait_ge(q_kept, v + 1)
                    for b in range(GB):
                        last = nc.tensor.matmul(xa[:, b * T:(b + 1) * T], hid[:, b * T:(b + 1) * T], c["obw"][:, 2 * D:3 * D],
                                                start=True, stop=True)
                    last.then_inc(v_made, 1)

                def scores(u, half, b):
                    pe.wait_ge(k_kept, u + 1)
                    pe.wait_ge(qm_made, u * GB + b + 1)
                    for i in range(HQ):
                        pe.wait_ge(p_made, u * GB * HQ + b * HQ + i + 1 + FREE - HQ)
                        nc.tensor.matmul(s_ps[i][:].rearrange("p h t -> p (h t)"), kT[:, half, b * T:(b + 1) * T],
                                         qm[:, b % 2, i * HQ:(i + 1) * HQ, :].rearrange("p h t -> p (h t)"),
                                         start=True, stop=True).then_inc(s_made, 1)

                def values(u, half, b):
                    pe.wait_ge(v_kept, u + 1)
                    pe.wait_ge(p_made, u * GB * HQ + b * HQ + HQ + FREE)
                    for i in range(HQ):
                        for k in range(HQ):
                            last = nc.tensor.matmul(y_ps[half][i * 32:(i + 1) * 32, b * T:(b + 1) * T],
                                                    vm[:, half, b, k, i * 32:(i + 1) * 32], pT[:, b % 2, i * HQ + k, :],
                                                    start=(k == 0), stop=(k == HQ - 1))
                    if b == GB - 1:
                        last.then_inc(y_made, 1)

                def norm_mean(u):
                    pe.wait_ge(means, u + 1)
                    nc.tensor.matmul(tb[:, 0:GB], w["by8"][:], mv[:, :, 0], start=True, stop=True).then_inc(mean_made, 1)

                def norm_var(u):
                    pe.wait_ge(spreads, u + 1)
                    nc.tensor.matmul(tb[:, 8:8 + GB], w["by8"][:], spread[:], start=True, stop=True).then_inc(var_made, 1)

                def output(u):
                    pe.wait_ge(yn_kept, u + 1)
                    nc.tensor.matmul(tb[:], w["WoT"][:], yn[:], start=True, stop=True).then_inc(o_made, 1)

                def gate_logits(u, h):
                    pe.wait_ge(x1_kept, u + 1)
                    pe.wait_ge(sq_kept, u + 1)
                    for b in range(GB):
                        nc.tensor.matmul(tb[:, b * NE:(b + 1) * NE], x1T[:, h, b * T:(b + 1) * T], c["wg1"][:], start=True, stop=True)
                        last = nc.tensor.matmul(tb[:, GB * NE + b:GB * NE + b + 1], sq[:, b * T:(b + 1) * T], w["ones"][:, 0:1],
                                                start=True, stop=True)
                    last.then_inc(g["logits"], 1)

                def gate_turn(u):
                    pe.wait_ge(g["picked"], u + 1)
                    nc.tensor.transpose(tb[0:NE * GB, 0:T], g["cw"][:].rearrange("p e b -> p (e b)"),
                                        w["ident"][:]).then_inc(g["turned"], 1)

                project_1(0, 0, 16)
                project_2(0)
                project_3(0, 0)
                with pe.Fori(0, TURNS) as it:
                    for half in range(2):
                        u = it * 2 + half
                        scores(u, half, 0)
                        norm_mean(u)
                        scores(u, half, 1)
                        norm_var(u)
                        values(u, half, 0)
                        pe.wait_ge(v_kept, u + 1)
                        project_1(u + 1, 1 - half, it * 16 + 16 + 16 * half)
                        scores(u, half, 2)
                        output(u)
                        values(u, half, 1)
                        project_2(u + 1)
                        scores(u, half, 3)
                        gate_logits(u, 1 - half)
                        values(u, half, 2)
                        project_3(u + 1, 1 - half)
                        gate_turn(u)
                        values(u, half, 3)
                norm_mean(GROUPS)
                norm_var(GROUPS)
                output(GROUPS)
                gate_logits(GROUPS, 1)
                gate_turn(GROUPS)

            @block.scalar
            def _(act):
                def keep_qk(v, h):
                    act.wait_ge(q_made, v + 1)
                    nc.scalar.copy(qT[:, h, :], xa[:]).then_inc(q_kept, 1)
                    act.wait_ge(k_made, v + 1)
                    nc.scalar.copy(kT[:, h, :], y_ps[h][:]).then_inc(k_kept, 1)

                def norm_root(u):
                    act.wait_ge(gn_var, u + 1)
                    nc.scalar.activation(scale[:], scale[:], ACT.Sqrt).then_inc(gn_root, 1)

                def gate_root(u):
                    act.wait_ge(rms_var, u + 1)
                    nc.scalar.activation(rms[:], rms[:], ACT.Sqrt).then_inc(rms_root, 1)

                def norm(u, h):
                    act.wait_ge(affine, u + 1)
                    for b in range(GB):
                        last = nc.scalar.activation(yn[:, b * T:(b + 1) * T], y_ps[h][:, b * T:(b + 1) * T], ACT.Identity,
                                                    bias=shift[:, b:b + 1], scale=scale[:, b:b + 1])
                    last.then_inc(yn_kept, 1)

                def square(u, h):
                    act.wait_ge(x1_kept, u + 1)
                    nc.scalar.activation(sq[:], x1T[:, h, :], ACT.Square, scale=D ** -0.5).then_inc(sq_kept, 1)

                def gate_exp(u):
                    act.wait_ge(g["shifted"], u + 1)
                    nc.scalar.activation(g["p"][:, :, 0:NE], g["lg"][:], ACT.Exp).then_inc(g["exp"], 1)

                keep_qk(0, 0)
                with act.Fori(0, TURNS) as it:
                    for half in range(2):
                        u = it * 2 + half
                        norm_root(u)
                        norm(u, 1 - half)
                        square(u, 1 - half)
                        gate_root(u)
                        keep_qk(u + 1, 1 - half)
                        gate_exp(u)
                norm_root(GROUPS)
                norm(GROUPS, 1)
                square(GROUPS, 1)
                gate_root(GROUPS)
                gate_exp(GROUPS)

            @block.vector
            def _(dve):
                ch = Chain(dve, chain)

                def keep_proj(v):
                    dve.wait_ge(proj_made, v + 1)
                    nc.vector.tensor_tensor(proj[:].rearrange("p (b t) -> p b t", t=T), xa[0:K, :].rearrange("p (b t) -> p b t", t=T),
                                            of_group(w["condTp"], v).to_broadcast([K, GB, T]), ALU.mult).then_inc(proj_kept, 1)

                def keep_hid(v):
                    dve.wait_ge(hid_made, v + 1)
                    nc.vector.tensor_tensor(hid[:].rearrange("p (b t) -> p b t", t=T), xa[0:R, :].rearrange("p (b t) -> p b t", t=T),
                                            of_group(w["rankTp"], v).to_broadcast([R, GB, T]), ALU.mult).then_inc(hid_kept, 1)

                def keep_v(v, h):
                    dve.wait_ge(v_made, v + 1)
                    nc.vector.tensor_tensor(vm[:, h, :, :, :], xa[:].rearrange("p (b f) -> p b f", f=D).unsqueeze(2).to_broadcast([128, GB, HQ, D]),
                                            w["quartermask"][:].unsqueeze(1).to_broadcast([128, GB, HQ, D]), ALU.mult).then_inc(v_kept, 1)

                def decay(u, b):
                    for i in range(HQ):
                        dve.wait_ge(s_made, u * GB * HQ + b * HQ + i + 1)
                        nc.vector.tensor_tensor(pT[:, b % 2, i * HQ:(i + 1) * HQ, :], s_ps[i][:],
                                                w["decay"][:, i * HQ:(i + 1) * HQ, :], ALU.mult).then_inc(p_made, 1)

                def norm_stats(u, h):
                    dve.wait_ge(y_made, u + 1)
                    for b in range(GB):
                        last = nc.vector.bn_stats(bn[:, b, :], y_ps[h][:, b * T:(b + 1) * T])
                    ch.link(last)
                    nc.vector.memset(g["carry"][:], 0.0)
                    for b in range(GB):
                        last = nc.vector.bn_aggr(mv[:, b, :], bn[:, b, :])
                    last.then_inc(means, 1)

                def norm_spread(u):
                    dve.wait_ge(mean_made, u + 1)
                    ch.link(nc.vector.tensor_copy(gmean[:], tb[:, 0:GB]))
                    ch.link(nc.vector.tensor_tensor(dev[:], mv[:, :, 0], gmean[:], ALU.subtract))
                    ch.link(nc.vector.tensor_tensor(dev[:], dev[:], dev[:], ALU.mult))
                    nc.vector.tensor_tensor(spread[:], dev[:], mv[:, :, 1], ALU.add).then_inc(spreads, 1)

                def norm_affine(u):
                    dve.wait_ge(var_made, u + 1)
                    nc.vector.tensor_scalar(scale[:], tb[:, 8:8 + GB], EPS_GN, None, ALU.add).then_inc(gn_var, 1)

                def norm_scale(u):
                    dve.wait_ge(gn_root, u + 1)
                    ch.link(nc.vector.reciprocal(scale[:], scale[:]))
                    ch.link(nc.vector.tensor_scalar(scale[:], scale[:], w["gnw"][:], None, ALU.mult))
                    ch.link(nc.vector.scalar_tensor_tensor(shift[:], gmean[:], -1.0, scale[:], ALU.mult, ALU.mult))
                    nc.vector.tensor_scalar(shift[:], shift[:], w["gnb"][:], None, ALU.add).then_inc(affine, 1)

                def residual(u, h, store, load):
                    dve.wait_ge(o_made, u + 1)
                    dve.wait_ge(res_in[h], load)
                    dve.wait_ge(x1_stored[h], store)
                    nc.vector.tensor_tensor(x1T[:, h, :], tb[:], xres[:, h, :], ALU.add).then_inc(x1_kept, 1)

                def gate_before(u):
                    dve.wait_ge(g["logits"], u + 1)
                    nc.vector.tensor_scalar(rms[:], tb[:, GB * NE:GB * NE + GB], EPS_RMS, None, ALU.add).then_inc(rms_var, 1)

                def gate_norm(u):
                    dve.wait_ge(rms_root, u + 1)
                    ch.link(nc.vector.reciprocal(rms[:], rms[:]))
                    ch.link(nc.vector.tensor_tensor(g["lg"][:], tb[:, 0:GB * NE].rearrange("p (b e) -> p b e", e=NE),
                                                    over_experts(rms[:]), ALU.mult))
                    ch.link(nc.vector.tensor_tensor(g["lg"][:], g["lg"][:], c["gball"][:, bass.ds(u * GB, GB), :], ALU.add))
                    gate_shift(nc, ch, g)

                def gate_after(u):
                    dve.wait_ge(g["exp"], u + 1)
                    gate_pick(nc, ch, g)

                def gate_out(u):
                    dve.wait_ge(g["turned"], u + 1)
                    dve.wait_ge(g["stored"], u * 16 + 16)
                    nc.vector.tensor_copy(g["cwT"][:], tb[0:NE * GB, 0:T]).then_inc(g["out"], 1)

                nc.vector.memset(x1T[:], 0.0)
                nc.vector.memset(g["cwT"][:], 0.0).then_inc(primed, 1)
                nc.vector.memset(g["p"][:], -1.0).then_inc(primed, 1)
                dve.wait_ge(primed, 2)
                nc.vector.memset(y_ps[1][:], 0.0).then_inc(y_made, 1)
                dve.sem_inc(p_made, FREE)
                keep_proj(0)
                keep_hid(0)
                keep_v(0, 0)
                with dve.Fori(0, TURNS) as it:
                    ch.turn(it, 2 * LINKS)
                    for half in range(2):
                        u = it * 2 + half
                        norm_stats(u, 1 - half)
                        decay(u, 0)
                        norm_spread(u)
                        decay(u, 1)
                        norm_affine(u)
                        keep_proj(u + 1)
                        norm_scale(u)
                        decay(u, 2)
                        residual(u, 1 - half, it * 16 + 16, it * 16 + 16)
                        keep_hid(u + 1)
                        decay(u, 3)
                        gate_before(u)
                        keep_v(u + 1, 1 - half)
                        gate_norm(u)
                        gate_after(u)
                        gate_out(u)
                assert ch.n == 2 * LINKS, ch.n
                ch.turn(0, 0, GROUPS * LINKS)
                norm_stats(GROUPS, 1)
                norm_spread(GROUPS)
                norm_affine(GROUPS)
                norm_scale(GROUPS)
                residual(GROUPS, 1, TURNS * 16 + 16, TURNS * 16 + 16)
                gate_before(GROUPS)
                gate_norm(GROUPS)
                gate_after(GROUPS)
                gate_out(GROUPS)


def moe_first(nc, w, dram):
    HT = 2
    with ExitStack() as ctx:
        m = Memory(nc, ctx, "moe1")
        xT = m.sb("xT", [128, 2, GT])
        cwb = m.sb("cwb", [128, 2, NE, GT])
        cwe = m.sb("cwe", [NE, 2, GT])
        h1 = m.sb("h1", [128, 2, HT, GT])
        r2 = m.sb("r2", [128, 2, HT, GT])
        h2 = m.sb("h2", [128, 2, HT, GT])
        yT = m.sb("yT", [128, 2, GT])
        g = gate_memory(m)
        h1_ps = [m.ps(f"h1p{i}", [128, GT]) for i in range(HT)]
        h2_ps = [m.ps(f"h2p{i}", [128, GT]) for i in range(HT)]
        y_ps = [m.ps(f"yp{i}", [128, GT]) for i in range(2)]
        lg_ps = m.ps("lgp", [128, GB, NE])
        cw_ps = m.ps("cwp", [NE * GB, T])
        loaded = [m.sem(f"loaded{i}") for i in range(2)]
        y_stored = [m.sem(f"y_stored{i}") for i in range(2)]
        h1_made, h1_kept, h2_made, h2_kept, h2_weighed, y_made, y_kept, primed, chain = (
            m.sem(s) for s in ("h1_made", "h1_kept", "h2_made", "h2_kept", "h2_weighed",
                               "y_made", "y_kept", "primed", "chain"))
        LINKS = GATE_LINKS + 1

        with nc.Block() as block:
            @block.sync
            def _(sp):
                sp.wait_ge(primed, 3)
                sp.dma_start(dram["mT"][GROUPS + 1, :, :], yT[:, 0, :]).then_inc(y_stored[0], 16)
                sp.dma_start(dram["cw2"][GROUPS + 1, :, :].rearrange("e (b t) -> (e b) t", t=T),
                             g["cwT"][:]).then_inc(g["stored"], 16)
                with sp.Fori(0, TURNS) as it:
                    for half in range(2):
                        u = it * 2 + half
                        sp.wait_ge(y_kept, u + 1)
                        sp.dma_start(xT[:, half, :], dram["x1T"][bass.ds(u + 1, 1), :, :].squeeze(0)).then_inc(loaded[half], 16)
                        sp.dma_start(cwe[:, half, :], dram["cw1"][bass.ds(u + 1, 1), :, :].squeeze(0)).then_inc(loaded[half], 16)
                        sp.dma_start(cwb[:, half, :, :].rearrange("p e t -> p (e t)"),
                                     dram["cw1"][bass.ds(u + 1, 1), :, :].rearrange("u e t -> u (e t)").to_broadcast([128, NE * GT])
                                     ).then_inc(loaded[half], 16)
                        sp.wait_ge(y_kept, u + 2)
                        sp.dma_start(dram["mT"][bass.ds(u, 1), :, :].squeeze(0), yT[:, 1 - half, :]).then_inc(y_stored[1 - half], 16)
                        sp.wait_ge(g["out"], u + 1)
                        sp.dma_start(dram["cw2"][bass.ds(u, 1), :, :].rearrange("u e (b t) -> (u e b) t", t=T),
                                     g["cwT"][:]).then_inc(g["stored"], 16)
                sp.wait_ge(y_kept, GROUPS + 2)
                sp.dma_start(dram["mT"][GROUPS, :, :], yT[:, 1, :]).then_inc(y_stored[1], 16)
                sp.wait_ge(g["out"], GROUPS + 1)
                sp.dma_start(dram["cw2"][GROUPS, :, :].rearrange("e (b t) -> (e b) t", t=T),
                             g["cwT"][:]).then_inc(g["stored"], 16)
                sp.wait_ge(g["stored"], 16 * (GROUPS + 2))
                for half in range(2):
                    sp.wait_ge(y_stored[half], 16 * (TURNS + 1))

            @block.tensor
            def _(pe):
                def gate_logits(before, u):
                    pe.wait_ge(y_kept, u + 2)
                    for b in range(GB):
                        last = nc.tensor.matmul(lg_ps[:, b, :], yT[:, before, b * T:(b + 1) * T], w["wg2"][:],
                                                start=True, stop=True)
                    last.then_inc(g["logits"], 1)

                def gate_turn(u):
                    pe.wait_ge(g["picked"], u + 1)
                    nc.tensor.transpose(cw_ps[:], g["cw"][:].rearrange("p e b -> p (e b)"),
                                        w["ident"][:]).then_inc(g["turned"], 1)

                pe.wait_ge(primed, 1)
                with pe.Fori(0, TURNS) as it:
                    for half in range(2):
                        u = it * 2 + half
                        pe.wait_ge(loaded[half], it * 48 + 48)
                        for s in range(NE + 2):
                            if s < NE:
                                pe.wait_ge(h1_kept, u * NE * HT + HT * s + HT)
                                for i in range(HT):
                                    nc.tensor.matmul(h1_ps[i][:], w["W1"][:, s, i * 128:(i + 1) * 128], xT[:, half, :],
                                                     start=True, stop=True).then_inc(h1_made, 1)
                            if 1 <= s <= NE:
                                e = s - 1
                                pe.wait_ge(h1_kept, u * NE * HT + HT * e + 2 * HT)
                                pe.wait_ge(h2_kept, u * NE * HT + HT * e + HT)
                                for n in range(HT):
                                    for k in range(HT):
                                        last = nc.tensor.matmul(h2_ps[n][:], w["W2"][:, e, k, n * 128:(n + 1) * 128],
                                                                h1[:, e % 2, k, :], start=(k == 0), stop=(k == HT - 1))
                                    last.then_inc(h2_made, 1)
                            if s == 2:
                                pe.wait_ge(y_kept, u + 1)
                                nc.tensor.matmul(y_ps[half][:], w["b3"][:], cwe[:, half, :], start=True, stop=False)
                            if s >= 2:
                                e = s - 2
                                pe.wait_ge(h2_weighed, u * NE + e + 3)
                                for k in range(HT):
                                    last = nc.tensor.matmul(y_ps[half][:], w["W3"][:, e, k, :], h2[:, e % 2, k, :],
                                                            start=False, stop=(e == NE - 1 and k == HT - 1))
                                if e == NE - 1:
                                    last.then_inc(y_made, 1)
                            if s == 3:
                                gate_logits(1 - half, u)
                            if s == 7:
                                gate_turn(u)
                gate_logits(1, GROUPS)
                gate_turn(GROUPS)

            @block.scalar
            def _(act):
                def first(it, half, e):
                    u = it * 2 + half
                    for i in range(HT):
                        act.wait_ge(h1_made, u * NE * HT + HT * e + i + 1)
                        nc.scalar.activation(h1[:, e % 2, i, :], h1_ps[i][:], ACT.Relu,
                                             bias=w["b1"][:, e, i:i + 1]).then_inc(h1_kept, 1)

                def gate_exp(u):
                    act.wait_ge(g["shifted"], u + 1)
                    nc.scalar.activation(g["p"][:, :, 0:NE], g["lg"][:], ACT.Exp).then_inc(g["exp"], 1)

                act.sem_inc(h1_kept, HT)
                act.sem_inc(h2_kept, HT)
                with act.Fori(0, TURNS) as it:
                    for half in range(2):
                        u = it * 2 + half
                        for s in range(NE + 1):
                            if s < NE:
                                first(it, half, s)
                            if s >= 1:
                                e = s - 1
                                act.wait_ge(h2_weighed, u * NE + e + 1)
                                for n in range(HT):
                                    act.wait_ge(h2_made, u * NE * HT + HT * e + n + 1)
                                    nc.scalar.activation(r2[:, e % 2, n, :], h2_ps[n][:], ACT.Relu,
                                                         bias=w["b2"][:, e, n:n + 1]).then_inc(h2_kept, 1)
                            if s == 5:
                                gate_exp(u)
                gate_exp(GROUPS)

            @block.vector
            def _(dve):
                ch = Chain(dve, chain)

                def gate_before(u):
                    dve.wait_ge(g["logits"], u + 1)
                    ch.link(nc.vector.tensor_copy(g["lg"][:], lg_ps[:]))
                    gate_shift(nc, ch, g)

                def gate_after(u):
                    dve.wait_ge(g["exp"], u + 1)
                    gate_pick(nc, ch, g)

                def gate_out(u):
                    dve.wait_ge(g["turned"], u + 1)
                    dve.wait_ge(g["stored"], u * 16 + 16)
                    nc.vector.tensor_copy(g["cwT"][:], cw_ps[:]).then_inc(g["out"], 1)

                nc.vector.memset(yT[:], 0.0).then_inc(primed, 1)
                nc.vector.memset(g["cwT"][:], 0.0).then_inc(primed, 1)
                nc.vector.memset(g["p"][:], -1.0).then_inc(primed, 1)
                dve.wait_ge(primed, 3)
                dve.sem_inc(h2_weighed, 2)
                dve.sem_inc(y_kept, 2)
                with dve.Fori(0, TURNS) as it:
                    ch.turn(it, 2 * LINKS)
                    for half in range(2):
                        u = it * 2 + half
                        dve.wait_ge(loaded[half], it * 48 + 48)
                        for e in range(NE):
                            dve.wait_ge(h2_kept, u * NE * HT + HT * e + 2 * HT)
                            ins = nc.vector.tensor_tensor(
                                h2[:, e % 2, :, :], r2[:, e % 2, :, :],
                                cwb[:, half, e, :].unsqueeze(1).to_broadcast([128, HT, GT]), ALU.mult)
                            ins.then_inc(h2_weighed, 1)
                            if e == 3:
                                gate_before(u)
                            if e == 4:
                                gate_after(u)
                            if e == 6:
                                gate_out(u)
                        dve.wait_ge(y_made, u + 1)
                        dve.wait_ge(y_stored[half], it * 16 + 16)
                        nc.vector.tensor_copy(yT[:, half, :], y_ps[half][:]).then_inc(y_kept, 1)
                ch.turn(0, 0, GROUPS * LINKS)
                gate_before(GROUPS)
                gate_after(GROUPS)
                gate_out(GROUPS)


def moe_second(nc, w, dram):
    HT = 4
    with ExitStack() as ctx:
        m = Memory(nc, ctx, "moe2")
        mT = m.sb("mT", [128, 2, GT])
        xT = m.sb("xT", [128, 2, GT])
        cwb = m.sb("cwb", [128, 2, NE, GT])
        cwe = m.sb("cwe", [NE, 2, GT])
        act_h = m.sb("h", [128, 2, HT, GT])
        wgt_h = m.sb("hw", [128, 2, HT, GT])
        x2T = m.sb("x2T", [128, 2, GT])
        h_ps = [m.ps(f"hp{i}", [128, GT]) for i in range(HT)]
        y_ps = [m.ps(f"yp{i}", [128, GT]) for i in range(2)]
        loaded = [m.sem(f"loaded{i}") for i in range(2)]
        stored = [m.sem(f"stored{i}") for i in range(2)]
        h_made, h_kept, h_weighed, y_made, y_kept, primed, padded = (
            m.sem(s) for s in ("h_made", "h_kept", "h_weighed", "y_made", "y_kept", "primed", "padded"))

        with nc.Block() as block:
            @block.sync
            def _(sp):
                sp.wait_ge(primed, 1)
                sp.dma_start(dram["x2T"][GROUPS + 1, :, :], x2T[:, 0, :]).then_inc(stored[0], 16)
                sp.dma_start(dram["x2T"][GROUPS + 2, :, :], x2T[:, 0, :]).then_inc(padded, 16)
                with sp.Fori(0, TURNS) as it:
                    for half in range(2):
                        u = it * 2 + half
                        sp.wait_ge(y_kept, u + 1)
                        sp.dma_start(mT[:, half, :], dram["mT"][bass.ds(u + 1, 1), :, :].squeeze(0)).then_inc(loaded[half], 16)
                        sp.dma_start(xT[:, half, :], dram["x1T"][bass.ds(u + 1, 1), :, :].squeeze(0)).then_inc(loaded[half], 16)
                        sp.dma_start(cwe[:, half, :], dram["cw2"][bass.ds(u + 1, 1), :, :].squeeze(0)).then_inc(loaded[half], 16)
                        sp.dma_start(cwb[:, half, :, :].rearrange("p e t -> p (e t)"),
                                     dram["cw2"][bass.ds(u + 1, 1), :, :].rearrange("u e t -> u (e t)").to_broadcast([128, NE * GT])
                                     ).then_inc(loaded[half], 16)
                        sp.wait_ge(y_kept, u + 2)
                        sp.dma_start(dram["x2T"][bass.ds(u, 1), :, :].squeeze(0), x2T[:, 1 - half, :]).then_inc(stored[1 - half], 16)
                sp.wait_ge(y_kept, GROUPS + 2)
                sp.dma_start(dram["x2T"][GROUPS, :, :], x2T[:, 1, :]).then_inc(stored[1], 16)
                sp.wait_ge(padded, 16)
                for half in range(2):
                    sp.wait_ge(stored[half], 16 * (TURNS + 1))

            @block.tensor
            def _(pe):
                with pe.Fori(0, TURNS) as it:
                    for half in range(2):
                        u = it * 2 + half
                        pe.wait_ge(loaded[half], it * 64 + 64)
                        for s in range(NE + 1):
                            if s < NE:
                                for i in range(HT):
                                    pe.wait_ge(h_kept, u * NE * HT + HT * s + i + 1)
                                    nc.tensor.matmul(h_ps[i][:], w["F1"][:, s, i * 128:(i + 1) * 128], mT[:, half, :],
                                                     start=True, stop=True).then_inc(h_made, 1)
                            if s == 1:
                                pe.wait_ge(y_kept, u + 1)
                                nc.tensor.matmul(y_ps[half][:], w["fb2"][:], cwe[:, half, :], start=True, stop=False)
                            if s >= 1:
                                e = s - 1
                                for k in range(HT):
                                    pe.wait_ge(h_weighed, u * NE * HT + e * HT + k + 1 + 2 * HT)
                                    last = nc.tensor.matmul(y_ps[half][:], w["F2"][:, e, k, :], wgt_h[:, e % 2, k, :],
                                                            start=False, stop=(e == NE - 1 and k == HT - 1))
                                if e == NE - 1:
                                    last.then_inc(y_made, 1)

            @block.scalar
            def _(act):
                act.sem_inc(h_kept, HT)
                with act.Fori(0, TURNS) as it:
                    for half in range(2):
                        u = it * 2 + half
                        for e in range(NE):
                            for i in range(HT):
                                act.wait_ge(h_weighed, u * NE * HT + e * HT + i + 1)
                                act.wait_ge(h_made, u * NE * HT + e * HT + i + 1)
                                nc.scalar.activation(act_h[:, e % 2, i, :], h_ps[i][:], ACT.Gelu,
                                                     bias=w["fb1"][:, e, i:i + 1]).then_inc(h_kept, 1)

            @block.vector
            def _(dve):
                nc.vector.memset(x2T[:], 0.0).then_inc(primed, 1)
                dve.sem_inc(h_weighed, 2 * HT)
                dve.sem_inc(y_kept, 2)
                with dve.Fori(0, TURNS) as it:
                    for half in range(2):
                        u = it * 2 + half
                        dve.wait_ge(loaded[half], it * 64 + 64)
                        for e in range(NE):
                            for i in range(HT):
                                dve.wait_ge(h_kept, u * NE * HT + e * HT + i + 1 + HT)
                                nc.vector.tensor_tensor(wgt_h[:, e % 2, i, :], act_h[:, e % 2, i, :],
                                                        cwb[:, half, e, :], ALU.mult).then_inc(h_weighed, 1)
                        dve.wait_ge(y_made, u + 1)
                        dve.wait_ge(stored[half], it * 16 + 16)
                        nc.vector.tensor_tensor(x2T[:, half, :], y_ps[half][:], xT[:, half, :],
                                                ALU.add).then_inc(y_kept, 1)


FIELD = 0.3 * 0.7


def field_basis(nc, w, c, dram):
    CD = 32
    with ExitStack() as ctx:
        m = Memory(nc, ctx, "fbasis")
        r = m.sb("r", [128, B])
        fp = m.sb("fp", [B, D])
        bn = m.sb("bn", [B, 6])
        mv = m.sb("mv", [B, 2])
        rstd = m.sb("rstd", [B, 1])
        fpT = m.sb("fpT", [128, B])
        mx = m.sb("mx", [B, 1])
        e = m.sb("e", [B, T])
        z = m.sb("z", [B, 1])
        none = m.sb("none", [GB, T])
        c1_ps = m.ps("c1p", [128, B])
        r_ps = m.ps("rp", [128, B])
        fp_ps = m.ps("fpp", [B, D])
        fpT_ps = m.ps("fpTp", [128, B])
        fa_ps = m.ps("fap", [B, T])
        first, r_kept, fp_made, var, root, normed, turned, turn_kept, logits, peak, exps, fa, nothing, stored, chain = (
            m.sem(s) for s in ("first", "r_kept", "fp_made", "var", "root", "normed", "turned", "turn_kept",
                               "logits", "peak", "exps", "fa", "nothing", "stored", "chain"))
        with nc.Block() as block:
            @block.sync
            def _(sp):
                sp.wait_ge(nothing, 1)
                sp.dma_start(dram["fa"][0:GB, :], none[:]).then_inc(stored, 16)
                sp.dma_start(dram["fa"][GB + B:, :], none[:]).then_inc(stored, 16)
                sp.wait_ge(fa, 1)
                sp.dma_start(dram["fa"][GB:GB + B, :], e[:]).then_inc(stored, 16)
                sp.wait_ge(stored, 48)

            @block.tensor
            def _(pe):
                nc.tensor.matmul(c1_ps[:], w["Wc1cT"][:], w["condT"][:], start=True, stop=True)
                nc.tensor.matmul(r_ps[:], w["We1T"][:], w["condT"][:], start=True, stop=True).then_inc(first, 1)
                pe.wait_ge(r_kept, 1)
                nc.tensor.matmul(fp_ps[:], r[:], w["We2T"][:], start=True, stop=False)
                nc.tensor.matmul(fp_ps[:], w["ones"][0:1, 0:B], w["be2"][:], start=False, stop=True).then_inc(fp_made, 1)
                pe.wait_ge(normed, 1)
                nc.tensor.transpose(fpT_ps[:], fp[:], w["ident"][0:B, 0:B]).then_inc(turned, 1)
                pe.wait_ge(turn_kept, 1)
                nc.tensor.matmul(fa_ps[:], fpT[:], w["peT"][:], start=True, stop=True).then_inc(logits, 1)

            @block.scalar
            def _(act):
                nc.scalar.activation(c["expA"][:], w["Alog"][:], ACT.Exp)
                act.wait_ge(var, 1)
                nc.scalar.activation(rstd[:], rstd[:], ACT.Sqrt).then_inc(root, 1)
                act.wait_ge(peak, 1)
                nc.scalar.activation(e[:], fa_ps[:], ACT.Exp, bias=mx[:], accum_out=z[:]).then_inc(exps, 1)

            @block.vector
            def _(dve):
                ch = Chain(dve, chain)
                nc.vector.memset(none[:], 0.0).then_inc(nothing, 1)
                nc.vector.memset(c["c1b"][:, 0:GB], 0.0)
                nc.vector.memset(c["c1b"][:, GB + B:], 0.0)
                dve.wait_ge(first, 1)
                nc.vector.tensor_scalar(c["c1b"][:, GB:GB + B], c1_ps[:], w["bc1"][:], None, ALU.add)
                nc.vector.tensor_scalar(r[:], r_ps[:], w["be1"][:], 0.0, ALU.add, ALU.max).then_inc(r_kept, 1)
                dve.wait_ge(fp_made, 1)
                ch.link(nc.vector.bn_stats(bn[:], fp_ps[:]))
                ch.link(nc.vector.bn_aggr(mv[:], bn[:]))
                nc.vector.tensor_scalar(rstd[:], mv[:, 1:2], 1e-5, None, ALU.add).then_inc(var, 1)
                dve.wait_ge(root, 1)
                ch.link(nc.vector.reciprocal(rstd[:], rstd[:]))
                ch.link(nc.vector.tensor_scalar(fp[:], fp_ps[:], mv[:, 0:1], rstd[:], ALU.subtract, ALU.mult))
                ch.link(nc.vector.tensor_tensor(fp[:], fp[:], w["lng"][:], ALU.mult))
                nc.vector.tensor_tensor(fp[:], fp[:], w["lnb"][:], ALU.add).then_inc(normed, 1)
                dve.wait_ge(turned, 1)
                nc.vector.tensor_copy(fpT[:], fpT_ps[:]).then_inc(turn_kept, 1)
                dve.wait_ge(logits, 1)
                ch.link(nc.vector.tensor_reduce(mx[:], fa_ps[:], AX.X, ALU.max))
                nc.vector.tensor_scalar(mx[:], mx[:], -1.0, None, ALU.mult).then_inc(peak, 1)
                dve.wait_ge(exps, 1)
                ch.link(nc.vector.reciprocal(z[:], z[:]))
                nc.vector.tensor_scalar(e[:], e[:], z[:], FIELD, ALU.mult, ALU.mult).then_inc(fa, 1)


def field_attention(nc, w, c, dram):
    NH, HQ, HD, GH = 16, 4, 8, 8
    SCALE = HD ** -0.5
    EPS = 1e-6
    with ExitStack() as ctx:
        m = Memory(nc, ctx, "field")
        xT = m.sb("xT", [128, 2, GT])
        fab = m.sb("fab", [128, 2, GT])
        qT = m.sb("qT", [128, 2, GT])
        kT = m.sb("kT", [128, 2, GT])
        km = m.sb("km", [128, 2, NH, T])
        v = m.sb("v", [128, 2, GB, D])
        vm = m.sb("vm", [128, 2, GB, HQ, D])
        th = m.sb("th", [128, GT])
        c1g = m.sb("c1g", [128, GB])
        zc = m.sb("zc", [128, GB, NH])
        coh = m.sb("coh", [128, 2, GB, NH])
        nm = m.sb("nm", [128, 2, NH])
        zs = m.sb("zs", [128, 2, NH])
        rz = m.sb("rz", [128, 2, NH])
        p = m.sb("p", [128, 2, NH, T])
        pT = m.sb("pT", [128, NH, T])
        yT = m.sb("yT", [128, GT])
        aT = m.sb("aT", [128, GT])
        sq = m.sb("sq", [128, GT])
        rt = m.sb("rt", [128, GT])
        hT = m.sb("hT", [128, GT])
        ba = m.sb("ba", [128, GB, 2 * GH])
        ex = m.sb("ex", [128, GB, 2 * GH])
        pos = m.sb("pos", [128, GB, GH])
        lo = m.sb("lo", [128, GB, GH])
        beta = m.sb("beta", [128, GB, GH])
        al = m.sb("al", [128, GB, GH])
        alT = m.sb("alT", [GB * GH, T])
        s_ps = [m.ps(f"sp{i}", [128, HQ, T]) for i in range(HQ)]
        pt_ps = m.ps("ptp", [128, HQ, T])
        y_ps = m.ps("yp", [128, GT])
        xa = m.ps("xa", [128, GT])
        tb = m.ps("tb", [128, GT])
        x_in = [m.sem(f"x_in{i}") for i in range(2)]
        fa_in = [m.sem(f"fa_in{i}") for i in range(2)]
        names = ("primed q_made q_kept k_made k_kept v_made v_kept vm_made c1_kept t_made t_kept z_made z_kept z_exp coh_kept "
                 "km_made s_made peak exps rz_made p_made turned pt_kept y_made y_kept o_made a_kept sq_kept ms_made "
                 "ms_root h_kept ba_made ba_kept ba_exp one_kept ln_kept g_kept al_exp al_turned al_out "
                 "a_stored h_stored be_stored al_stored chain").split()
        s = {n: m.sem(n) for n in names}
        LINKS_TURN = 2 * GB * HQ + 7
        EXP0 = 2 * HQ

        with nc.Block() as block:
            @block.sync
            def _(sp):
                def store_before(u, slot):
                    sp.wait_ge(s["a_kept"], u + 1)
                    sp.dma_start(dram["aT"][slot, :, :].squeeze(0), aT[:]).then_inc(s["a_stored"], 16)
                    sp.wait_ge(s["h_kept"], u + 1)
                    sp.dma_start(dram["hT"][slot, :, :].squeeze(0), hT[:]).then_inc(s["h_stored"], 16)
                    sp.wait_ge(s["g_kept"], u + 1)
                    sp.dma_start(dram["beta"][slot, :, :].squeeze(0), beta[:].rearrange("p b h -> p (b h)")).then_inc(s["be_stored"], 16)
                    sp.wait_ge(s["al_out"], u + 1)
                    sp.dma_start(dram["alpha"][slot, :, :].squeeze(0), alT[:]).then_inc(s["al_stored"], 16)

                for half in range(2):
                    sp.dma_start(xT[:, half, :], dram["x2T"][1 + half, :, :]).then_inc(x_in[half], 16)
                sp.dma_start(fab[:, 0, :], dram["fa"][GB:2 * GB, :].rearrange("(o b) t -> o (b t)", o=1).to_broadcast([128, GT])).then_inc(fa_in[0], 16)
                sp.dma_start(fab[:, 1, :], dram["fa"][0:GB, :].rearrange("(o b) t -> o (b t)", o=1).to_broadcast([128, GT])).then_inc(fa_in[1], 16)
                sp.wait_ge(s["primed"], 1)
                sp.dma_start(dram["aT"][GROUPS + 1, :, :], aT[:]).then_inc(s["a_stored"], 16)
                sp.dma_start(dram["hT"][GROUPS + 1, :, :], hT[:]).then_inc(s["h_stored"], 16)
                sp.dma_start(dram["beta"][GROUPS + 1, :, :], beta[:].rearrange("p b h -> p (b h)")).then_inc(s["be_stored"], 16)
                sp.dma_start(dram["alpha"][GROUPS + 1, :, :], alT[:]).then_inc(s["al_stored"], 16)
                with sp.Fori(0, TURNS) as it:
                    for half in range(2):
                        u = it * 2 + half
                        sp.wait_ge(s["t_made"], u + 1)
                        sp.dma_start(xT[:, half, :], dram["x2T"][bass.ds(u + 3, 1), :, :].squeeze(0)).then_inc(x_in[half], 16)
                        sp.wait_ge(s["y_made"], u + 1)
                        sp.dma_start(fab[:, 1 - half, :], dram["fa"][bass.ds((u + 2) * GB, GB), :].rearrange("(o b) t -> o (b t)", o=1)
                                     .to_broadcast([128, GT])).then_inc(fa_in[1 - half], 16)
                        store_before(u, bass.ds(u, 1))
                store_before(GROUPS, bass.ds(GROUPS, 1))
                for n in ("a_stored", "h_stored", "be_stored", "al_stored"):
                    sp.wait_ge(s[n], 16 * (GROUPS + 2))
                for half in range(2):
                    sp.wait_ge(x_in[half], 16 * (TURNS + 1))
                    sp.wait_ge(fa_in[half], 16 * (TURNS + 1))

            @block.gpsimd
            def _(pool):
                def mask_k(n, kk, h, b, r):
                    pool.wait_ge(s["k_kept"], kk)
                    pool.wait_ge(s["exps"], n * HQ + HQ)
                    nc.gpsimd.tensor_tensor(km[:, r, :, :], kT[:, h, b * T:(b + 1) * T].unsqueeze(1).to_broadcast([128, NH, T]),
                                            w["headmask"][:].unsqueeze(2).to_broadcast([128, NH, T]), ALU.mult).then_inc(s["km_made"], 1)

                def weigh(n, r, i):
                    pool.wait_ge(s["rz_made"], n)
                    nc.gpsimd.tensor_tensor(p[:, r, i * HQ:(i + 1) * HQ, :], p[:, r, i * HQ:(i + 1) * HQ, :],
                                            rz[:, r, i * HQ:(i + 1) * HQ].unsqueeze(2).to_broadcast([128, HQ, T]),
                                            ALU.mult).then_inc(s["p_made"], 1)

                def mask_v(vv, h):
                    pool.wait_ge(s["v_kept"], vv)
                    nc.gpsimd.tensor_tensor(vm[:, h, :, :, :], v[:, h, :, :].unsqueeze(2).to_broadcast([128, GB, HQ, D]),
                                            w["quartermask"][:].unsqueeze(1).to_broadcast([128, GB, HQ, D]), ALU.mult).then_inc(s["vm_made"], 1)

                pool.sem_inc(s["p_made"], HQ - 1)
                mask_v(1, 0)
                mask_k(0, 1, 0, 0, 0)
                with pool.Fori(0, TURNS) as it:
                    for half in range(2):
                        u = it * 2 + half
                        for b in range(GB):
                            n = u * GB + b
                            weigh(n * HQ + 1, (b + 1) % 2, HQ - 1)
                            if b < GB - 1:
                                mask_k(n + 1, u + 1, half, b + 1, (b + 1) % 2)
                            else:
                                mask_v(u + 2, 1 - half)
                                mask_k(n + 1, u + 2, 1 - half, 0, 0)
                            for i in range(HQ - 1):
                                weigh(n * HQ + i + 2, b % 2, i)
                weigh(B * HQ + 1, 1, HQ - 1)

            @block.tensor
            def _(pe):
                def project_qkv(vv, h, load, part):
                    if part == "q":
                        pe.wait_ge(x_in[h], load)
                        pe.wait_ge(s["z_kept"], vv + 1)
                        nc.tensor.matmul(xa[:], w["WqT1"][:], xT[:, h, :], start=True, stop=True).then_inc(s["q_made"], 1)
                    if part == "k":
                        pe.wait_ge(s["q_kept"], vv + 1)
                        nc.tensor.matmul(xa[:], w["WkT1"][:], xT[:, h, :], start=True, stop=True).then_inc(s["k_made"], 1)
                    if part == "v":
                        pe.wait_ge(s["k_kept"], vv + 1)
                        for b in range(GB):
                            last = nc.tensor.matmul(xa[:, b * T:(b + 1) * T], xT[:, h, b * T:(b + 1) * T], w["WvT1"][:], start=True, stop=True)
                        last.then_inc(s["v_made"], 1)
                    if part == "t":
                        pe.wait_ge(s["v_kept"], vv + 1)
                        nc.tensor.matmul(xa[:], w["Wc1xT"][:], xT[:, h, :], start=True, stop=True).then_inc(s["t_made"], 1)
                    if part == "z":
                        pe.wait_ge(s["t_kept"], vv + 1)
                        for b in range(GB):
                            last = nc.tensor.matmul(xa[:, b * NH:(b + 1) * NH], th[:, b * T:(b + 1) * T], w["Wc2T"][:], start=True, stop=True)
                        last.then_inc(s["z_made"], 1)

                def scores(n, half, b, i):
                    if i == 0:
                        pe.wait_ge(s["km_made"], n + 1)
                    pe.wait_ge(s["exps"], n * HQ + i + 1 + EXP0 - HQ)
                    nc.tensor.matmul(s_ps[i][:].rearrange("p h t -> p (h t)"), qT[:, half, b * T:(b + 1) * T],
                                     km[:, b % 2, i * HQ:(i + 1) * HQ, :].rearrange("p h t -> p (h t)"),
                                     start=True, stop=True).then_inc(s["s_made"], 1)

                def turn_before(n, r, i):
                    pe.wait_ge(s["p_made"], n * HQ + i + 1)
                    pe.wait_ge(s["pt_kept"], n * HQ + i + 1)
                    for k in range(HQ):
                        last = nc.tensor.transpose(pt_ps[:, k, :], p[:, r, i * HQ + k, :], w["ident"][:])
                    last.then_inc(s["turned"], 1)

                def values_before(n, h, b, done, load):
                    pe.wait_ge(fa_in[h], load)
                    pe.wait_ge(s["pt_kept"], n * HQ + HQ + 1)
                    for i in range(HQ):
                        for k in range(HQ):
                            last = nc.tensor.matmul(y_ps[i * 32:(i + 1) * 32, b * T:(b + 1) * T], vm[:, h, b, k, i * 32:(i + 1) * 32],
                                                    pT[:, i * HQ + k, :], start=(k == 0), stop=False, skip_group_check=True)
                    last = nc.tensor.matmul(y_ps[:, b * T:(b + 1) * T], v[:, h, b, :], fab[:, h, b * T:(b + 1) * T],
                                            start=False, stop=True, skip_group_check=True)
                    if done:
                        last.then_inc(s["y_made"], 1)

                def output(u):
                    pe.wait_ge(s["y_kept"], u + 1)
                    nc.tensor.matmul(tb[:], w["WoutT"][:], yT[:], start=True, stop=True).then_inc(s["o_made"], 1)

                def mean_square(u):
                    pe.wait_ge(s["sq_kept"], u + 1)
                    nc.tensor.matmul(tb[:], w["mean"][:], sq[:], start=True, stop=True).then_inc(s["ms_made"], 1)

                def alpha_beta(u):
                    pe.wait_ge(s["h_kept"], u + 1)
                    for b in range(GB):
                        last = nc.tensor.matmul(tb[:, b * 2 * GH:(b + 1) * 2 * GH], hT[:, b * T:(b + 1) * T], w["Wba"][:], start=True, stop=True)
                    last.then_inc(s["ba_made"], 1)

                def alpha_turn(u):
                    pe.wait_ge(s["al_exp"], u + 1)
                    nc.tensor.transpose(tb[0:GB * GH, 0:T], al[:].rearrange("p b h -> p (b h)"), w["ident"][:]).then_inc(s["al_turned"], 1)

                for part in "qkvtz":
                    project_qkv(0, 0, 16, part)
                with pe.Fori(0, TURNS) as it:
                    for half in range(2):
                        u = it * 2 + half
                        ahead = lambda part: project_qkv(u + 1, 1 - half, it * 16 + 16 + 16 * half, part)
                        for b in range(GB):
                            n = u * GB + b
                            for i in range(HQ):
                                scores(n, half, b, i)
                                turn_before(n, (b + 1) % 2, i)
                                if i == 1:
                                    [lambda: ahead("q"), lambda: output(u), lambda: ahead("t"), lambda: ahead("z")][b]()
                                if i == 2 and b == 1:
                                    ahead("v")
                                if i == 2 and b == 2:
                                    alpha_beta(u)
                                if i == 3:
                                    [lambda: ahead("k"), lambda: mean_square(u), lambda: None, lambda: alpha_turn(u)][b]()
                            if b == 0:
                                pe.wait_ge(s["vm_made"], u + 1)
                                values_before(n, 1 - half, GB - 1, True, it * 16 + 16)
                            else:
                                if b == 1:
                                    pe.wait_ge(s["y_kept"], u + 1)
                                values_before(n, half, b - 1, False, it * 16 + 16 + 16 * half)
                for i in range(HQ):
                    turn_before(B, 1, i)
                values_before(B, 1, GB - 1, True, TURNS * 16 + 16)
                output(GROUPS)
                mean_square(GROUPS)
                alpha_beta(GROUPS)
                alpha_turn(GROUPS)

            @block.scalar
            def _(act):
                def keep_q(vv, h):
                    act.wait_ge(s["q_made"], vv + 1)
                    nc.scalar.activation(qT[:, h, :], xa[:], ACT.Identity, bias=w["bq"][:]).then_inc(s["q_kept"], 1)

                def keep_k(vv, h):
                    act.wait_ge(s["k_made"], vv + 1)
                    nc.scalar.activation(kT[:, h, :], xa[:], ACT.Identity, bias=w["bk"][:]).then_inc(s["k_kept"], 1)

                def keep_t(vv):
                    act.wait_ge(s["c1_kept"], vv + 1)
                    act.wait_ge(s["t_made"], vv + 1)
                    for b in range(GB):
                        last = nc.scalar.activation(th[:, b * T:(b + 1) * T], xa[:, b * T:(b + 1) * T], ACT.Tanh, bias=c1g[:, b:b + 1])
                    last.then_inc(s["t_kept"], 1)

                def exp_z(vv):
                    act.wait_ge(s["z_kept"], vv + 2)
                    nc.scalar.activation(zc[:], zc[:], ACT.Exp, scale=-1.0).then_inc(s["z_exp"], 1)

                def exp_scores(n, r, i):
                    act.wait_ge(s["peak"], n * HQ + i + 1)
                    for k in range(HQ):
                        h = i * HQ + k
                        last = nc.scalar.activation(p[:, r, h, :], s_ps[i][:, k, :], ACT.Exp, bias=nm[:, r, h:h + 1], scale=SCALE,
                                                    accum_out=zs[:, r, h:h + 1])
                    last.then_inc(s["exps"], 1)

                def keep_y(u):
                    act.wait_ge(s["y_made"], u + 1)
                    nc.scalar.copy(yT[:], y_ps[:]).then_inc(s["y_kept"], 1)

                def keep_a(u):
                    act.wait_ge(s["o_made"], u + 1)
                    act.wait_ge(s["a_stored"], u * 16 + 16)
                    nc.scalar.activation(aT[:], tb[:], ACT.Identity, bias=w["bout"][:]).then_inc(s["a_kept"], 1)

                def root_ms(u):
                    act.wait_ge(s["ms_made"], u + 1)
                    nc.scalar.activation(rt[:], tb[:], ACT.Sqrt, bias=w["eps6"][:]).then_inc(s["ms_root"], 1)

                def alpha_exp(u):
                    act.wait_ge(s["ba_kept"], u + 1)
                    nc.scalar.activation(ex[:], ba[:], ACT.Exp, scale=-1.0).then_inc(s["ba_exp"], 1)

                def alpha_ln(u):
                    act.wait_ge(s["one_kept"], u + 1)
                    nc.scalar.activation(lo[:], lo[:], ACT.Ln).then_inc(s["ln_kept"], 1)

                def alpha_last(u):
                    act.wait_ge(s["g_kept"], u + 1)
                    nc.scalar.activation(al[:], pos[:], ACT.Exp, scale=-1.0).then_inc(s["al_exp"], 1)

                act.sem_inc(s["exps"], EXP0)
                keep_q(0, 0)
                keep_k(0, 0)
                keep_t(0)
                exp_z(0)
                with act.Fori(0, TURNS) as it:
                    for half in range(2):
                        u = it * 2 + half
                        for b in range(GB):
                            n = u * GB + b
                            for i in range(HQ):
                                exp_scores(n, b % 2, i)
                                if b == 0 and i == 2:
                                    keep_q(u + 1, 1 - half)
                                if b == 1 and i == 0:
                                    keep_y(u)
                                    keep_k(u + 1, 1 - half)
                                if b == 1 and i == 2:
                                    keep_a(u)
                                if b == 2 and i == 0:
                                    root_ms(u)
                                if b == 2 and i == 2:
                                    keep_t(u + 1)
                                if b == 3 and i == 0:
                                    alpha_exp(u)
                                if b == 3 and i == 2:
                                    alpha_ln(u)
                                    exp_z(u + 1)
                                    alpha_last(u)
                keep_y(GROUPS)
                keep_a(GROUPS)
                root_ms(GROUPS)
                alpha_exp(GROUPS)
                alpha_ln(GROUPS)
                alpha_last(GROUPS)

            @block.vector
            def _(dve):
                ch = Chain(dve, s["chain"])

                def keep_v(vv, h):
                    dve.wait_ge(s["v_made"], vv + 1)
                    nc.vector.tensor_tensor(v[:, h, :, :], xa[:].rearrange("p (b f) -> p b f", f=D),
                                            w["bvb"][:].unsqueeze(1).to_broadcast([128, GB, D]), ALU.add).then_inc(s["v_kept"], 1)

                def keep_c1(vv):
                    nc.vector.tensor_scalar(c1g[:], c["c1b"][:, bass.ds(vv * GB + GB, GB)], 0.0, None, ALU.add).then_inc(s["c1_kept"], 1)

                def keep_z(vv):
                    dve.wait_ge(s["z_made"], vv + 1)
                    nc.vector.tensor_tensor(zc[:], xa[:, 0:GB * NH].rearrange("p (b h) -> p b h", h=NH),
                                            w["bc2b"][:].unsqueeze(1).to_broadcast([128, GB, NH]), ALU.add).then_inc(s["z_kept"], 1)

                def coherence(vv, h):
                    dve.wait_ge(s["z_exp"], vv + 1)
                    ch.link(nc.vector.tensor_scalar(coh[:, h, :, :], zc[:], 1.0, 1e-8, ALU.add, ALU.mult))
                    ch.link(nc.vector.tensor_scalar(coh[:, h, :, :], coh[:, h, :, :], 1.0, 1.0 / (1.0 - FIELD), ALU.add, ALU.mult))
                    nc.vector.reciprocal(coh[:, h, :, :], coh[:, h, :, :]).then_inc(s["coh_kept"], 1)
                    dve.wait_ge(s["coh_kept"], vv + 1)

                def peaks(n, r, i):
                    dve.wait_ge(s["s_made"], n * HQ + i + 1)
                    hs = slice(i * HQ, (i + 1) * HQ)
                    ch.link(nc.vector.tensor_reduce(nm[:, r, hs], s_ps[i][:], AX.X, ALU.max))
                    nc.vector.tensor_scalar(nm[:, r, hs], nm[:, r, hs], -SCALE, None, ALU.mult).then_inc(s["peak"], 1)

                def factors(n, r, i, h, b):
                    dve.wait_ge(s["exps"], n)
                    hs = slice(i * HQ, (i + 1) * HQ)
                    ch.link(nc.vector.reciprocal(rz[:, r, hs], zs[:, r, hs]))
                    nc.vector.tensor_tensor(rz[:, r, hs], rz[:, r, hs], coh[:, h, b, hs], ALU.mult).then_inc(s["rz_made"], 1)

                def keep_turned(n, i):
                    dve.wait_ge(s["turned"], n * HQ + i + 1)
                    nc.vector.tensor_copy(pT[:, i * HQ:(i + 1) * HQ, :], pt_ps[:]).then_inc(s["pt_kept"], 1)

                def square(u):
                    dve.wait_ge(s["a_kept"], u + 1)
                    nc.vector.tensor_tensor(sq[:], aT[:], aT[:], ALU.mult).then_inc(s["sq_kept"], 1)

                def norm(u):
                    dve.wait_ge(s["ms_root"], u + 1)
                    dve.wait_ge(s["h_stored"], u * 16 + 16)
                    ch.link(nc.vector.reciprocal(rt[:], rt[:]))
                    nc.vector.tensor_tensor(hT[:], aT[:], rt[:], ALU.mult).then_inc(s["h_kept"], 1)

                def alpha_in(u):
                    dve.wait_ge(s["ba_made"], u + 1)
                    tbv = tb[:, 0:GB * 2 * GH].rearrange("p (b h) -> p b h", h=2 * GH)
                    nc.vector.tensor_copy(ba[:, :, 0:GH], tbv[:, :, 0:GH])
                    ch.link(nc.vector.tensor_tensor(pos[:], tbv[:, :, GH:], w["dtb"][:].unsqueeze(1).to_broadcast([128, GB, GH]), ALU.add))
                    ch.link(nc.vector.tensor_scalar(ba[:, :, GH:], pos[:], -1.0, None, ALU.mult))
                    nc.vector.tensor_tensor(ba[:, :, GH:], ba[:, :, GH:], pos[:], ALU.max).then_inc(s["ba_kept"], 1)

                def alpha_one(u):
                    dve.wait_ge(s["ba_exp"], u + 1)
                    nc.vector.tensor_scalar(lo[:], ex[:, :, GH:], 1.0, None, ALU.add).then_inc(s["one_kept"], 1)

                def alpha_sum(u):
                    dve.wait_ge(s["ln_kept"], u + 1)
                    dve.wait_ge(s["be_stored"], u * 16 + 16)
                    ch.link(nc.vector.scalar_tensor_tensor(pos[:], pos[:], 0.0, lo[:], ALU.max, ALU.add))
                    ch.link(nc.vector.tensor_scalar(beta[:], ex[:, :, 0:GH], 1.0, None, ALU.add))
                    nc.vector.reciprocal(beta[:], beta[:])
                    nc.vector.tensor_tensor(pos[:], pos[:], c["expA"][:].unsqueeze(1).to_broadcast([128, GB, GH]),
                                            ALU.mult).then_inc(s["g_kept"], 1)

                def alpha_out(u):
                    dve.wait_ge(s["al_turned"], u + 1)
                    dve.wait_ge(s["al_stored"], u * 16 + 16)
                    nc.vector.tensor_copy(alT[:, 1:], tb[0:GB * GH, 1:T]).then_inc(s["al_out"], 1)

                for t in (p, pT, vm, v, coh, rz, aT, hT, beta):
                    nc.vector.memset(t[:], 0.0)
                nc.vector.memset(zs[:], 1.0)
                nc.vector.memset(y_ps[:], 0.0)
                nc.vector.memset(alT[:], 0.0).then_inc(s["primed"], 1)
                dve.wait_ge(s["primed"], 1)
                dve.sem_inc(s["z_kept"], 1)
                dve.sem_inc(s["pt_kept"], 1)
                keep_c1(0)
                keep_v(0, 0)
                keep_z(0)
                coherence(0, 0)
                before = ch.n
                with dve.Fori(0, TURNS) as it:
                    ch.turn(it, 2 * LINKS_TURN, before)
                    for half in range(2):
                        u = it * 2 + half
                        for b in range(GB):
                            n = u * GB + b
                            for i in range(HQ):
                                peaks(n, b % 2, i)
                                if i == 0:
                                    factors(n * HQ + EXP0, (b + 1) % 2, HQ - 1, half if b else 1 - half, (b - 1) % GB)
                                else:
                                    factors(n * HQ + i + EXP0, b % 2, i - 1, half, b)
                                keep_turned(n, i)
                                if b == 0 and i == 0:
                                    keep_c1(u + 1)
                                if b == 1 and i == 3:
                                    square(u)
                                    keep_v(u + 1, 1 - half)
                                if b == 2 and i == 1:
                                    norm(u)
                                if b == 3 and i == 0:
                                    alpha_in(u)
                                if b == 3 and i == 1:
                                    alpha_one(u)
                                if b == 3 and i == 2:
                                    keep_z(u + 1)
                                    alpha_sum(u)
                                if b == 3 and i == 3:
                                    coherence(u + 1, 1 - half)
                                    alpha_out(u)
                assert ch.n == 2 * LINKS_TURN, ch.n
                ch.turn(0, 0, before + GROUPS * LINKS_TURN)
                factors(B * HQ + EXP0, 1, HQ - 1, 1, GB - 1)
                for i in range(HQ):
                    keep_turned(B, i)
                square(GROUPS)
                norm(GROUPS)
                alpha_in(GROUPS)
                alpha_one(GROUPS)
                alpha_sum(GROUPS)
                alpha_out(GROUPS)


def delta_rule(nc, w, dram):
    H, HH = 8, 4
    BL, NB = 32, 4
    AHEAD = RING = 8
    EPS = 1e-6
    ROW_TURNS = B // RING
    ROWS = {(0, 0): (1, 8), (0, 1): (8, 12), (0, 2): (12, 15), (0, 3): (15, 17), (1, 0): (17, 19), (1, 1): (19, 21),
            (1, 2): (21, 23), (1, 3): (23, 24), (2, 0): (24, 25), (2, 1): (25, 26), (2, 2): (26, 27), (2, 3): (27, 28),
            (3, 0): (28, 30), (3, 1): (30, BL)}
    with ExitStack() as ctx:
        m = Memory(nc, ctx, "delta")
        hk = m.sb("hk", [128, 2, T])
        hv = m.sb("hv", [128, 2, T])
        aT = m.sb("aT", [128, 2, T])
        xo = m.sb("xo", [128, 2, T])
        al = m.sb("al", [128, 2, H * T])
        ball = m.sb("ball", [128, GROUPS + 1, GB * H])
        bt = m.sb("bt", [128, H])
        kq = m.sb("kq", [128, 2, H, 2 * T])
        sq = m.sb("sq", [128, H, 2 * T])
        nrow = m.sb("nrow", [128, 2 * T])
        arg = m.sb("arg", [128, 2 * H])
        rt = m.sb("rt", [128, 2 * H])
        qe = m.sb("qe", [128, RING, H])
        qn = m.sb("qn", [128, H])
        kn = m.sb("kn", [128, RING, H])
        ck = m.sb("ck", [128, H])
        dc = m.sb("dc", [128, 2, H, T])
        la = m.sb("la", [128, RING, H, 2 * T])
        ll = m.sb("ll", [128, BL, BL])
        dd = m.sb("dd", [128, BL, BL])
        prod = m.sb("prod", [128, BL * BL])
        di = m.sb("di", [128, 2, GB * H, T])
        ct = m.sb("ct", [128, H, T])
        ad = m.sb("ad", [128, H, T])
        sv = m.sb("sv", [128, H, T])
        z = m.sb("z", [128, H, T])
        gw = m.sb("gw", [128, H, T])
        og = m.sb("og", [128, H, T])
        oT = m.sb("oT", [128, H, T])
        carry = m.sb("carry", [128, 2])
        ms = m.sb("ms", [128, H])
        x_ps = [m.ps(f"xp{i}", [128, HH, 2 * T]) for i in range(2)]
        z_ps = [m.ps(f"zp{i}", [128, HH, T]) for i in range(2)]
        n_ps = m.ps("np", [128, GT])
        w_ps = m.ps("wp", [128, HH, T])
        k_rows, k_cols, q_cols = n_ps[:, 0:2 * T], n_ps[:, 256:256 + H], n_ps[:, 256 + H:256 + 2 * H]
        ring2 = lambda name: [m.sem(f"{name}{i}") for i in range(2)]
        hk_in, hv_in, at_in, al_in, x_stored, lanes_out, inv_in = (ring2(n) for n in (
            "hk_in", "hv_in", "at_in", "al_in", "x_stored", "lanes_out", "inv_in"))
        names = ("beta_in ll_in pre_made pre_kept pre_root inv_out primed kq_made kq_kept sq_kept n_made nrow_kept ncol_made ck_made diag_made kkq_made la_kept "
                 "ca_made c_kept ad_kept g_made g_kept gw_made v_made v_kept r_made z_made z_kept o_made osq_kept og_kept "
                 "arg_made root_made rs_made o_done ot_made ot_kept wo_made x_kept dd_made chain").split()
        s = {n: m.sem(n) for n in names}

        class Row:

            def __init__(self, t, k):
                self.n, self.two, self.four = t * RING + k, t * (RING // 2) + k // 2, t * (RING // GB) + k // GB
                self.half, self.pair, self.b, self.slot = k % 2, k // GB % 2, k % GB, k % RING
                self.group = bass.ds(self.four + 1, 1)
                self.group_v = bass.ds((t + 1) * (RING // GB) + (k // GB - 1), 1)

        def turns(eng, step, begin=lambda t: None):
            with eng.Fori(0, ROW_TURNS - 1) as t:
                begin(t)
                for k in range(RING):
                    step(t, k)
            begin(ROW_TURNS - 1)
            for k in range(RING):
                step(ROW_TURNS - 1, k)

        def looped(t):
            return not isinstance(t, int)

        heads = [slice(i * HH, (i + 1) * HH) for i in range(2)]

        with nc.Block() as block:
            @block.sync
            def _(sp):
                def load_tokens(buf, src, r, sem):
                    sp.dma_start(buf[:, r.half, :], dram[src][r.group_v if buf is hv else r.group, :, r.b * T:(r.b + 1) * T].squeeze(0)).then_inc(sem[r.half], 16)

                def load_alpha(r):
                    sp.dma_start(al[:, r.half, :], dram["alpha"][r.group, r.b * H:(r.b + 1) * H, :].rearrange("u h t -> u (h t)")
                                 .to_broadcast([128, H * T])).then_inc(al_in[r.half], 16)

                def store_lanes(p):
                    sp.wait_ge(s["la_kept"], p.n * 2 + 2)
                    for g in range(NB):
                        sp.dma_start(dram["lanes"][p.pair, g, p.b * H:(p.b + 1) * H, :, :].rearrange("h j i -> j h i"),
                                     la[g * BL:(g + 1) * BL, p.slot, :, g * BL:(g + 1) * BL]).then_inc(lanes_out[p.half], 16)

                def load_lanes(p, before):
                    for half in range(2):
                        sp.wait_ge(lanes_out[half], p.four * 128 + 128)
                    if before:
                        sp.wait_ge(s["dd_made"], p.four)
                    sp.dma_start(ll[:].rearrange("p j i -> p (j i)"),
                                 dram["lanes"][p.pair, :, :, :, :].rearrange("g h j i -> (g h) (j i)")).then_inc(s["ll_in"], 16)

                def move_inverses(p):
                    sp.wait_ge(s["dd_made"], p.four + 1)
                    sp.dma_start(dram["inverses"][p.pair, :, :, :, :].rearrange("g h i j -> (g h) (i j)"),
                                 dd[:].rearrange("p i j -> p (i j)")).then_inc(s["inv_out"], 16)
                    sp.wait_ge(s["inv_out"], p.four * 16 + 16)
                    for g in range(NB):
                        sp.dma_start(di[g * BL:(g + 1) * BL, p.pair, :, g * BL:(g + 1) * BL],
                                     dram["inverses"][p.pair, g, :, :, :].rearrange("h i j -> i h j")).then_inc(inv_in[p.pair], 16)

                def store_x(r):
                    sp.wait_ge(s["x_kept"], r.n + 2)
                    sp.dma_start(dram["xpT"][r.group, :, r.b * T:(r.b + 1) * T].squeeze(0), xo[:, r.half, :]).then_inc(x_stored[r.half], 16)

                def step(t, k):
                    r = Row(t, k)
                    load_tokens(aT, "aT", r, at_in)
                    if looped(t):
                        sp.wait_ge(s["la_kept"], r.n * 2 + 2 * AHEAD)
                        load_alpha(Row(t, k + AHEAD + 1))
                        sp.wait_ge(s["n_made"], r.n + AHEAD + 1)
                        load_tokens(hk, "hT", Row(t, k + AHEAD + 2), hk_in)
                    store_x(Row(t, k - 1))
                    if looped(t) or k + 2 < RING:
                        sp.wait_ge(s["g_made"], r.n * 2 + 2)
                        load_tokens(hv, "hT", Row(t, k + 2), hv_in)
                    if k % GB == GB - 1 and (looped(t) or k + 1 < RING):
                        move_inverses(Row(t, k + 1))
                    if looped(t):
                        p = Row(t, k + AHEAD)
                        store_lanes(p)
                        if p.b == GB - 1:
                            load_lanes(p, True)

                sp.dma_start(ball[:], dram["beta"][1:GROUPS + 2, :, :].rearrange("g t h -> t g h")).then_inc(s["beta_in"], 16)
                for k in range(2):
                    load_tokens(hk, "hT", Row(0, k), hk_in)
                    load_alpha(Row(0, k))
                for k in range(2):
                    load_tokens(hv, "hT", Row(0, k), hv_in)
                load_tokens(aT, "aT", Row(0, -1), at_in)
                sp.wait_ge(s["primed"], 1)
                for half in range(2):
                    sp.dma_start(dram["xpT"][GROUPS + 1, :, half * T:(half + 1) * T], xo[:, half, :]).then_inc(x_stored[half], 16)
                for k in range(AHEAD):
                    sp.wait_ge(s["n_made"], k + 1)
                    load_tokens(hk, "hT", Row(0, k + 2), hk_in)
                    store_lanes(Row(0, k))
                    if k + 2 <= AHEAD:
                        load_alpha(Row(0, k + 2))
                    if k == GB - 1:
                        load_lanes(Row(0, k), False)
                move_inverses(Row(0, 0))
                load_lanes(Row(0, RING - 1), True)
                turns(sp, step)
                store_x(Row(ROW_TURNS - 1, RING - 1))
                for half in range(2):
                    sp.wait_ge(x_stored[half], 16 * (B // 2 + 1 + half))
                    sp.wait_ge(hk_in[half], 16 * (B // 2 + 1))
                sp.wait_ge(al_in[0], 16 * (B // 2 + 1))

            @block.tensor
            def _(pe):
                def project(ps, p, heads):
                    for j, h in enumerate(heads):
                        nc.tensor.matmul(ps[:, j, 0:T], w["dWk"][:, h * T:(h + 1) * T], hk[:, p.half, :], start=True, stop=True)
                        last = nc.tensor.matmul(ps[:, j, T:], w["dWq"][:, h * T:(h + 1) * T], hk[:, p.half, :], start=True, stop=True)
                    return last

                def project_kq(p, i):
                    if i == 0:
                        pe.wait_ge(hk_in[p.half], p.two * 16 + 16)
                    project(x_ps[i], p, range(i * HH, (i + 1) * HH)).then_inc(s["kq_made"], 1)

                def project_ahead(p):
                    pe.wait_ge(hk_in[p.half], p.two * 16 + 16)
                    for i in range(4):
                        if p.n * 4 + i > 1:
                            pe.wait_ge(s["pre_kept"], p.n * 4 + i - 1)
                        project(z_ps[i % 2][:].rearrange("p (h a) t -> p h (a t)", a=2), p, range(2 * i, 2 * i + 2)).then_inc(s["pre_made"], 1)

                def norms(p, before=True):
                    pe.wait_ge(s["sq_kept"], p.n + 1)
                    if before:
                        pe.wait_ge(s["ck_made"], p.n)
                    for a in range(2):
                        for g in range(4):
                            last = nc.tensor.matmul(k_rows[g * 32:(g + 1) * 32, :], w["headrow"][:, a, :], sq[:, g + 4 * a, :],
                                                    start=(a == 0), stop=(a == 1))
                    last.then_inc(s["n_made"], 1)

                def norm_columns(p):
                    pe.wait_ge(s["nrow_kept"], p.n + 1)
                    nc.tensor.matmul(k_cols, nrow[:, 0:T], w["headpick"][:], start=True, stop=True)
                    nc.tensor.matmul(q_cols, nrow[:, T:], w["headpick"][:], start=True, stop=True).then_inc(s["ncol_made"], 1)

                def key_products(p, i):
                    for j, h in enumerate(range(i * HH, (i + 1) * HH)):
                        last = nc.tensor.matmul(x_ps[i][:, j, :], kq[:, p.half, h, 0:T], kq[:, p.half, h, :], start=True, stop=True)
                    last.then_inc(s["kkq_made"], 1)

                def invert(r, i):
                    for j, h in enumerate(range(i * HH, (i + 1) * HH)):
                        last = nc.tensor.matmul(x_ps[i][:, j, :], di[:, r.pair, r.b * H + h, :], la[:, r.slot, h, :], start=True, stop=True)
                    last.then_inc(s["ca_made"], 1)

                def project_gate(r, i):
                    pe.wait_ge(s["v_kept"], r.n * 2 + i + 1)
                    nc.tensor.matmul(z_ps[i][:].rearrange("p h t -> p (h t)"), hv[:, r.half, :], w["dWg"][:, i * GT:(i + 1) * GT],
                                     start=True, stop=True).then_inc(s["g_made"], 1)

                def project_v(r, i):
                    if i == 0:
                        pe.wait_ge(hv_in[r.half], r.two * 16 + 16)
                    pe.wait_ge(s["og_kept"], r.n * 2 + i + 1)
                    nc.tensor.matmul(z_ps[i][:].rearrange("p h t -> p (h t)"), hv[:, r.half, :], w["dWv"][:, i * GT:(i + 1) * GT],
                                     start=True, stop=True).then_inc(s["v_made"], 1)

                def correct(r, round, i):
                    if round == 0:
                        pe.wait_ge(s["c_kept"], r.n * 2 + i + 1)
                        pe.wait_ge(s["g_kept"], r.n * 2 + i + 1)
                        pe.wait_ge(s["r_made"], r.n + 1)
                    else:
                        pe.wait_ge(s["z_kept"], r.n * 6 + 2 * round + i - 1)
                    for j, h in enumerate(range(i * HH, (i + 1) * HH)):
                        last = nc.tensor.matmul(z_ps[i][:, j, :], ct[:, h, :], (z if round else sv)[:, h, :], start=True, stop=True)
                    last.then_inc(s["z_made"], 1)

                def attend(r, i):
                    pe.wait_ge(s["z_kept"], r.n * 6 + i + 5)
                    pe.wait_ge(s["ad_kept"], r.n * 2 + i + 1)
                    for j, h in enumerate(range(i * HH, (i + 1) * HH)):
                        last = nc.tensor.matmul(z_ps[i][:, j, :], ad[:, h, :], z[:, h, :], start=True, stop=True)
                    last.then_inc(s["o_made"], 1)

                def turn_output(r, i):
                    if i == 0:
                        pe.wait_ge(s["o_done"], r.n + 2)
                    else:
                        pe.wait_ge(s["ot_kept"], r.n * 2 + 3)
                    for j, h in enumerate(range(i * HH, (i + 1) * HH)):
                        last = nc.tensor.transpose(w_ps[:, j, :], og[:, h, :], w["ident"][:])
                    last.then_inc(s["ot_made"], 1)

                def output(r):
                    pe.wait_ge(s["ot_kept"], r.n * 2 + 4)
                    for h in range(H):
                        last = nc.tensor.matmul(w_ps[:, 0, :], w["dWo"][:, h, :], oT[:, h, :], start=(h == 0), stop=(h == H - 1))
                    last.then_inc(s["wo_made"], 1)

                def step(t, k):
                    r, q, p, before = Row(t, k), Row(t, k + AHEAD), Row(t, k + AHEAD + 1), Row(t, k - 1)
                    if r.b == 0:
                        pe.wait_ge(inv_in[r.pair], (t + 1) * 16 * NB)
                    for i in range(2):
                        if looped(t) or k == 0:
                            pe.wait_ge(s["sq_kept"], r.n + AHEAD + 1)
                        else:
                            pe.wait_ge(s["ad_kept"], (r.n - 1) * 2 + i + 1)
                        invert(r, i)
                    for i in range(2):
                        project_v(r, i)
                    for i in range(2):
                        if looped(t):
                            pe.wait_ge(s["ad_kept"], r.n * 2 + i + 1)
                            key_products(q, i)
                        if i == 0:
                            project_gate(r, 0)
                            project_gate(r, 1)
                    for i in range(2):
                        correct(r, 0, i)
                    if looped(t):
                        pe.wait_ge(s["la_kept"], q.n * 2 + 1)
                        project_kq(p, 0)
                    turn_output(before, 0)
                    for i in range(2):
                        correct(r, 1, i)
                    if looped(t):
                        pe.wait_ge(s["la_kept"], q.n * 2 + 2)
                        project_kq(p, 1)
                    turn_output(before, 1)
                    for i in range(2):
                        correct(r, 2, i)
                    output(before)
                    if looped(t):
                        norms(p)
                    for i in range(2):
                        attend(r, i)
                    if looped(t):
                        norm_columns(p)

                project_ahead(Row(0, 0))
                for k in range(AHEAD + 1):
                    p = Row(0, k)
                    norms(p, k > 0)
                    if k < AHEAD:
                        project_ahead(Row(0, k + 1))
                    norm_columns(p)
                    if k < AHEAD:
                        for i in range(2):
                            if k:
                                pe.wait_ge(s["la_kept"], 2 * k + i - 1)
                            key_products(p, i)
                pe.wait_ge(s["la_kept"], 2 * AHEAD)
                pe.wait_ge(s["pre_kept"], 4 * AHEAD + 4)
                pe.wait_ge(s["primed"], 1)
                turns(pe, step)
                last = Row(ROW_TURNS - 1, RING - 1)
                for i in range(2):
                    turn_output(last, i)
                output(last)

            @block.scalar
            def _(act):
                def square(p):
                    nc.scalar.activation(sq[:], kq[:, p.half, :, :], ACT.Square).then_inc(s["sq_kept"], 1)

                def keep_ahead(p):
                    for i in range(4):
                        act.wait_ge(s["pre_made"], p.n * 4 + i + 1)
                        nc.scalar.activation(kq[:, p.half, 2 * i:2 * i + 2, :].rearrange("p h t -> p (h t)"),
                                             z_ps[i % 2][:].rearrange("p h t -> p (h t)"), ACT.Silu).then_inc(s["pre_kept"], 1)
                    act.wait_ge(s["pre_kept"], p.n * 4 + 4)
                    square(p)

                def keep_kq(p, i):
                    act.wait_ge(s["kq_made"], (p.n - AHEAD - 1) * 2 + i + 1)
                    nc.scalar.activation(kq[:, p.half, heads[i], :], x_ps[i][:], ACT.Silu).then_inc(s["kq_kept"], 1)

                def keep_v(r):
                    for i in range(2):
                        act.wait_ge(s["v_made"], r.n * 2 + i + 1)
                        nc.scalar.activation(sv[:, heads[i], :], z_ps[i][:], ACT.Silu).then_inc(s["v_kept"], 1)

                def turn_kept(r, i):
                    act.wait_ge(s["ot_made"], r.n * 2 + i + 3)
                    nc.scalar.copy(oT[:, heads[i], :], w_ps[:]).then_inc(s["ot_kept"], 1)

                def step(t, k):
                    r, p, before = Row(t, k), Row(t, k + AHEAD + 1), Row(t, k - 1)
                    for i in range(2):
                        act.wait_ge(s["c_kept"], r.n * 2 + i + 1)
                        nc.scalar.copy(ad[:, heads[i], :], x_ps[i][:, :, T:]).then_inc(s["ad_kept"], 1)
                    keep_v(r)
                    for i in range(2):
                        act.wait_ge(s["g_made"], r.n * 2 + i + 1)
                        nc.scalar.activation(gw[:, heads[i], :], z_ps[i][:], ACT.Silu).then_inc(s["g_kept"], 1)
                    if looped(t):
                        keep_kq(p, 0)
                    turn_kept(before, 0)
                    if looped(t):
                        keep_kq(p, 1)
                    turn_kept(before, 1)
                    if looped(t):
                        act.wait_ge(s["kq_kept"], (p.n - AHEAD - 1) * 2 + 2)
                        square(p)
                    for i in range(2):
                        act.wait_ge(s["o_made"], r.n * 2 + i + 1)
                        for j in range(HH):
                            last = nc.scalar.activation(sq[:, i * HH + j, 0:T], z_ps[i][:, j, :], ACT.Square, scale=T ** -0.5,
                                                        accum_out=ms[:, i * HH + j:i * HH + j + 1])
                        last.then_inc(s["osq_kept"], 1)
                    act.wait_ge(s["arg_made"], r.n + 2)
                    nc.scalar.activation(rt[:], arg[:], ACT.Sqrt).then_inc(s["root_made"], 1)

                for k in range(AHEAD + 1):
                    keep_ahead(Row(0, k))
                act.wait_ge(s["arg_made"], 1)
                nc.scalar.activation(kn[:], kn[:], ACT.Sqrt).then_inc(s["pre_root"], 1)
                nc.scalar.activation(rt[:, 0:H], arg[:, 0:H], ACT.Sqrt).then_inc(s["root_made"], 1)
                turns(act, step)
                for i in range(2):
                    turn_kept(Row(ROW_TURNS - 1, RING - 1), i)

            @block.gpsimd
            def _(pool):
                def diagonal(p):
                    pool.wait_ge(s["ck_made"], p.n + 1)
                    nc.gpsimd.tensor_tensor(dc[:, p.half, :, :], w["ident"][:].unsqueeze(1).to_broadcast([128, H, T]),
                                            ck[:].unsqueeze(2).to_broadcast([128, H, T]), ALU.mult).then_inc(s["diag_made"], 1)

                def scale_v(r):
                    pool.wait_ge(s["v_kept"], r.n * 2 + 2)
                    nc.gpsimd.tensor_tensor(sv[:], sv[:], kn[:, r.slot, :].unsqueeze(2).to_broadcast([128, H, T]),
                                            ALU.mult).then_inc(s["r_made"], 1)

                def step(t, k):
                    r, p = Row(t, k), Row(t, k + AHEAD + 1)
                    scale_v(r)
                    pool.wait_ge(s["g_kept"], r.n * 2 + 2)
                    nc.gpsimd.tensor_tensor(gw[:], gw[:], w["onw"][:].unsqueeze(1).to_broadcast([128, H, T]),
                                            ALU.mult).then_inc(s["gw_made"], 1)
                    pool.wait_ge(s["og_kept"], r.n * 2 + 4)
                    pool.wait_ge(s["rs_made"], r.n + 1)
                    nc.gpsimd.tensor_tensor(og[:], og[:], rt[:, H:].unsqueeze(2).to_broadcast([128, H, T]),
                                            ALU.mult).then_inc(s["o_done"], 1)
                    if looped(t):
                        diagonal(p)

                nc.gpsimd.memset(di[:], 0.0)
                nc.gpsimd.memset(xo[:], 0.0)
                nc.gpsimd.memset(og[:], 0.0).then_inc(s["primed"], 1)
                pool.wait_ge(s["primed"], 1)
                pool.sem_inc(s["o_done"], 1)
                for k in range(AHEAD + 1):
                    diagonal(Row(0, k))
                pool.wait_ge(s["pre_root"], 1)
                turns(pool, step)

            @block.vector
            def _(dve):
                ch = Chain(dve, s["chain"])

                def keep_rows(p):
                    ch.link(nc.vector.tensor_scalar(bt[:], ball[:].rearrange("p g h -> p (g h)")[:, bass.ds(p.n * H, H)], 0.0, None, ALU.add))
                    dve.wait_ge(s["n_made"], p.n + 1)
                    nc.vector.tensor_copy(nrow[:], k_rows).then_inc(s["nrow_kept"], 1)

                def keep_columns(p, squares, eps_q):
                    dve.wait_ge(s["ncol_made"], p.n + 1)
                    ch.link(nc.vector.tensor_scalar(squares, k_cols, EPS, None, ALU.add))
                    nc.vector.tensor_scalar(eps_q, q_cols, EPS, EPS * T, ALU.add, ALU.mult)
                    ch.link(nc.vector.reciprocal(ck[:], squares))
                    nc.vector.tensor_tensor(ck[:], ck[:], bt[:], ALU.mult).then_inc(s["ck_made"], 1)

                def decays(p):
                    dve.wait_ge(s["diag_made"], p.n + 1)
                    dve.wait_ge(al_in[p.half], p.two * 16 + 16)
                    dcf = dc[:, p.half, :, :].rearrange("p h t -> p (h t)")
                    ch.link(nc.vector.tensor_tensor_scan(dcf, al[:, p.half, :], dcf, 0.0, ALU.mult, ALU.add))

                def keep_la(p):
                    for i in range(2):
                        dve.wait_ge(s["kkq_made"], p.n * 2 + i + 1)
                        nc.vector.tensor_tensor(la[:, p.slot, heads[i], :].rearrange("p h (a t) -> p h a t", t=T),
                                                x_ps[i][:].rearrange("p h (a t) -> p h a t", t=T),
                                                dc[:, p.half, heads[i], :].unsqueeze(2).to_broadcast([128, HH, 2, T]), ALU.mult).then_inc(s["la_kept"], 1)

                def inverses(p, first, end, before):
                    if first == 1:
                        dve.wait_ge(s["ll_in"], p.four * 16 + 16)
                        if before:
                            dve.wait_ge(s["inv_out"], p.four * 16)
                    for i in range(first, end):
                        pr = prod[:, 0:i * i].rearrange("p (j a) -> p j a", a=i)
                        ch.link(nc.vector.tensor_tensor(pr, dd[:, 0:i, 0:i].rearrange("p a j -> p j a"),
                                                        ll[:, 0:i, i].unsqueeze(1).to_broadcast([128, i, i]), ALU.mult))
                        last = nc.vector.tensor_reduce(dd[:, i, 0:i], pr, AX.X, ALU.add, negate=True)
                        if i < BL - 1:
                            ch.link(last)
                        else:
                            last.then_inc(s["dd_made"], 1)

                def residual(r):
                    dve.wait_ge(s["wo_made"], r.n + 2)
                    dve.wait_ge(at_in[r.half], (r.two + 1 + r.half) * 16)
                    dve.wait_ge(x_stored[r.half], (r.two + 1 + r.half) * 16)
                    nc.vector.tensor_tensor(xo[:, r.half, :], aT[:, r.half, :], w_ps[:, 0, :], ALU.add).then_inc(s["x_kept"], 1)

                def step(t, k):
                    r, q, p, before = Row(t, k), Row(t, k + AHEAD), Row(t, k + AHEAD + 1), Row(t, k - 1)
                    group = Row(t, (k // GB + 1) * GB)

                    def part(place):
                        if (k % GB, place) in ROWS and (looped(t) or k < GB):
                            inverses(group, *ROWS[k % GB, place], True)

                    def correct(round):
                        for i in range(2):
                            dve.wait_ge(s["z_made"], r.n * 6 + 2 * round + i + 1)
                            nc.vector.tensor_tensor(z[:, heads[i], :], sv[:, heads[i], :], z_ps[i][:], ALU.subtract).then_inc(s["z_kept"], 1)

                    for i in range(2):
                        dve.wait_ge(s["ca_made"], r.n * 2 + i + 1)
                        nc.vector.tensor_tensor(ct[:, heads[i], :], x_ps[i][:, :, 0:T],
                                                w["offblock"][:].unsqueeze(1).to_broadcast([128, HH, T]), ALU.mult).then_inc(s["c_kept"], 1)
                    if looped(t):
                        decays(q)
                    part(0)
                    if looped(t):
                        keep_la(q)
                    correct(0)
                    part(1)
                    correct(1)
                    part(2)
                    correct(2)
                    residual(before)
                    part(3)
                    if looped(t):
                        keep_rows(p)
                    for i in range(2):
                        dve.wait_ge(s["osq_kept"], r.n * 2 + i + 1)
                        if i == 0:
                            dve.wait_ge(s["gw_made"], r.n + 1)
                        nc.vector.tensor_tensor(og[:, heads[i], :], z_ps[i][:], gw[:, heads[i], :], ALU.mult).then_inc(s["og_kept"], 1)
                    last = nc.vector.tensor_tensor(arg[:, H:], ms[:], qe[:, r.slot, :], ALU.add)
                    if looped(t):
                        ch.link(last)
                        nc.vector.tensor_copy(kn[:, r.slot, :], rt[:, 0:H])
                        nc.vector.tensor_copy(qe[:, r.slot, :], qn[:])
                        keep_columns(p, arg[:, 0:H], qn[:])
                        last = nc.vector.memset(carry[:, r.half:r.half + 1], 0.0)
                    last.then_inc(s["arg_made"], 1)
                    dve.wait_ge(s["root_made"], r.n + 2)
                    nc.vector.reciprocal(rt[:, H:], rt[:, H:]).then_inc(s["rs_made"], 1)

                nc.vector.memset(arg[:], 1.0)
                ch.link(nc.vector.memset(dd[:], 0.0))
                ch.link(nc.vector.memset(dd[:].rearrange("p i j -> p (i j)")[:, 0:BL * BL:BL + 1], 1.0))
                dve.sem_inc(s["og_kept"], 2)
                dve.wait_ge(s["beta_in"], 16)
                for k in range(AHEAD + 1):
                    p = Row(0, k)

                    def part(place):
                        n = (k - GB) * 3 + place
                        if 0 <= n < len(ROWS):
                            inverses(Row(0, 0), *list(ROWS.values())[n], False)

                    keep_rows(p)
                    part(0)
                    if k == AHEAD:
                        keep_columns(p, arg[:, 0:H], qn[:])
                    else:
                        keep_columns(p, kn[:, p.slot, :], qe[:, p.slot, :])
                        part(1)
                        decays(p)
                        keep_la(p)
                        part(2)
                for n in range((AHEAD - GB) * 3 + 1, len(ROWS)):
                    inverses(Row(0, 0), *list(ROWS.values())[n], False)
                nc.vector.memset(carry[:, 1:2], 0.0).then_inc(s["arg_made"], 1)
                before = ch.n
                links = RING * 5 + RING // GB * (2 * BL - 3)
                turns(dve, step, lambda t: ch.turn(t, links, before))
                residual(Row(ROW_TURNS - 1, RING - 1))


def last_layer(nc, w, dram):
    HT = 4
    Q = 32
    A16, W8 = 32767.0, 127.0
    ROUND = 1.5 * 2.0 ** 23
    EPS, TINY = 1e-6, 1e-8
    with ExitStack() as ctx:
        m = Memory(nc, ctx, "last")
        xp = m.sb("xp", [128, 2, GT])
        x2 = m.sb("x2", [128, 2, GT])
        xs = m.sb("xs", [128, 2, GT])
        sq = m.sb("sq", [128, GT])
        r2 = m.sb("r2", [128, 2, GT])
        rl = m.sb("rl", [128, HT, GT])
        f2 = m.sb("f2", [128, 2, HT, GT])
        x3 = m.sb("x3", [128, 2, GT])
        x3b = m.sb("x3b", [128, GROUPS * GT])
        xr = m.sb("xr", [128, GROUPS * GT])
        xi = m.sb("xi", [128, 2, GT])
        hid = m.sb("hid", [128, GROUPS * HT * GT])
        out = m.sb("out", [128, 2, GT])
        rotT = m.sb("rotT", [128, D])
        side = m.sb("side", [128, 2, 4, Q])
        qsq = m.sb("qsq", [128, B + 4])
        qn = m.sb("qn", [128, 2])
        qc = m.sb("qc", [128, 2, 4])
        win = m.sb("win", [128, HT, D])
        wq = m.sb("wq", [128, 2, HT, D])
        wsc = m.sb("wsc", [128, 2, HT])
        gsc = m.sb("gsc", [128, HT])
        am = m.sb("am", [128, GROUPS])
        peak = m.sb("peak", [128, 1])
        one = m.sb("one", [1, 1])
        sc = m.sb("sc", [128, 2])
        isc = m.sb("isc", [128, 1])
        shift = m.sb("shift", [128, 1])
        carry = m.sb("carry", [128, 2])
        carry_a = m.sb("carry_a", [128, 2])
        f_ps = [m.ps(f"fp{j}", [128, GT]) for j in range(HT)]
        ms_ps, y_ps, r_ps, s_ps = (m.ps(n, [128, GT]) for n in ("msp", "yp", "rp", "sp"))
        h_ps = [f_ps, [ms_ps, y_ps, r_ps, s_ps]]
        o_ps = [y_ps, r_ps]
        x_in = [m.sem(f"x_in{i}") for i in range(2)]
        out_stored = [m.sem(f"out_stored{i}") for i in range(2)]
        names = ("primed q_made q_root sides_made rot_made rot_kept win_made win_turned win_kept sq_kept fc_made rl_kept "
                 "f2_low f2_high ms_made r2_kept xs_made y_made y_kept x3_kept x3b_kept xr_made xr_kept am_made peak_made peak_turned "
                 "one_made one_spread scaled xi_rounded xi_made h_made h_kept t_made t_low t_high o_made o_kept chain").split()
        s = {n: m.sem(n) for n in names}

        class Group:

            def __init__(self, it, k):
                self.n, self.half = it * 2 + k, k % 2
                self.loads, self.stores = it * 32 + k // 2 * 32 + 32, it * 16 + k // 2 * 16 + 16

            def of(self, size):
                return bass.ds(self.n * size, size)

        def groups(eng, first, second, begin=lambda it: None):
            first(Group(0, 0))
            with eng.Fori(0, TURNS - 1) as it:
                begin(it)
                for k in range(2):
                    first(Group(it, k + 1))
                    second(Group(it, k))
            begin(TURNS - 1)
            first(Group(TURNS - 1, 1))
            second(Group(TURNS - 1, 0))
            second(Group(TURNS - 1, 1))

        with nc.Block() as block:
            @block.sync
            def _(sp):
                def load(g):
                    slot = bass.ds(g.n + 1, 1)
                    sp.dma_start(xp[:, g.half, :], dram["xpT"][slot, :, :].squeeze(0)).then_inc(x_in[g.half], 16)
                    sp.dma_start(x2[:, g.half, :], dram["x2T"][slot, :, :].squeeze(0)).then_inc(x_in[g.half], 16)

                def store(g):
                    sp.wait_ge(s["o_kept"], g.n + 1)
                    sp.dma_start(dram["outT"][bass.ds(g.n, 1), :, :].squeeze(0), out[:, g.half, :]).then_inc(out_stored[g.half], 16)

                load(Group(0, 0))
                load(Group(0, 1))
                sp.wait_ge(s["primed"], 1)
                for half in range(2):
                    sp.dma_start(dram["xpT"][GROUPS + 1, :, :], out[:, half, :]).then_inc(out_stored[half], 16)
                    sp.wait_ge(out_stored[half], 16)
                with sp.Fori(0, TURNS - 1) as it:
                    for k in range(2):
                        sp.wait_ge(s["xs_made"], it * 2 + k + 1)
                        sp.wait_ge(s["sq_kept"], it * 2 + k + 1)
                        sp.wait_ge(s["fc_made"], (it * 2 + k) * HT + HT)
                        load(Group(it, k + 2))
                with sp.Fori(0, TURNS) as it:
                    for k in range(2):
                        store(Group(it, k))
                for half in range(2):
                    sp.wait_ge(out_stored[half], 16 * (TURNS + 1))

            @block.tensor
            def _(pe):
                def feed(g):
                    pe.wait_ge(x_in[g.half], g.loads)
                    for j in range(HT):
                        pe.wait_ge(s["rl_kept"], g.n * HT + j + 1)
                        nc.tensor.matmul(f_ps[j][:], w["Wfc"][:, j * D:(j + 1) * D], xp[:, g.half, :], start=True, stop=True).then_inc(s["fc_made"], 1)
                    pe.wait_ge(s["sq_kept"], g.n + 1)
                    pe.wait_ge(s["r2_kept"], g.n + 1)
                    nc.tensor.matmul(ms_ps[:], w["mean"][:], sq[:], start=True, stop=True).then_inc(s["ms_made"], 1)

                def rotate(g):
                    pe.wait_ge(s["f2_low"], g.n + 2)
                    pe.wait_ge(s["f2_high"], g.n + 2)
                    pe.wait_ge(s["y_kept"], g.n + 1)
                    for j in range(HT):
                        last = nc.tensor.matmul(y_ps[:], w["Wproj"][:, j, :], f2[:, g.half, j, :], start=(j == 0), stop=(j == HT - 1))
                    last.then_inc(s["y_made"], 1)
                    pe.wait_ge(s["x3_kept"], g.n + 3)
                    pe.wait_ge(s["xr_kept"], g.n + 1)
                    nc.tensor.matmul(r_ps[:], rotT[:], x3[:, g.half, :], start=True, stop=True).then_inc(s["xr_made"], 1)

                def spread(k):
                    pe.wait_ge(s["peak_made"], k + 1)
                    nc.tensor.matmul(s_ps[0:1, 0:128], peak[:], w["ident"][:], start=True, stop=True).then_inc(s["peak_turned"], 1)
                    pe.wait_ge(s["one_made"], k + 1)
                    nc.tensor.matmul(s_ps[:, 128:129], w["ones"][0:1, :], one[:], start=True, stop=True).then_inc(s["one_spread"], 1)

                def hidden(g):
                    pe.wait_ge(s["xi_made"], g.n + 1)
                    for j in range(HT):
                        last = nc.tensor.matmul(h_ps[g.half][j][:], win[:, j, :], xi[:, g.half, :], start=True, stop=True)
                    last.then_inc(s["h_made"], 1)

                def output(g):
                    pe.wait_ge(s["t_low"], g.n + 1)
                    pe.wait_ge(s["t_high"], g.n + 1)
                    for j in range(HT):
                        last = nc.tensor.matmul(o_ps[g.half][:], wq[:, 1, j, :], f2[:, g.half, j, :], start=(j == 0), stop=(j == HT - 1))
                    last.then_inc(s["o_made"], 1)

                pe.wait_ge(s["sides_made"], 1)
                nc.tensor.matmul(s_ps[:, 0:D], side[:, 0, :, :].rearrange("p c d -> p (c d)"), side[:, 1, :, :].rearrange("p c d -> p (c d)"),
                                 start=True, stop=True).then_inc(s["rot_made"], 1)
                pe.wait_ge(s["win_made"], 1)
                for j in range(HT):
                    last = nc.tensor.transpose(ms_ps[:, j * D:(j + 1) * D], wq[:, 0, j, :], w["ident"][:])
                last.then_inc(s["win_turned"], 1)
                pe.wait_ge(s["win_kept"], 1)
                pe.wait_ge(s["rot_kept"], 1)
                groups(pe, feed, rotate)
                spread(0)
                with pe.Fori(0, TURNS) as it:
                    for k in range(2):
                        hidden(Group(it, k))
                spread(1)
                with pe.Fori(0, TURNS) as it:
                    for k in range(2):
                        output(Group(it, k))

            @block.scalar
            def _(act):
                def feed(g):
                    for j in range(HT):
                        act.wait_ge(s["fc_made"], g.n * HT + j + 1)
                        act.wait_ge(s["f2_low" if j < 2 else "f2_high"], g.n + 1)
                        nc.scalar.activation(rl[:, j, :], f_ps[j][:], ACT.Relu).then_inc(s["rl_kept"], 1)
                        if j == 0:
                            nc.scalar.activation(sq[:], xp[:, g.half, :], ACT.Square).then_inc(s["sq_kept"], 1)

                def keep_x3(g):
                    act.wait_ge(s["x3_kept"], g.n + 3)
                    nc.scalar.copy(carry_a[:, g.half:g.half + 1], shift[:])
                    nc.scalar.activation(x3b[:, g.of(GT)], x3[:, g.half, :], ACT.Identity, bias=w["bout2"][:]).then_inc(s["x3b_kept"], 1)

                def keep_hidden(g):
                    act.wait_ge(s["h_made"], g.n + 1)
                    nc.scalar.copy(carry_a[:, g.half:g.half + 1], shift[:])
                    for j in range(HT):
                        last = nc.scalar.activation(hid[:, bass.ds(g.n * (HT * GT) + j * GT, GT)], h_ps[g.half][j][:], ACT.Gelu,
                                                    bias=w["bin"][:, j:j + 1], scale=gsc[:, j:j + 1])
                    last.then_inc(s["h_kept"], 1)

                def round_high(g):
                    act.wait_ge(s["t_made"], g.n + 1)
                    nc.scalar.activation(f2[:, g.half, 2:, :], f2[:, g.half, 2:, :], ACT.Identity, bias=shift[:]).then_inc(s["t_high"], 1)

                act.sem_inc(s["rl_kept"], HT)
                act.wait_ge(s["q_made"], 1)
                nc.scalar.activation(qn[:], qn[:], ACT.Sqrt).then_inc(s["q_root"], 1)
                groups(act, feed, keep_x3)
                act.wait_ge(s["x3b_kept"], GROUPS)
                act.wait_ge(s["scaled"], 1)
                with act.Fori(0, TURNS) as it:
                    for k in range(2):
                        keep_hidden(Group(it, k))
                with act.Fori(0, TURNS) as it:
                    for k in range(2):
                        round_high(Group(it, k))

            @block.gpsimd
            def _(pool):
                def feed(g):
                    pool.wait_ge(x_in[g.half], g.loads)
                    pool.wait_ge(s["x3_kept"], g.n + 1)
                    nc.gpsimd.tensor_tensor(xs[:, g.half, :], xp[:, g.half, :], x2[:, g.half, :], ALU.add).then_inc(s["xs_made"], 1)
                    pool.wait_ge(s["rl_kept"], g.n * HT + 2 * HT)
                    nc.gpsimd.tensor_tensor(f2[:, g.half, 2:, :], rl[:, 2:, :], rl[:, 2:, :], ALU.mult).then_inc(s["f2_high"], 1)

                pool.sem_inc(s["f2_high"], 1)
                nc.gpsimd.memset(out[:], 0.0).then_inc(s["primed"], 1)
                with pool.Fori(0, TURNS) as it:
                    for k in range(2):
                        feed(Group(it, k))
                with pool.Fori(0, TURNS) as it:
                    for k in range(2):
                        pool.wait_ge(s["xi_rounded"], it * 2 + k + 1)
                        nc.gpsimd.tensor_tensor(xi[:, k, :], xi[:, k, :], shift[:].to_broadcast([128, GT]), ALU.add).then_inc(s["xi_made"], 1)
                with pool.Fori(0, TURNS) as it:
                    for k in range(2):
                        pool.wait_ge(s["t_made"], it * 2 + k + 1)
                        nc.gpsimd.tensor_tensor(f2[:, k, 0:2, :], f2[:, k, 0:2, :], shift[:].unsqueeze(2).to_broadcast([128, 2, GT]),
                                                ALU.add).then_inc(s["t_low"], 1)

            @block.vector
            def _(dve):
                ch = Chain(dve, s["chain"])

                def quaternions():
                    ch.link(nc.vector.tensor_tensor(qsq[:, 0:B], w["qleft_all"][:], w["qleft_all"][:], ALU.mult))
                    ch.link(nc.vector.tensor_tensor(qsq[:, B:], w["qright"][:], w["qright"][:], ALU.mult))
                    nc.vector.tensor_reduce(qn[:, 0:1], qsq[:, B:], AX.X, ALU.add)
                    ch.link(nc.vector.tensor_reduce(qn[:, 1:2], qsq[:, 0:B], AX.X, ALU.add))
                    nc.vector.tensor_scalar(qn[:], qn[:], TINY, None, ALU.add).then_inc(s["q_made"], 1)
                    nc.vector.tensor_tensor(qc[:, 0, :], w["qright"][:], w["right_sign"][:], ALU.mult)
                    ch.link(nc.vector.tensor_tensor(qc[:, 1, :], w["qleft"][:], w["left_sign"][:], ALU.mult))
                    ch.link(nc.vector.tensor_scalar(qc[:, 0, :], qc[:, 0, :], w["sgate"][:], None, ALU.mult))
                    dve.wait_ge(s["q_root"], 1)
                    ch.link(nc.vector.reciprocal(qn[:], qn[:]))
                    ch.link(nc.vector.tensor_tensor(qc[:], qc[:], qn[:].unsqueeze(2).to_broadcast([128, 2, 4]), ALU.mult))
                    for i in range(2):
                        last = nc.vector.tensor_tensor(side[:, i, :, :], w["same"][:].rearrange("p (c d) -> p c d", d=Q),
                                                       qc[:, i, :].unsqueeze(2).to_broadcast([128, 4, Q]), ALU.mult)
                    last.then_inc(s["sides_made"], 1)
                    dve.wait_ge(s["rot_made"], 1)
                    nc.vector.tensor_copy(rotT[:], s_ps[:, 0:D]).then_inc(s["rot_kept"], 1)

                def quantised_weights():
                    for i, name in enumerate(("WinT", "Wout2")):
                        wide = wsc[:, i, :].unsqueeze(2).to_broadcast([128, HT, D])
                        ch.link(nc.vector.tensor_reduce(wsc[:, i, :], w[name][:], AX.X, ALU.max, apply_absolute_value=True))
                        ch.link(nc.vector.tensor_scalar(wsc[:, i, :], wsc[:, i, :], TINY, None, ALU.max))
                        ch.link(nc.vector.reciprocal(wsc[:, i, :], wsc[:, i, :]))
                        ch.link(nc.vector.tensor_scalar(wsc[:, i, :], wsc[:, i, :], W8, None, ALU.mult))
                        ch.link(nc.vector.tensor_tensor(wq[:, i, :, :], w[name][:], wide, ALU.mult))
                        ch.link(nc.vector.tensor_scalar(wq[:, i, :, :], wq[:, i, :, :], ROUND, None, ALU.add))
                        last = nc.vector.tensor_scalar(wq[:, i, :, :], wq[:, i, :, :], ROUND, None, ALU.subtract)
                        if i == 0:
                            last.then_inc(s["win_made"], 1)
                        else:
                            ch.link(last)
                            ch.link(nc.vector.reciprocal(gsc[:], wsc[:, i, :]))
                            ch.link(nc.vector.tensor_tensor(wq[:, i, :, :], wq[:, i, :, :], gsc[:].unsqueeze(2).to_broadcast([128, HT, D]), ALU.mult))
                    dve.wait_ge(s["win_turned"], 1)
                    nc.vector.tensor_copy(win[:].rearrange("p j h -> p (j h)"), ms_ps[:]).then_inc(s["win_kept"], 1)

                def feed(g):
                    dve.wait_ge(s["rl_kept"], g.n * HT + HT + 2)
                    nc.vector.tensor_tensor(f2[:, g.half, 0:2, :], rl[:, 0:2, :], rl[:, 0:2, :], ALU.mult).then_inc(s["f2_low"], 1)
                    dve.wait_ge(s["ms_made"], g.n + 1)
                    nc.vector.tensor_scalar(r2[:, g.half, :], ms_ps[:], EPS, None, ALU.add).then_inc(s["r2_kept"], 1)
                    dve.wait_ge(s["r2_kept"], g.n + 2)
                    nc.vector.reciprocal(r2[:, g.half, :], r2[:, g.half, :])

                def rotate(g):
                    dve.wait_ge(s["y_made"], g.n + 1)
                    nc.vector.tensor_tensor(x3[:, g.half, :], y_ps[:], r2[:, g.half, :], ALU.mult).then_inc(s["y_kept"], 1)
                    dve.wait_ge(s["y_kept"], g.n + 2)
                    dve.wait_ge(s["xs_made"], g.n + 1)
                    nc.vector.tensor_tensor(x3[:, g.half, :], x3[:, g.half, :], xs[:, g.half, :], ALU.add).then_inc(s["x3_kept"], 1)
                    dve.wait_ge(s["xr_made"], g.n + 1)
                    nc.vector.memset(carry[:, g.half:g.half + 1], 0.0)
                    nc.vector.tensor_reduce(am[:, g.of(1)], r_ps[:], AX.X, ALU.max, apply_absolute_value=True)
                    nc.vector.tensor_copy(xr[:, g.of(GT)], r_ps[:]).then_inc(s["xr_kept"], 1)

                def scale(k):
                    if k == 0:
                        dve.wait_ge(s["xr_kept"], GROUPS + 1)
                    else:
                        dve.wait_ge(s["am_made"], GROUPS)
                    ch.link(nc.vector.tensor_reduce(peak[:], am[:], AX.X, ALU.max))
                    nc.vector.tensor_scalar(peak[:], peak[:], TINY, None, ALU.max).then_inc(s["peak_made"], 1)
                    dve.wait_ge(s["peak_turned"], k + 1)
                    nc.vector.tensor_reduce(one[:], s_ps[0:1, 0:128], AX.X, ALU.max).then_inc(s["one_made"], 1)
                    dve.wait_ge(s["one_spread"], k + 1)
                    ch.link(nc.vector.reciprocal(sc[:, k:k + 1], s_ps[:, 128:129]))
                    ch.link(nc.vector.tensor_scalar(sc[:, k:k + 1], sc[:, k:k + 1], A16, None, ALU.mult))

                def round_xr(g):
                    nc.vector.tensor_scalar(xi[:, g.half, :], xr[:, g.of(GT)], sc[:, 0:1], ROUND, ALU.mult, ALU.add).then_inc(s["xi_rounded"], 1)

                def hidden_peak(g):
                    dve.wait_ge(s["h_kept"], g.n + 1)
                    nc.vector.memset(carry[:, g.half:g.half + 1], 0.0)
                    nc.vector.tensor_reduce(am[:, g.of(1)], hid[:, g.of(HT * GT)], AX.X, ALU.max, apply_absolute_value=True).then_inc(s["am_made"], 1)

                def round_hidden(g):
                    nc.vector.tensor_scalar(f2[:, g.half, :, :].rearrange("p j t -> p (j t)"), hid[:, g.of(HT * GT)], sc[:, 1:2], ROUND,
                                            ALU.mult, ALU.add).then_inc(s["t_made"], 1)

                def output(g):
                    dve.wait_ge(out_stored[g.half], g.stores)
                    dve.wait_ge(s["o_made"], g.n + 1)
                    nc.vector.memset(carry[:, g.half:g.half + 1], 0.0)
                    nc.vector.scalar_tensor_tensor(out[:, g.half, :], o_ps[g.half][:], isc[:], x3b[:, g.of(GT)], ALU.mult, ALU.add).then_inc(s["o_kept"], 1)

                nc.vector.memset(shift[:], -ROUND)
                quaternions()
                quantised_weights()
                for n in ("f2_low", "r2_kept", "y_kept", "xr_kept", "x3_kept", "x3_kept"):
                    dve.sem_inc(s[n], 1)
                groups(dve, feed, rotate)
                scale(0)
                ch.link(nc.vector.tensor_scalar(gsc[:], wsc[:, 0, :], sc[:, 0:1], None, ALU.mult))
                nc.vector.reciprocal(gsc[:], gsc[:]).then_inc(s["scaled"], 1)
                groups(dve, round_xr, hidden_peak)
                scale(1)
                ch.link(nc.vector.reciprocal(isc[:], sc[:, 1:2]))
                dve.wait_ge(s["x3b_kept"], GROUPS)
                groups(dve, round_hidden, output)


SHARED = {"ident": (128, 128), "ones": (128, 128), "mean": (128, 128)}
HEADS = {"headmask": (128, 16), "quartermask": (128, 4, 128), "condT": (32, 32)}
MIXING = {"raw": (32, 64), "OBT": (128, 64), "WqkvT": (128, 384), "wg1": (128, 8), "rms_w": (128, 1), "wgb": (1, 8),
          "ggb": (1, 8), "ggW": (32, 8), "below": (64, 64), "ibT": (128, 32), "by8": (128, 128), "WoT": (128, 128),
          "gnw": (128, 1), "gnb": (128, 1), "decay": (128, 16, 128), "condTp": (32, 36), "rankTp": (64, 36)}
EXPERTS = {"W1": (128, 8, 256), "W2": (128, 8, 2, 256), "W3": (128, 8, 2, 128), "b1": (128, 8, 2), "b2": (128, 8, 2),
           "b3": (8, 128), "wg2": (128, 8), "F1": (128, 8, 512), "F2": (128, 8, 4, 128), "fb1": (128, 8, 4), "fb2": (8, 128)}
FIELDS = {"Wc1cT": (32, 128), "Wc1xT": (128, 128), "We1T": (32, 128), "We2T": (128, 128), "be2": (1, 128), "be1": (128, 1),
          "bc1": (128, 1), "lng": (32, 128), "lnb": (32, 128), "peT": (128, 128), "Alog": (128, 8), "WqT1": (128, 128),
          "WkT1": (128, 128), "WvT1": (128, 128), "bq": (128, 1), "bk": (128, 1), "bvb": (128, 128), "Wc2T": (128, 16),
          "bc2b": (128, 16), "WoutT": (128, 128), "bout": (128, 1), "eps6": (128, 1), "Wba": (128, 16), "dtb": (128, 8)}
DELTA = {"dWq": (128, 1024), "dWk": (128, 1024), "dWv": (128, 1024), "dWg": (128, 1024), "dWo": (128, 8, 128),
         "onw": (128, 128), "offblock": (128, 128), "headrow": (128, 2, 32), "headpick": (128, 8)}
LAST = {"Wfc": (128, 512), "Wproj": (128, 4, 128), "qleft_all": (128, 32), "qright": (128, 4), "qleft": (128, 4),
        "right_sign": (128, 4), "left_sign": (128, 4), "sgate": (128, 1), "same": (128, 128), "WinT": (128, 4, 128),
        "Wout2": (128, 4, 128), "bin": (128, 4), "bout2": (128, 1)}
KEPT = {"wg1": (128, 8), "obw": (64, 384), "gball": (128, GB + B, 8), "mtr": (32, 64), "c1b": (128, 2 * GB + B), "expA": (128, 8)}
INPUTS = {"xT": (GROUPS + 2, 128, GT), **SHARED, **HEADS, **MIXING, **EXPERTS, **FIELDS, **DELTA, **LAST}


def program(nc, I, outT):
    dram = {"xT": I["xT"], "outT": outT}
    for name, shape in (("x1T", (GROUPS + 3, 128, GT)), ("x2T", (GROUPS + 3, 128, GT)), ("mT", (GROUPS + 2, 128, GT)),
                        ("cw1", (GROUPS + 2, NE, GT)), ("cw2", (GROUPS + 2, NE, GT)), ("fa", (2 * GB + B, T)),
                        ("aT", (GROUPS + 2, 128, GT)), ("hT", (GROUPS + 2, 128, GT)), ("beta", (GROUPS + 2, T, 32)),
                        ("alpha", (GROUPS + 2, 32, T)), ("lanes", (2, 4, 32, 32, 32)), ("inverses", (2, 4, 32, 32, 32)),
                        ("xpT", (GROUPS + 2, 128, GT))):
        dram[name] = nc.dram_tensor(name, shape, F32, kind="Internal").ap()
    w, c = {"raw_dram": I["raw"]}, {}

    def place(ctx, names):
        for name, shape in names.items():
            w[name] = ctx.enter_context(nc.sbuf_tensor(f"w_{name}", shape, F32))

    sets = {"mixing": {**MIXING, **SHARED, **HEADS}, "experts": EXPERTS, "fields": FIELDS, "delta": DELTA, "last": LAST}
    loaded = {k: nc.alloc_semaphore(f"{k}_loaded") for k in sets}

    def load(*names):
        with nc.Block() as block:
            @block.sync
            def _(sp):
                for k in names:
                    for name in sets[k]:
                        sp.dma_start(w[name][:], I[name]).then_inc(loaded[k], 16)

    def arrived(k):
        with nc.Block() as block:
            @block.sync
            def _(sp):
                sp.wait_ge(loaded[k], 16 * len(sets[k]))

    with ExitStack() as layer1:
        place(layer1, SHARED)
        place(layer1, DELTA)
        with ExitStack() as field:
            for name, shape in KEPT.items():
                c[name] = field.enter_context(nc.sbuf_tensor(f"c_{name}", shape, F32))
            place(field, HEADS)
            place(field, FIELDS)
            with ExitStack() as layer0:
                place(layer0, EXPERTS)
                with ExitStack() as mixing:
                    place(mixing, MIXING)
                    load("mixing", "experts", "fields", "delta")
                    arrived("mixing")
                    mixing_basis(nc, w, c)
                    retention(nc, w, c, dram)
                arrived("experts")
                moe_first(nc, w, dram)
                moe_second(nc, w, dram)
            arrived("fields")
            field_basis(nc, w, c, dram)
            field_attention(nc, w, c, dram)
        arrived("delta")
        delta_rule(nc, w, dram)
        place(layer1, LAST)
        load("last")
        arrived("last")
        last_layer(nc, w, dram)


def laid_out(i):
    f = np.float32
    turned = lambda z: np.ascontiguousarray(z.T)
    column = lambda z: z[:, None]
    tiles = lambda z, n: z.reshape(n, 128, -1).transpose(1, 0, 2)
    rows = lambda z, n=128: np.broadcast_to(z[None], (n, z.shape[0]))
    behind = lambda z: np.concatenate([z, np.zeros((z.shape[0], GB), f)], 1)
    eye = np.eye(128, dtype=f)
    head, pos, block = np.arange(128) // 8, np.arange(T), np.arange(T) // 32
    a = {}
    xT = i["x"].reshape(GROUPS, GT, D).transpose(0, 2, 1)
    a["xT"] = np.concatenate([xT, np.zeros((2, D, GT), f)])
    a["ident"], a["ones"], a["mean"] = eye, np.ones((128, 128), f), np.full((128, 128), 1 / D, f)
    a["headmask"] = (head[:, None] == np.arange(16)[None]).astype(f)
    a["quartermask"] = np.broadcast_to((head[None] % 4 == np.arange(4)[:, None]).astype(f), (128, 4, 128))
    a["condT"] = turned(i["cond_256"])
    a["raw"], a["OBT"], a["ibT"] = i["L0_cond_mode_to_rank"], turned(i["L0_cond_output_basis"]), turned(i["L0_cond_input_basis"])
    a["WqkvT"] = np.concatenate([i["L0_attn_W_" + k].T for k in "qkv"], 1)
    a["wg1"], a["rms_w"], a["ggW"] = i["L0_cond2_wg_W"], column(i["L0_cond2_rms_w"]), i["L0_cond2_gg_W"]
    a["wgb"], a["ggb"] = i["L0_cond2_wg_b"][None], i["L0_cond2_gg_b"][None]
    a["below"] = np.tril(np.ones((64, 64), f))
    a["by8"] = ((head[:, None] == head[None]) / 8).astype(f)
    a["WoT"], a["gnw"], a["gnb"] = turned(i["L0_attn_W_o"]), column(i["L0_attn_gn_weight"]), column(i["L0_attn_gn_bias"])
    gamma = (1 - 2.0 ** (-5.0 - np.arange(16)))[None, :, None]
    ahead = (pos[None] - pos[:, None])[:, None, :]
    a["decay"] = np.where(ahead >= 0, gamma ** np.maximum(ahead, 0) / np.sqrt(8.0), 0.0).astype(f)
    a["condTp"], a["rankTp"] = behind(i["cond_256"].T), behind(i["cond_64"].T)
    a["W1"], a["b3"] = i["L0_cond2_W1"].transpose(1, 0, 2), i["L0_cond2_b3"]
    a["W2"] = i["L0_cond2_W2"].reshape(NE, 2, 128, 256).transpose(2, 0, 1, 3)
    a["W3"] = i["L0_cond2_W3"].reshape(NE, 2, 128, D).transpose(2, 0, 1, 3)
    a["b1"], a["b2"] = (i["L0_cond2_" + k].reshape(NE, 2, 128).transpose(2, 0, 1) for k in ("b1", "b2"))
    a["wg2"], a["fb2"] = turned(i["L0_ffn_w_gate"]), i["L0_ffn_b2"]
    a["F1"] = i["L0_ffn_W1"].transpose(1, 0, 2)
    a["F2"] = i["L0_ffn_W2"].reshape(NE, 4, 128, D).transpose(2, 0, 1, 3)
    a["fb1"] = i["L0_ffn_b1"].reshape(NE, 4, 128).transpose(2, 0, 1)
    Wc1, Wqkv, bqkv = i["L1_cond_Wc1"], i["L1_cond_Wqkv"], i["L1_cond_bqkv"]
    a["Wc1xT"], a["Wc1cT"] = turned(Wc1[:, :D]), turned(Wc1[:, D:])
    a["We1T"], a["We2T"], a["Wc2T"], a["WoutT"] = (turned(i["L1_cond_" + k]) for k in ("We1", "We2", "Wc2", "Wout"))
    a["be2"], a["be1"], a["bc1"] = i["L1_cond_be2"][None], column(i["L1_cond_be1"]), column(i["L1_cond_bc1"])
    a["lng"], a["lnb"] = rows(i["L1_cond_ln_g"], B), rows(i["L1_cond_ln_b"], B)
    inv = f(10000.0) ** np.repeat(np.arange(0, D, 2, dtype=f) / f(D), 2)
    a["peT"] = turned(np.sin((pos.astype(f)[:, None] / inv[None]).astype(f)).astype(f))
    a["WqT1"], a["WkT1"], a["WvT1"] = (turned(Wqkv[k * D:(k + 1) * D]) for k in range(3))
    a["bq"], a["bk"], a["bvb"] = column(bqkv[:D]), column(bqkv[D:2 * D]), rows(bqkv[2 * D:])
    a["bc2b"], a["bout"] = rows(i["L1_cond_bc2"]), column(i["L1_cond_bout"])
    a["eps6"], a["Alog"], a["dtb"] = np.full((128, 1), 1e-6, f), rows(i["L1_attn_A_log"]), rows(i["L1_attn_dt_bias"])
    a["Wba"] = np.concatenate([i["L1_attn_Wb"], i["L1_attn_Wa"]], 1)
    for k in "qkvg":
        a["dW" + k] = i["L1_attn_W" + k]
    a["dWo"], a["onw"] = tiles(i["L1_attn_Wo"], 8), rows(i["L1_attn_o_norm_w"])
    a["offblock"] = (block[None] > block[:, None]).astype(f)
    a["headrow"] = np.broadcast_to(np.eye(32, dtype=f)[:2][None], (128, 2, 32))
    quarter, place, heads = np.arange(128)[:, None] // 32, np.arange(128)[:, None] % 32, np.arange(8)[None]
    a["headpick"] = ((quarter == heads % 4) & (place == heads // 4)).astype(f)
    a["Wfc"], a["Wproj"] = i["L1_attn_W_fc"], tiles(i["L1_attn_W_proj"], 4)
    part = np.arange(4)[:, None] ^ np.arange(4)[None]
    spread = lambda q: q[part].transpose(0, 2, 1).reshape(128, 4)
    right = np.array([[1, -1, -1, -1], [1, 1, 1, -1], [1, -1, 1, 1], [1, 1, -1, 1]], f) * np.where(part > 0, -1, 1)
    left = np.array([[1, 1, 1, 1], [-1, 1, 1, -1], [-1, -1, 1, 1], [-1, 1, -1, 1]], f)
    a["right_sign"], a["left_sign"] = np.repeat(right, 32, 0).astype(f), np.repeat(left, 32, 0)
    a["qright"], a["qleft"] = spread(i["L1_cond2_q_right"]), spread(i["cond_256"][:4])
    a["qleft_all"] = np.tile(i["cond_256"].T, (4, 1))
    a["sgate"] = np.tile(i["L1_cond2_spectral_gate"].reshape(32), 4)[:, None]
    a["same"] = np.tile(np.eye(32, dtype=f), (4, 4))
    a["WinT"], a["Wout2"] = tiles(i["L1_ffn_W_in"].T, 4), tiles(i["L1_ffn_W_out"], 4)
    a["bin"], a["bout2"] = turned(i["L1_ffn_b_in"].reshape(4, 128)), column(i["L1_ffn_b_out"])
    return a


def kernel(**inputs):
    import concourse.bacc as bacc
    from concourse.bass_utils import run_bass_kernel_spmd

    a = laid_out({k: np.asarray(v) for k, v in inputs.items()})
    arrays = {f"in_{k}_dram": np.ascontiguousarray(a[k]) for k in INPUTS}
    nc = bacc.Bacc("TRN2", target_bir_lowering=False, num_devices=1)
    I = {k: nc.dram_tensor(f"in_{k}_dram", shape, F32, kind="ExternalInput").ap() for k, shape in INPUTS.items()}
    outT = nc.dram_tensor("out_0_dram", (GROUPS, D, GT), F32, kind="ExternalOutput").ap()
    program(nc, I, outT)
    r = run_bass_kernel_spmd(nc, [arrays], core_ids=[0])
    return np.ascontiguousarray(r.results[0]["out_0_dram"].transpose(0, 2, 1)).reshape(B, T, D)
```

```python
from contextlib import ExitStack

import concourse.bass as bass
import numpy as np
from concourse import mybir

B = 32
T = 128
D = 128
GB = 4
GROUPS = B // GB
GT = GB * T
NE = 8
HALVES = 2
TURNS = GROUPS // HALVES
F32 = mybir.dt.float32
BF16 = mybir.dt.bfloat16
ACT = mybir.ActivationFunctionType
ALU = mybir.AluOpType
AX = mybir.AxisListType


class Chain:

    def __init__(self, eng, sem):
        self.eng, self.sem, self.base, self.n = eng, sem, 0, 0

    def turn(self, it, per_turn, before=0):
        self.base, self.n = it * per_turn + before, 0

    def link(self, ins):
        ins.then_inc(self.sem, 1)
        self.n += 1
        self.eng.wait_ge(self.sem, self.base + self.n)


class Memory:

    def __init__(self, nc, ctx, stage):
        self.nc, self.ctx, self.stage, self.sems = nc, ctx, stage, []
        ctx.callback(self.release)

    def release(self):
        self.nc.clear_and_free_semaphores(self.sems)
        self.nc.all_engine_barrier()

    def sb(self, name, shape, dt=F32):
        return self.ctx.enter_context(self.nc.sbuf_tensor(f"{self.stage}_{name}", shape, dt))

    def ps(self, name, shape, dt=F32):
        return self.ctx.enter_context(self.nc.psum_tensor(f"{self.stage}_{name}", shape, dt))

    def sem(self, name):
        self.sems.append(self.nc.alloc_semaphore(f"{self.stage}_{name}"))
        return self.sems[-1]


def over_experts(ap):
    return ap.unsqueeze(2).to_broadcast([128, ap.shape[1], NE])


def gate_shift(nc, ch, g):
    ch.link(nc.vector.tensor_reduce(g["mx"][:], g["lg"][:], AX.X, ALU.max))
    nc.vector.tensor_tensor(g["lg"][:], g["lg"][:], over_experts(g["mx"][:]),
                            ALU.subtract).then_inc(g["shifted"], 1)


def gate_pick(nc, ch, g):
    p = g["p"][:, :, 0:NE]
    ch.link(nc.vector.tensor_reduce(g["mx"][:], p, AX.X, ALU.add))
    ch.link(nc.vector.reciprocal(g["mx"][:], g["mx"][:]))
    ch.link(nc.vector.tensor_tensor(p, p, over_experts(g["mx"][:]), ALU.mult))
    nc.vector.memset(g["carry"][:], 0.0)
    for b in range(g["rows"]):
        last = nc.vector.max(g["t8"][:, b, :], g["p"][:, b, :])
    ch.link(last)
    ch.link(nc.vector.memset(g["t8"][:, :, 2:8], -1.0))
    nc.vector.memset(g["carry"][:], 0.0)
    for b in range(g["rows"]):
        last = nc.vector.match_replace(g["rest"][:, b, :], g["t8"][:, b, :], g["p"][:, b, :], 0.0)
    ch.link(last)
    by_group = lambda ap: ap.rearrange("p (g b) e -> p g b e", b=GB)
    nc.vector.tensor_tensor(g["cw"][:].rearrange("p g e b -> p g b e"), by_group(p), by_group(g["rest"][:, :, 0:NE]),
                            ALU.subtract).then_inc(g["picked"], 1)


GATE_LINKS = 7


def gate_memory(m, groups=1):
    rows = groups * GB
    g = {"rows": rows, "lg": m.sb("gate_logits", [128, rows, NE]), "p": m.sb("gate_weights", [128, rows, 2 * NE]),
         "mx": m.sb("gate_max", [128, rows]), "t8": m.sb("gate_top", [128, rows, 8]),
         "carry": m.sb("gate_carry", [128, 1]),
         "rest": m.sb("gate_rest", [128, rows, 2 * NE]), "cw": m.sb("gate_kept", [128, groups, NE, GB])}
    for s in ("logits", "shifted", "exp", "picked", "turned", "out", "stored"):
        g[s] = m.sem("gate_" + s)
    return g


def mixing_basis(nc, w, c, start_loads):
    K, R = 32, 64
    with ExitStack() as ctx:
        m = Memory(nc, ctx, "basis")
        a = m.sb("a", [R + K, R])
        cols = m.sb("cols", [R + K, R])
        diag = m.sb("diag", [R, 2, R])
        rp = m.sb("rp", [R + K, 1])
        fac = m.sb("fac", [R + K, 1])
        cross = m.sb("cross", [R + K, 1])
        row1 = m.sb("row1", [R + K, R])
        qs = m.sb("qs", [R + K, R])
        q0 = m.sb("q0", [K, R])
        prod = m.sb("prod", [K, R])
        sgn = m.sb("sgn", [K, R])
        gg = m.sb("gg", [K, B, NE])
        bias = m.sb("bias", [1, NE])
        brow = m.sb("brow", [1, B, NE])
        gram_ps = m.ps("gramp", [R, R])
        row_ps = m.ps("rowp", [R + K, 2, R])
        obw_ps = m.ps("obwp", [R, 3 * D])
        sum_ps = m.ps("sump", [K, R])
        gb_ps = m.ps("gbp", [128, B * NE])
        gram, folded, picked, spread, moved, products, sums, gate_rows, gate_bias, roots, chain, done = (
            m.sem(s) for s in ("gram", "folded", "picked", "spread", "moved", "products", "sums",
                               "gate_rows", "gate_bias", "roots", "chain", "done"))
        LINKS = 7

        with nc.Block() as block:
            @block.sync
            def _(sp):
                sp.dma_start(a[R:R + K, :], w["raw_dram"]).then_inc(moved, 16)
                start_loads(sp)
                sp.wait_ge(done, 1)
                sp.dma_start(q0[:], qs[R:R + K, :]).then_inc(moved, 16)

            @block.scalar
            def _(act):
                act.wait_ge(spread, R // 2 + 1)
                nc.scalar.activation(qs[:], row_ps[:, 0, :], ACT.Sqrt).then_inc(roots, 1)

            @block.tensor
            def _(pe):
                nc.tensor.matmul(gram_ps[:], w["raw"][:], w["raw"][:], start=True, stop=True).then_inc(gram, 1)
                nc.tensor.matmul(obw_ps[:], w["OBT"][:], w["WqkvT"][:], start=True, stop=True).then_inc(folded, 1)
                pe.wait_ge(gate_rows, 1)
                nc.tensor.matmul(gb_ps[:], w["ones"][0:K, :], gg[:].rearrange("p b e -> p (b e)"), start=True, stop=False)
                nc.tensor.matmul(gb_ps[:], w["ones"][0:1, :], brow[:].rearrange("p b e -> p (b e)"),
                                 start=False, stop=True).then_inc(gate_bias, 1)
                with pe.Fori(0, R // 2 + 1) as turn:
                    pe.wait_ge(picked, turn + 1)
                    nc.tensor.matmul(row_ps[:].rearrange("p c r -> p (c r)"), w["ones"][0:R, 0:R + K],
                                     diag[:].rearrange("p c r -> p (c r)"), start=True, stop=True).then_inc(spread, 1)
                pe.wait_ge(products, 1)
                nc.tensor.matmul(sum_ps[:], w["ones"][0:K, 0:K], prod[:], start=True, stop=True).then_inc(sums, 1)

            @block.vector
            def _(dve):
                ch = Chain(dve, chain)
                nc.vector.tensor_scalar(c["wg1"][:], w["wg1"][:], w["rms_w"][:], None, ALU.mult)
                ch.link(nc.vector.tensor_tensor(bias[:], w["wgb"][:], w["ggb"][:], ALU.add))
                nc.vector.tensor_copy(brow[:], bias[:].unsqueeze(1).to_broadcast([1, B, NE]))
                nc.vector.tensor_tensor(gg[:], w["condT"][:].unsqueeze(2).to_broadcast([K, B, NE]),
                                        w["ggW"][:].unsqueeze(1).to_broadcast([K, B, NE]), ALU.mult).then_inc(gate_rows, 1)
                dve.wait_ge(gram, 1)
                ch.link(nc.vector.scalar_tensor_tensor(a[0:R, :], w["ident"][0:R, 0:R], 1e-4, gram_ps[:], ALU.mult, ALU.add))
                dve.wait_ge(folded, 1)
                nc.vector.tensor_copy(c["obw"][:], obw_ps[:])
                nc.vector.memset(c["gball"][:, 0:GB, :], 0.0)
                dve.wait_ge(gate_bias, 1)
                nc.vector.tensor_copy(c["gball"][:, GB:, :].rearrange("p b e -> p (b e)"), gb_ps[:])
                dve.wait_ge(moved, 16)
                before = ch.n
                def eliminate(turn):
                    col = [bass.ds(turn * 2 + j, 1) for j in range(2)]
                    nc.vector.tensor_tensor(diag[:], w["ident"][0:R, 0:R].unsqueeze(1).to_broadcast([R, 2, R]),
                                            a[0:R, bass.ds(turn * 2, 2)].unsqueeze(2).to_broadcast([R, 2, R]), ALU.mult).then_inc(picked, 1)
                    ch.link(nc.vector.tensor_copy(cols[:, col[0]], a[:, col[0]]))
                    dve.wait_ge(spread, turn + 1)
                    ch.link(nc.vector.reciprocal(rp[:], row_ps[:, 0, col[0]]))
                    nc.vector.tensor_copy(row1[:], row_ps[:, 1, :])
                    nc.vector.scalar_tensor_tensor(fac[:], cols[:, col[0]], -1.0, rp[:], ALU.mult, ALU.mult)
                    ch.link(nc.vector.scalar_tensor_tensor(cross[:], row_ps[:, 0, col[1]], -1.0, rp[:], ALU.mult, ALU.mult))
                    nc.vector.scalar_tensor_tensor(row1[:], row_ps[:, 0, :], cross[:], row1[:], ALU.mult, ALU.add)
                    ch.link(nc.vector.scalar_tensor_tensor(a[:], row_ps[:, 0, :], fac[:], a[:], ALU.mult, ALU.add))
                    nc.vector.tensor_copy(cols[:, col[1]], a[:, col[1]])
                    ch.link(nc.vector.reciprocal(rp[:], row1[:, col[1]]))
                    ch.link(nc.vector.scalar_tensor_tensor(fac[:], cols[:, col[1]], -1.0, rp[:], ALU.mult, ALU.mult))
                    ch.link(nc.vector.scalar_tensor_tensor(a[:], row1[:], fac[:], a[:], ALU.mult, ALU.add))

                with dve.Fori(0, R // 4) as pair:
                    ch.turn(pair, 2 * LINKS, before)
                    for k in range(2):
                        eliminate(pair * 2 + k)
                ch.turn(0, 0, before + R // 2 * LINKS)
                nc.vector.tensor_tensor(diag[:, 0, :], w["ident"][0:R, 0:R], cols[0:R, :], ALU.mult).then_inc(picked, 1)
                dve.wait_ge(roots, 1)
                ch.link(nc.vector.reciprocal(qs[:], qs[:]))
                nc.vector.tensor_tensor(qs[:], qs[:], cols[:], ALU.mult).then_inc(done, 1)
                dve.wait_ge(moved, 32)
                nc.vector.tensor_tensor(prod[:], q0[:], w["raw"][:], ALU.mult).then_inc(products, 1)
                dve.wait_ge(sums, 1)
                ch.link(nc.vector.tensor_scalar(sgn[:], sum_ps[:], 0.0, 2.0, ALU.is_ge, ALU.mult))
                ch.link(nc.vector.tensor_scalar(sgn[:], sgn[:], -1.0, None, ALU.add))
                nc.vector.tensor_tensor(c["mtr"][:], sgn[:], q0[:], ALU.mult).then_inc(done, 1)


def retention(nc, w, c, dram):
    NH, HQ = 16, 4
    K, R = 32, 64
    EPS_GN, EPS_RMS = 1e-5, 1e-6
    with ExitStack() as ctx:
        m = Memory(nc, ctx, "ret")
        xT = m.sb("xT", [128, 2, GT])
        xres = m.sb("xres", [128, 2, GT])
        proj = m.sb("proj", [K, GT])
        hid = m.sb("hid", [R, GT])
        qT = m.sb("qT", [128, 2, GT])
        kT = m.sb("kT", [128, 2, GT])
        vm = m.sb("vm", [128, 2, GB, HQ, D])
        qm = m.sb("qm", [128, 2, NH, T])
        pT = m.sb("pT", [128, 2, NH, T])
        bn = m.sb("bn", [128, GB, 6])
        mv = m.sb("mv", [128, GB, 2])
        dev = m.sb("dev", [128, GB])
        spread = m.sb("spread", [128, GB])
        gmean = m.sb("gmean", [128, GB])
        scale = m.sb("scale", [128, GB])
        shift = m.sb("shift", [128, GB])
        yn = m.sb("yn", [128, GT])
        x1T = m.sb("x1T", [128, 2, GT])
        sq = m.sb("sq", [128, GT])
        rms = m.sb("rms", [128, B])
        g = gate_memory(m, GROUPS)
        seen = m.sb("seen", [128, GROUPS + 1, GB * NE + GB])
        cwT = m.sb("cwT", [NE * GB, GROUPS + 1, T])
        s_ps = [m.ps(f"sp{i}", [128, HQ, T]) for i in range(HQ)]
        y_ps = [m.ps(f"yp{i}", [128, GT]) for i in range(2)]
        xa = m.ps("xa", [128, GT])
        tb = m.ps("tb", [128, GT])
        x_in = [m.sem(f"x_in{i}") for i in range(2)]
        res_in = [m.sem(f"res_in{i}") for i in range(2)]
        x1_stored = [m.sem(f"x1_stored{i}") for i in range(2)]
        (primed, proj_made, proj_kept, hid_made, hid_kept, q_made, q_kept, k_made, k_kept, v_made, v_kept, qm_made,
         s_made, p_made, y_made, means, mean_made, spreads, var_made, affine, yn_kept, o_made, x1_kept, sq_kept,
         gn_var, gn_root, gate_seen, rms_var, rms_root, chain) = (m.sem(s) for s in (
             "primed", "proj_made", "proj_kept", "hid_made", "hid_kept", "q_made", "q_kept", "k_made", "k_kept",
             "v_made", "v_kept", "qm_made", "s_made", "p_made", "y_made", "means", "mean_made", "spreads",
             "var_made", "affine", "yn_kept", "o_made", "x1_kept", "sq_kept", "gn_var", "gn_root", "gate_seen", "rms_var", "rms_root",
             "chain"))
        FREE = 2 * HQ
        LINKS = 1 + 3 + 3

        def of_group(ap, u):
            return ap[:, bass.ds(u * GB, GB)].unsqueeze(2)

        with nc.Block() as block:
            @block.sync
            def _(sp):
                for half in range(2):
                    sp.dma_start(xT[:, half, :], dram["xT"][half, :, :]).then_inc(x_in[half], 16)
                sp.dma_start(xres[:, 0, :], dram["xT"][0, :, :]).then_inc(res_in[0], 16)
                sp.dma_start(xres[:, 1, :], dram["xT"][0, :, :]).then_inc(res_in[1], 16)
                sp.wait_ge(primed, 2)
                for half in range(2):
                    sp.dma_start(dram["x1T"][GROUPS + 1 + half, :, :], x1T[:, half, :]).then_inc(x1_stored[half], 16)
                with sp.Fori(0, TURNS) as it:
                    for half in range(2):
                        u = it * 2 + half
                        sp.wait_ge(proj_made, u + 1)
                        sp.dma_start(xT[:, half, :], dram["xT"][bass.ds(u + 2, 1), :, :].squeeze(0)).then_inc(x_in[half], 16)
                        sp.wait_ge(x1_kept, u + 1)
                        sp.dma_start(xres[:, 1 - half, :], dram["xT"][bass.ds(u + 1, 1), :, :].squeeze(0)).then_inc(res_in[1 - half], 16)
                        sp.dma_start(dram["x1T"][bass.ds(u, 1), :, :].squeeze(0), x1T[:, 1 - half, :]).then_inc(x1_stored[1 - half], 16)
                sp.wait_ge(x1_kept, GROUPS + 1)
                sp.dma_start(dram["x1T"][GROUPS, :, :], x1T[:, 1, :]).then_inc(x1_stored[1], 16)
                sp.wait_ge(g["out"], 1)
                sp.dma_start(dram["cw1"][1:GROUPS + 2, :, :].rearrange("g e (b t) -> (e b) g t", t=T),
                             cwT[:]).then_inc(g["stored"], 16)
                sp.wait_ge(g["stored"], 16)
                sp.wait_ge(x1_stored[0], 16 * (TURNS + 1))
                sp.wait_ge(x1_stored[1], 16 * (TURNS + 2))
                for half in range(2):
                    sp.wait_ge(x_in[half], 16 * (TURNS + 1))
                    sp.wait_ge(res_in[half], 16 * (TURNS + 1))

            @block.gpsimd
            def _(pool):
                with pool.Fori(0, TURNS) as it:
                    for half in range(2):
                        u = it * 2 + half
                        pool.wait_ge(q_kept, u + 1)
                        for b in range(GB):
                            pool.wait_ge(p_made, u * GB * HQ + b * HQ + HQ)
                            nc.gpsimd.tensor_tensor(
                                qm[:, b % 2, :, :], qT[:, half, b * T:(b + 1) * T].unsqueeze(1).to_broadcast([128, NH, T]),
                                w["headmask"][:].unsqueeze(2).to_broadcast([128, NH, T]), ALU.mult).then_inc(qm_made, 1)

            @block.tensor
            def _(pe):
                def project_1(v, h, load):
                    pe.wait_ge(x_in[h], load)
                    nc.tensor.matmul(xa[0:K, :], w["ibT"][:], xT[:, h, :], start=True, stop=True).then_inc(proj_made, 1)

                def project_2(v):
                    pe.wait_ge(proj_kept, v + 1)
                    nc.tensor.matmul(xa[0:R, :], c["mtr"][:], proj[:], start=True, stop=True).then_inc(hid_made, 1)

                def project_3(v, h):
                    pe.wait_ge(hid_kept, v + 1)
                    nc.tensor.matmul(xa[:], c["obw"][:, 0:D], hid[:], start=True, stop=True).then_inc(q_made, 1)
                    nc.tensor.matmul(y_ps[h][:], c["obw"][:, D:2 * D], hid[:], start=True, stop=True).then_inc(k_made, 1)
                    pe.wait_ge(q_kept, v + 1)
                    for b in range(GB):
                        last = nc.tensor.matmul(xa[:, b * T:(b + 1) * T], hid[:, b * T:(b + 1) * T], c["obw"][:, 2 * D:3 * D],
                                                start=True, stop=True)
                    last.then_inc(v_made, 1)

                def scores(u, half, b):
                    pe.wait_ge(k_kept, u + 1)
                    pe.wait_ge(qm_made, u * GB + b + 1)
                    for i in range(HQ):
                        pe.wait_ge(p_made, u * GB * HQ + b * HQ + i + 1 + FREE - HQ)
                        nc.tensor.matmul(s_ps[i][:].rearrange("p h t -> p (h t)"), kT[:, half, b * T:(b + 1) * T],
                                         qm[:, b % 2, i * HQ:(i + 1) * HQ, :].rearrange("p h t -> p (h t)"),
                                         start=True, stop=True).then_inc(s_made, 1)

                def values(u, half, b):
                    pe.wait_ge(v_kept, u + 1)
                    pe.wait_ge(p_made, u * GB * HQ + b * HQ + HQ + FREE)
                    for i in range(HQ):
                        for k in range(HQ):
                            last = nc.tensor.matmul(y_ps[half][i * 32:(i + 1) * 32, b * T:(b + 1) * T],
                                                    vm[:, half, b, k, i * 32:(i + 1) * 32], pT[:, b % 2, i * HQ + k, :],
                                                    start=(k == 0), stop=(k == HQ - 1))
                    if b == GB - 1:
                        last.then_inc(y_made, 1)

                def norm_mean(u):
                    pe.wait_ge(means, u + 1)
                    nc.tensor.matmul(tb[:, 0:GB], w["by8"][:], mv[:, :, 0], start=True, stop=True).then_inc(mean_made, 1)

                def norm_var(u):
                    pe.wait_ge(spreads, u + 1)
                    nc.tensor.matmul(tb[:, 8:8 + GB], w["by8"][:], spread[:], start=True, stop=True).then_inc(var_made, 1)

                def output(u):
                    pe.wait_ge(yn_kept, u + 1)
                    nc.tensor.matmul(tb[:], w["WoT"][:], yn[:], start=True, stop=True).then_inc(o_made, 1)

                def gate_logits(u, h):
                    pe.wait_ge(x1_kept, u + 1)
                    pe.wait_ge(sq_kept, u + 1)
                    for b in range(GB):
                        nc.tensor.matmul(tb[:, b * NE:(b + 1) * NE], x1T[:, h, b * T:(b + 1) * T], c["wg1"][:], start=True, stop=True)
                        last = nc.tensor.matmul(tb[:, GB * NE + b:GB * NE + b + 1], sq[:, b * T:(b + 1) * T], w["ones"][:, 0:1],
                                                start=True, stop=True)
                    last.then_inc(g["logits"], 1)

                def gate_turn():
                    pe.wait_ge(g["picked"], 1)
                    for n in range(GROUPS):
                        bank = tb if n < GROUPS // 2 else xa
                        at = n % (GROUPS // 2) * T
                        last = nc.tensor.transpose(bank[0:NE * GB, at:at + T], g["cw"][:, n, :, :].rearrange("p e b -> p (e b)"), w["ident"][:])
                    last.then_inc(g["turned"], 1)

                project_1(0, 0, 16)
                project_2(0)
                project_3(0, 0)
                with pe.Fori(0, TURNS) as it:
                    for half in range(2):
                        u = it * 2 + half
                        scores(u, half, 0)
                        norm_mean(u)
                        scores(u, half, 1)
                        norm_var(u)
                        values(u, half, 0)
                        pe.wait_ge(v_kept, u + 1)
                        project_1(u + 1, 1 - half, it * 16 + 16 + 16 * half)
                        scores(u, half, 2)
                        output(u)
                        values(u, half, 1)
                        project_2(u + 1)
                        scores(u, half, 3)
                        gate_logits(u, 1 - half)
                        values(u, half, 2)
                        project_3(u + 1, 1 - half)
                        values(u, half, 3)
                norm_mean(GROUPS)
                norm_var(GROUPS)
                output(GROUPS)
                gate_logits(GROUPS, 1)
                gate_turn()

            @block.scalar
            def _(act):
                def keep_qk(v, h):
                    act.wait_ge(q_made, v + 1)
                    nc.scalar.copy(qT[:, h, :], xa[:]).then_inc(q_kept, 1)
                    act.wait_ge(k_made, v + 1)
                    nc.scalar.copy(kT[:, h, :], y_ps[h][:]).then_inc(k_kept, 1)

                def norm_root(u):
                    act.wait_ge(gn_var, u + 1)
                    nc.scalar.activation(scale[:], scale[:], ACT.Sqrt).then_inc(gn_root, 1)

                def gate_root():
                    act.wait_ge(rms_var, 1)
                    nc.scalar.activation(rms[:], rms[:], ACT.Sqrt).then_inc(rms_root, 1)

                def norm(u, h):
                    act.wait_ge(affine, u + 1)
                    for b in range(GB):
                        last = nc.scalar.activation(yn[:, b * T:(b + 1) * T], y_ps[h][:, b * T:(b + 1) * T], ACT.Identity,
                                                    bias=shift[:, b:b + 1], scale=scale[:, b:b + 1])
                    last.then_inc(yn_kept, 1)

                def square(u, h):
                    act.wait_ge(x1_kept, u + 1)
                    nc.scalar.activation(sq[:], x1T[:, h, :], ACT.Square, scale=D ** -0.5).then_inc(sq_kept, 1)

                def gate_exp():
                    act.wait_ge(g["shifted"], 1)
                    nc.scalar.activation(g["p"][:, :, 0:NE], g["lg"][:], ACT.Exp).then_inc(g["exp"], 1)

                keep_qk(0, 0)
                with act.Fori(0, TURNS) as it:
                    for half in range(2):
                        u = it * 2 + half
                        norm_root(u)
                        norm(u, 1 - half)
                        square(u, 1 - half)
                        keep_qk(u + 1, 1 - half)
                norm_root(GROUPS)
                norm(GROUPS, 1)
                square(GROUPS, 1)
                gate_root()
                gate_exp()

            @block.vector
            def _(dve):
                ch = Chain(dve, chain)

                def keep_proj(v):
                    dve.wait_ge(proj_made, v + 1)
                    nc.vector.tensor_tensor(proj[:].rearrange("p (b t) -> p b t", t=T), xa[0:K, :].rearrange("p (b t) -> p b t", t=T),
                                            of_group(w["condTp"], v).to_broadcast([K, GB, T]), ALU.mult).then_inc(proj_kept, 1)

                def keep_hid(v):
                    dve.wait_ge(hid_made, v + 1)
                    nc.vector.tensor_tensor(hid[:].rearrange("p (b t) -> p b t", t=T), xa[0:R, :].rearrange("p (b t) -> p b t", t=T),
                                            of_group(w["rankTp"], v).to_broadcast([R, GB, T]), ALU.mult).then_inc(hid_kept, 1)

                def keep_v(v, h):
                    dve.wait_ge(v_made, v + 1)
                    nc.vector.tensor_tensor(vm[:, h, :, :, :], xa[:].rearrange("p (b f) -> p b f", f=D).unsqueeze(2).to_broadcast([128, GB, HQ, D]),
                                            w["quartermask"][:].unsqueeze(1).to_broadcast([128, GB, HQ, D]), ALU.mult).then_inc(v_kept, 1)

                def decay(u, b):
                    for i in range(HQ):
                        dve.wait_ge(s_made, u * GB * HQ + b * HQ + i + 1)
                        nc.vector.tensor_tensor(pT[:, b % 2, i * HQ:(i + 1) * HQ, :], s_ps[i][:],
                                                w["decay"][:, i * HQ:(i + 1) * HQ, :], ALU.mult).then_inc(p_made, 1)

                def norm_stats(u, h):
                    dve.wait_ge(y_made, u + 1)
                    for b in range(GB):
                        last = nc.vector.bn_stats(bn[:, b, :], y_ps[h][:, b * T:(b + 1) * T])
                    ch.link(last)
                    nc.vector.memset(g["carry"][:], 0.0)
                    for b in range(GB):
                        last = nc.vector.bn_aggr(mv[:, b, :], bn[:, b, :])
                    last.then_inc(means, 1)

                def norm_spread(u):
                    dve.wait_ge(mean_made, u + 1)
                    ch.link(nc.vector.tensor_copy(gmean[:], tb[:, 0:GB]))
                    ch.link(nc.vector.tensor_tensor(dev[:], mv[:, :, 0], gmean[:], ALU.subtract))
                    ch.link(nc.vector.tensor_tensor(dev[:], dev[:], dev[:], ALU.mult))
                    nc.vector.tensor_tensor(spread[:], dev[:], mv[:, :, 1], ALU.add).then_inc(spreads, 1)

                def norm_affine(u):
                    dve.wait_ge(var_made, u + 1)
                    nc.vector.tensor_scalar(scale[:], tb[:, 8:8 + GB], EPS_GN, None, ALU.add).then_inc(gn_var, 1)

                def norm_scale(u):
                    dve.wait_ge(gn_root, u + 1)
                    ch.link(nc.vector.reciprocal(scale[:], scale[:]))
                    ch.link(nc.vector.tensor_scalar(scale[:], scale[:], w["gnw"][:], None, ALU.mult))
                    ch.link(nc.vector.scalar_tensor_tensor(shift[:], gmean[:], -1.0, scale[:], ALU.mult, ALU.mult))
                    nc.vector.tensor_scalar(shift[:], shift[:], w["gnb"][:], None, ALU.add).then_inc(affine, 1)

                def residual(u, h, store, load):
                    dve.wait_ge(o_made, u + 1)
                    dve.wait_ge(res_in[h], load)
                    dve.wait_ge(x1_stored[h], store)
                    nc.vector.tensor_tensor(x1T[:, h, :], tb[:], xres[:, h, :], ALU.add).then_inc(x1_kept, 1)

                def gate_keep(u):
                    dve.wait_ge(g["logits"], u + 1)
                    nc.vector.tensor_copy(seen[:, bass.ds(u, 1), :].squeeze(1), tb[:, 0:GB * NE + GB]).then_inc(gate_seen, 1)

                def gate_before():
                    dve.wait_ge(gate_seen, GROUPS + 1)
                    nc.vector.tensor_scalar(rms[:].rearrange("p (g b) -> p g b", b=GB), seen[:, 1:, GB * NE:], EPS_RMS, None,
                                            ALU.add).then_inc(rms_var, 1)

                def gate_norm():
                    dve.wait_ge(rms_root, 1)
                    ch.link(nc.vector.reciprocal(rms[:], rms[:]))
                    ch.link(nc.vector.tensor_tensor(g["lg"][:].rearrange("p (g b) e -> p g b e", b=GB),
                                                    seen[:, 1:, 0:GB * NE].rearrange("p g (b e) -> p g b e", e=NE),
                                                    over_experts(rms[:]).rearrange("p (g b) e -> p g b e", b=GB), ALU.mult))
                    ch.link(nc.vector.tensor_tensor(g["lg"][:], g["lg"][:], c["gball"][:, GB:, :], ALU.add))
                    gate_shift(nc, ch, g)

                def gate_after():
                    dve.wait_ge(g["exp"], 1)
                    gate_pick(nc, ch, g)

                def gate_out():
                    dve.wait_ge(g["turned"], 1)
                    for k, bank in enumerate((tb, xa)):
                        gs = slice(k * GROUPS // 2, (k + 1) * GROUPS // 2)
                        last = nc.vector.tensor_copy(cwT[:, gs, :], bank[0:NE * GB, :].rearrange("p (g t) -> p g t", t=T))
                    last.then_inc(g["out"], 1)

                nc.vector.memset(x1T[:], 0.0)
                nc.vector.memset(cwT[:], 0.0).then_inc(primed, 1)
                nc.vector.memset(g["p"][:], -1.0).then_inc(primed, 1)
                dve.wait_ge(primed, 2)
                nc.vector.memset(y_ps[1][:], 0.0).then_inc(y_made, 1)
                dve.sem_inc(p_made, FREE)
                keep_proj(0)
                keep_hid(0)
                keep_v(0, 0)
                with dve.Fori(0, TURNS) as it:
                    ch.turn(it, 2 * LINKS)
                    for half in range(2):
                        u = it * 2 + half
                        norm_stats(u, 1 - half)
                        decay(u, 0)
                        norm_spread(u)
                        decay(u, 1)
                        norm_affine(u)
                        keep_proj(u + 1)
                        norm_scale(u)
                        decay(u, 2)
                        residual(u, 1 - half, it * 16 + 16, it * 16 + 16)
                        keep_hid(u + 1)
                        decay(u, 3)
                        gate_keep(u)
                        keep_v(u + 1, 1 - half)
                assert ch.n == 2 * LINKS, ch.n
                ch.turn(0, 0, GROUPS * LINKS)
                norm_stats(GROUPS, 1)
                norm_spread(GROUPS)
                norm_affine(GROUPS)
                norm_scale(GROUPS)
                residual(GROUPS, 1, TURNS * 16 + 16, TURNS * 16 + 16)
                gate_keep(GROUPS)
                gate_before()
                gate_norm()
                gate_after()
                gate_out()


def moe_first(nc, w, dram):
    HT = 2
    with ExitStack() as ctx:
        m = Memory(nc, ctx, "moe1")
        xT = m.sb("xT", [128, 2, GT])
        cwb = m.sb("cwb", [128, 2, NE, GT])
        cwe = m.sb("cwe", [NE, 2, GT])
        h1 = m.sb("h1", [128, 2, HT, GT])
        r2 = m.sb("r2", [128, 2, HT, GT])
        h2 = m.sb("h2", [128, 2, HT, GT])
        yT = m.sb("yT", [128, 2, GT])
        g = gate_memory(m)
        cwT = m.sb("cwT", [NE * GB, T])
        h1_ps = [m.ps(f"h1p{i}", [128, GT]) for i in range(HT)]
        h2_ps = [m.ps(f"h2p{i}", [128, GT]) for i in range(HT)]
        y_ps = [m.ps(f"yp{i}", [128, GT]) for i in range(2)]
        lg_ps = m.ps("lgp", [128, GB, NE])
        cw_ps = m.ps("cwp", [NE * GB, T])
        loaded = [m.sem(f"loaded{i}") for i in range(2)]
        y_stored = [m.sem(f"y_stored{i}") for i in range(2)]
        h1_made, h1_kept, h2_made, h2_kept, h2_weighed, y_made, y_kept, primed, chain = (
            m.sem(s) for s in ("h1_made", "h1_kept", "h2_made", "h2_kept", "h2_weighed",
                               "y_made", "y_kept", "primed", "chain"))
        LINKS = GATE_LINKS + 1

        with nc.Block() as block:
            @block.sync
            def _(sp):
                def load(u, half):
                    sp.dma_start(xT[:, half, :], dram["x1T"][bass.ds(u + 1, 1), :, :].squeeze(0)).then_inc(loaded[half], 16)
                    sp.dma_start(cwe[:, half, :], dram["cw1"][bass.ds(u + 1, 1), :, :].squeeze(0)).then_inc(loaded[half], 16)
                    sp.dma_start(cwb[:, half, :, :].rearrange("p e t -> p (e t)"),
                                 dram["cw1"][bass.ds(u + 1, 1), :, :].rearrange("u e t -> u (e t)").to_broadcast([128, NE * GT])
                                 ).then_inc(loaded[half], 16)

                sp.wait_ge(primed, 3)
                sp.dma_start(dram["mT"][GROUPS + 1, :, :], yT[:, 0, :]).then_inc(y_stored[0], 16)
                sp.dma_start(dram["cw2"][GROUPS + 1, :, :].rearrange("e (b t) -> (e b) t", t=T),
                             cwT[:]).then_inc(g["stored"], 16)
                load(0, 0)
                with sp.Fori(0, TURNS) as it:
                    for half in range(2):
                        u = it * 2 + half
                        sp.wait_ge(y_kept, u + 2)
                        load(u + 1, 1 - half)
                        sp.dma_start(dram["mT"][bass.ds(u, 1), :, :].squeeze(0), yT[:, 1 - half, :]).then_inc(y_stored[1 - half], 16)
                        sp.wait_ge(g["out"], u + 1)
                        sp.dma_start(dram["cw2"][bass.ds(u, 1), :, :].rearrange("u e (b t) -> (u e b) t", t=T),
                                     cwT[:]).then_inc(g["stored"], 16)
                sp.wait_ge(y_kept, GROUPS + 2)
                sp.dma_start(dram["mT"][GROUPS, :, :], yT[:, 1, :]).then_inc(y_stored[1], 16)
                sp.wait_ge(g["out"], GROUPS + 1)
                sp.dma_start(dram["cw2"][GROUPS, :, :].rearrange("e (b t) -> (e b) t", t=T),
                             cwT[:]).then_inc(g["stored"], 16)
                sp.wait_ge(g["stored"], 16 * (GROUPS + 2))
                for half in range(2):
                    sp.wait_ge(y_stored[half], 16 * (TURNS + 1))
                sp.wait_ge(loaded[0], 48 * (TURNS + 1))

            @block.tensor
            def _(pe):
                def gate_logits(before, u):
                    pe.wait_ge(y_kept, u + 2)
                    for b in range(GB):
                        last = nc.tensor.matmul(lg_ps[:, b, :], yT[:, before, b * T:(b + 1) * T], w["wg2"][:],
                                                start=True, stop=True)
                    last.then_inc(g["logits"], 1)

                def gate_turn(u):
                    pe.wait_ge(g["picked"], u + 1)
                    nc.tensor.transpose(cw_ps[:], g["cw"][:, 0, :, :].rearrange("p e b -> p (e b)"),
                                        w["ident"][:]).then_inc(g["turned"], 1)

                def first_layer(n, half, s):
                    pe.wait_ge(h1_kept, n * HT + HT)
                    for i in range(HT):
                        nc.tensor.matmul(h1_ps[i][:], w["W1"][:, s, i * 128:(i + 1) * 128], xT[:, half, :],
                                         start=True, stop=True).then_inc(h1_made, 1)

                def second_layer(n, e):
                    pe.wait_ge(h1_kept, n * HT + 2 * HT)
                    pe.wait_ge(h2_kept, n * HT + HT)
                    for i in range(HT):
                        for k in range(HT):
                            last = nc.tensor.matmul(h2_ps[i][:], w["W2"][:, e, k, i * 128:(i + 1) * 128],
                                                    h1[:, e % 2, k, :], start=(k == 0), stop=(k == HT - 1))
                        last.then_inc(h2_made, 1)

                def third_layer(n, u, half, e):
                    if e == 0:
                        pe.wait_ge(y_kept, u + 1)
                        nc.tensor.matmul(y_ps[half][:], w["b3"][:], cwe[:, half, :], start=True, stop=False)
                    pe.wait_ge(h2_weighed, n + 3)
                    for k in range(HT):
                        last = nc.tensor.matmul(y_ps[half][:], w["W3"][:, e, k, :], h2[:, e % 2, k, :],
                                                start=False, stop=(e == NE - 1 and k == HT - 1))
                    if e == NE - 1:
                        last.then_inc(y_made, 1)

                pe.wait_ge(primed, 1)
                pe.wait_ge(loaded[0], 48)
                first_layer(0, 0, 0)
                first_layer(1, 0, 1)
                second_layer(0, 0)
                with pe.Fori(0, TURNS) as it:
                    for half in range(2):
                        u = it * 2 + half
                        for e in range(NE):
                            n = u * NE + e
                            if e == NE - 2:
                                pe.wait_ge(loaded[1 - half], it * 48 + 48 + 48 * half)
                            first_layer(n + 2, half if e < NE - 2 else 1 - half, (e + 2) % NE)
                            second_layer(n + 1, (e + 1) % NE)
                            third_layer(n, u, half, e)
                            if e == 1:
                                gate_logits(1 - half, u)
                            if e == 5:
                                gate_turn(u)
                gate_logits(1, GROUPS)
                gate_turn(GROUPS)

            @block.scalar
            def _(act):
                def first_layer(n, e):
                    for i in range(HT):
                        act.wait_ge(h1_made, n * HT + i + 1)
                        nc.scalar.activation(h1[:, e % 2, i, :], h1_ps[i][:], ACT.Relu,
                                             bias=w["b1"][:, e, i:i + 1]).then_inc(h1_kept, 1)

                def second_layer(n, e):
                    act.wait_ge(h2_weighed, n + 1)
                    for i in range(HT):
                        act.wait_ge(h2_made, n * HT + i + 1)
                        nc.scalar.activation(r2[:, e % 2, i, :], h2_ps[i][:], ACT.Relu,
                                             bias=w["b2"][:, e, i:i + 1]).then_inc(h2_kept, 1)

                def gate_exp(u):
                    act.wait_ge(g["shifted"], u + 1)
                    nc.scalar.activation(g["p"][:, :, 0:NE], g["lg"][:], ACT.Exp).then_inc(g["exp"], 1)

                act.sem_inc(h1_kept, HT)
                act.sem_inc(h2_kept, HT)
                first_layer(0, 0)
                first_layer(1, 1)
                second_layer(0, 0)
                with act.Fori(0, TURNS) as it:
                    for half in range(2):
                        u = it * 2 + half
                        for e in range(NE):
                            first_layer(u * NE + e + 2, (e + 2) % NE)
                            second_layer(u * NE + e + 1, (e + 1) % NE)
                            if e == 3:
                                gate_exp(u)
                gate_exp(GROUPS)

            @block.vector
            def _(dve):
                ch = Chain(dve, chain)

                def gate_before(u):
                    dve.wait_ge(g["logits"], u + 1)
                    ch.link(nc.vector.tensor_copy(g["lg"][:], lg_ps[:]))
                    gate_shift(nc, ch, g)

                def gate_after(u):
                    dve.wait_ge(g["exp"], u + 1)
                    gate_pick(nc, ch, g)

                def gate_out(u):
                    dve.wait_ge(g["turned"], u + 1)
                    dve.wait_ge(g["stored"], u * 16 + 16)
                    nc.vector.tensor_copy(cwT[:], cw_ps[:]).then_inc(g["out"], 1)

                nc.vector.memset(yT[:], 0.0).then_inc(primed, 1)
                nc.vector.memset(cwT[:], 0.0).then_inc(primed, 1)
                nc.vector.memset(g["p"][:], -1.0).then_inc(primed, 1)
                dve.wait_ge(primed, 3)
                dve.sem_inc(h2_weighed, 2)
                dve.sem_inc(y_kept, 2)
                with dve.Fori(0, TURNS) as it:
                    ch.turn(it, 2 * LINKS)
                    for half in range(2):
                        u = it * 2 + half
                        dve.wait_ge(loaded[half], it * 48 + 48)
                        for e in range(NE):
                            dve.wait_ge(h2_kept, u * NE * HT + HT * e + 2 * HT)
                            ins = nc.vector.tensor_tensor(
                                h2[:, e % 2, :, :], r2[:, e % 2, :, :],
                                cwb[:, half, e, :].unsqueeze(1).to_broadcast([128, HT, GT]), ALU.mult)
                            ins.then_inc(h2_weighed, 1)
                            if e == 3:
                                gate_before(u)
                            if e == 4:
                                gate_after(u)
                            if e == 6:
                                gate_out(u)
                        dve.wait_ge(y_made, u + 1)
                        dve.wait_ge(y_stored[half], it * 16 + 16)
                        nc.vector.tensor_copy(yT[:, half, :], y_ps[half][:]).then_inc(y_kept, 1)
                ch.turn(0, 0, GROUPS * LINKS)
                gate_before(GROUPS)
                gate_after(GROUPS)
                gate_out(GROUPS)


def moe_second(nc, w, dram):
    HT = 4
    with ExitStack() as ctx:
        m = Memory(nc, ctx, "moe2")
        mT = m.sb("mT", [128, 2, GT])
        xT = m.sb("xT", [128, 2, GT])
        cwb = m.sb("cwb", [128, 2, NE, GT])
        cwe = m.sb("cwe", [NE, 2, GT])
        act_h = m.sb("h", [128, 2, HT, GT])
        wgt_h = m.sb("hw", [128, 2, HT, GT])
        x2T = m.sb("x2T", [128, 2, GT])
        h_ps = [m.ps(f"hp{i}", [128, GT]) for i in range(HT)]
        y_ps = [m.ps(f"yp{i}", [128, GT]) for i in range(2)]
        loaded = [m.sem(f"loaded{i}") for i in range(2)]
        stored = [m.sem(f"stored{i}") for i in range(2)]
        h_made, h_kept, h_weighed, y_made, y_kept, primed, padded = (
            m.sem(s) for s in ("h_made", "h_kept", "h_weighed", "y_made", "y_kept", "primed", "padded"))

        with nc.Block() as block:
            @block.sync
            def _(sp):
                sp.wait_ge(primed, 1)
                sp.dma_start(dram["x2T"][GROUPS + 1, :, :], x2T[:, 0, :]).then_inc(stored[0], 16)
                sp.dma_start(dram["x2T"][GROUPS + 2, :, :], x2T[:, 0, :]).then_inc(padded, 16)
                with sp.Fori(0, TURNS) as it:
                    for half in range(2):
                        u = it * 2 + half
                        sp.wait_ge(y_kept, u + 1)
                        sp.dma_start(mT[:, half, :], dram["mT"][bass.ds(u + 1, 1), :, :].squeeze(0)).then_inc(loaded[half], 16)
                        sp.dma_start(xT[:, half, :], dram["x1T"][bass.ds(u + 1, 1), :, :].squeeze(0)).then_inc(loaded[half], 16)
                        sp.dma_start(cwe[:, half, :], dram["cw2"][bass.ds(u + 1, 1), :, :].squeeze(0)).then_inc(loaded[half], 16)
                        sp.dma_start(cwb[:, half, :, :].rearrange("p e t -> p (e t)"),
                                     dram["cw2"][bass.ds(u + 1, 1), :, :].rearrange("u e t -> u (e t)").to_broadcast([128, NE * GT])
                                     ).then_inc(loaded[half], 16)
                        sp.wait_ge(y_kept, u + 2)
                        sp.dma_start(dram["x2T"][bass.ds(u, 1), :, :].squeeze(0), x2T[:, 1 - half, :]).then_inc(stored[1 - half], 16)
                sp.wait_ge(y_kept, GROUPS + 2)
                sp.dma_start(dram["x2T"][GROUPS, :, :], x2T[:, 1, :]).then_inc(stored[1], 16)
                sp.wait_ge(padded, 16)
                for half in range(2):
                    sp.wait_ge(stored[half], 16 * (TURNS + 1))

            @block.tensor
            def _(pe):
                with pe.Fori(0, TURNS) as it:
                    for half in range(2):
                        u = it * 2 + half
                        pe.wait_ge(loaded[half], it * 64 + 64)
                        for s in range(NE + 1):
                            if s < NE:
                                for i in range(HT):
                                    pe.wait_ge(h_kept, u * NE * HT + HT * s + i + 1)
                                    nc.tensor.matmul(h_ps[i][:], w["F1"][:, s, i * 128:(i + 1) * 128], mT[:, half, :],
                                                     start=True, stop=True).then_inc(h_made, 1)
                            if s == 1:
                                pe.wait_ge(y_kept, u + 1)
                                nc.tensor.matmul(y_ps[half][:], w["fb2"][:], cwe[:, half, :], start=True, stop=False)
                            if s >= 1:
                                e = s - 1
                                for k in range(HT):
                                    pe.wait_ge(h_weighed, u * NE * HT + e * HT + k + 1 + 2 * HT)
                                    last = nc.tensor.matmul(y_ps[half][:], w["F2"][:, e, k, :], wgt_h[:, e % 2, k, :],
                                                            start=False, stop=(e == NE - 1 and k == HT - 1))
                                if e == NE - 1:
                                    last.then_inc(y_made, 1)

            @block.scalar
            def _(act):
                act.sem_inc(h_kept, HT)
                with act.Fori(0, TURNS) as it:
                    for half in range(2):
                        u = it * 2 + half
                        for e in range(NE):
                            for i in range(HT):
                                act.wait_ge(h_weighed, u * NE * HT + e * HT + i + 1)
                                act.wait_ge(h_made, u * NE * HT + e * HT + i + 1)
                                nc.scalar.activation(act_h[:, e % 2, i, :], h_ps[i][:], ACT.Gelu,
                                                     bias=w["fb1"][:, e, i:i + 1]).then_inc(h_kept, 1)

            @block.vector
            def _(dve):
                nc.vector.memset(x2T[:], 0.0).then_inc(primed, 1)
                dve.sem_inc(h_weighed, 2 * HT)
                dve.sem_inc(y_kept, 2)
                with dve.Fori(0, TURNS) as it:
                    for half in range(2):
                        u = it * 2 + half
                        dve.wait_ge(loaded[half], it * 64 + 64)
                        for e in range(NE):
                            for i in range(HT):
                                dve.wait_ge(h_kept, u * NE * HT + e * HT + i + 1 + HT)
                                nc.vector.tensor_tensor(wgt_h[:, e % 2, i, :], act_h[:, e % 2, i, :],
                                                        cwb[:, half, e, :], ALU.mult).then_inc(h_weighed, 1)
                        dve.wait_ge(y_made, u + 1)
                        dve.wait_ge(stored[half], it * 16 + 16)
                        nc.vector.tensor_tensor(x2T[:, half, :], y_ps[half][:], xT[:, half, :],
                                                ALU.add).then_inc(y_kept, 1)


FIELD = 0.3 * 0.7
HEAD_DIM = 8


def field_basis(nc, w, c, dram):
    CD = 32
    with ExitStack() as ctx:
        m = Memory(nc, ctx, "fbasis")
        r = m.sb("r", [128, B])
        fp = m.sb("fp", [B, D])
        bn = m.sb("bn", [B, 6])
        mv = m.sb("mv", [B, 2])
        rstd = m.sb("rstd", [B, 1])
        fpT = m.sb("fpT", [128, B])
        mx = m.sb("mx", [B, 1])
        e = m.sb("e", [B, T])
        z = m.sb("z", [B, 1])
        none = m.sb("none", [GB, T])
        c1_ps = m.ps("c1p", [128, B])
        r_ps = m.ps("rp", [128, B])
        fp_ps = m.ps("fpp", [B, D])
        fpT_ps = m.ps("fpTp", [128, B])
        fa_ps = m.ps("fap", [B, T])
        first, r_kept, fp_made, var, root, normed, turned, turn_kept, logits, peak, exps, fa, nothing, stored, chain = (
            m.sem(s) for s in ("first", "r_kept", "fp_made", "var", "root", "normed", "turned", "turn_kept",
                               "logits", "peak", "exps", "fa", "nothing", "stored", "chain"))
        with nc.Block() as block:
            @block.sync
            def _(sp):
                sp.wait_ge(nothing, 1)
                sp.dma_start(dram["fa"][0:GB, :], none[:]).then_inc(stored, 16)
                sp.dma_start(dram["fa"][GB + B:, :], none[:]).then_inc(stored, 16)
                sp.wait_ge(fa, 1)
                sp.dma_start(dram["fa"][GB:GB + B, :], e[:]).then_inc(stored, 16)
                sp.wait_ge(stored, 48)

            @block.tensor
            def _(pe):
                nc.tensor.matmul(c1_ps[:], w["Wc1cT"][:], w["condT"][:], start=True, stop=True)
                nc.tensor.matmul(r_ps[:], w["We1T"][:], w["condT"][:], start=True, stop=True).then_inc(first, 1)
                pe.wait_ge(r_kept, 1)
                nc.tensor.matmul(fp_ps[:], r[:], w["We2T"][:], start=True, stop=False)
                nc.tensor.matmul(fp_ps[:], w["ones"][0:1, 0:B], w["be2"][:], start=False, stop=True).then_inc(fp_made, 1)
                pe.wait_ge(normed, 1)
                nc.tensor.transpose(fpT_ps[:], fp[:], w["ident"][0:B, 0:B]).then_inc(turned, 1)
                pe.wait_ge(turn_kept, 1)
                nc.tensor.matmul(fa_ps[:], fpT[:], w["peT"][:], start=True, stop=True).then_inc(logits, 1)

            @block.scalar
            def _(act):
                nc.scalar.activation(c["expA"][:], w["Alog"][:], ACT.Exp)
                act.wait_ge(var, 1)
                nc.scalar.activation(rstd[:], rstd[:], ACT.Sqrt).then_inc(root, 1)
                act.wait_ge(peak, 1)
                nc.scalar.activation(e[:], fa_ps[:], ACT.Exp, bias=mx[:], accum_out=z[:]).then_inc(exps, 1)

            @block.vector
            def _(dve):
                ch = Chain(dve, chain)
                nc.vector.memset(none[:], 0.0).then_inc(nothing, 1)
                nc.vector.tensor_scalar(c["bqs"][:], w["bq"][:], HEAD_DIM ** -0.5, None, ALU.mult)
                nc.vector.memset(c["c1b"][:, 0:GB], 0.0)
                nc.vector.memset(c["c1b"][:, GB + B:], 0.0)
                dve.wait_ge(first, 1)
                nc.vector.tensor_scalar(c["c1b"][:, GB:GB + B], c1_ps[:], w["bc1"][:], None, ALU.add)
                nc.vector.tensor_scalar(r[:], r_ps[:], w["be1"][:], 0.0, ALU.add, ALU.max).then_inc(r_kept, 1)
                dve.wait_ge(fp_made, 1)
                ch.link(nc.vector.bn_stats(bn[:], fp_ps[:]))
                ch.link(nc.vector.bn_aggr(mv[:], bn[:]))
                nc.vector.tensor_scalar(rstd[:], mv[:, 1:2], 1e-5, None, ALU.add).then_inc(var, 1)
                dve.wait_ge(root, 1)
                ch.link(nc.vector.reciprocal(rstd[:], rstd[:]))
                ch.link(nc.vector.tensor_scalar(fp[:], fp_ps[:], mv[:, 0:1], rstd[:], ALU.subtract, ALU.mult))
                ch.link(nc.vector.tensor_tensor(fp[:], fp[:], w["lng"][:], ALU.mult))
                nc.vector.tensor_tensor(fp[:], fp[:], w["lnb"][:], ALU.add).then_inc(normed, 1)
                dve.wait_ge(turned, 1)
                nc.vector.tensor_copy(fpT[:], fpT_ps[:]).then_inc(turn_kept, 1)
                dve.wait_ge(logits, 1)
                ch.link(nc.vector.tensor_reduce(mx[:], fa_ps[:], AX.X, ALU.max))
                nc.vector.tensor_scalar(mx[:], mx[:], -1.0, None, ALU.mult).then_inc(peak, 1)
                dve.wait_ge(exps, 1)
                ch.link(nc.vector.reciprocal(z[:], z[:]))
                nc.vector.tensor_scalar(e[:], e[:], z[:], FIELD, ALU.mult, ALU.mult).then_inc(fa, 1)


def field_attention(nc, w, c, dram):
    NH, HQ, GH = 16, 4, 8
    SCALE = HEAD_DIM ** -0.5
    EPS = 1e-6
    with ExitStack() as ctx:
        m = Memory(nc, ctx, "field")
        xT = m.sb("xT", [128, 2, GT])
        fab = m.sb("fab", [128, 2, GT])
        qT = m.sb("qT", [128, 2, GT])
        kT = m.sb("kT", [128, 2, GT])
        km = m.sb("km", [128, 2, NH, T])
        v = m.sb("v", [128, 2, GB, D])
        vm = m.sb("vm", [128, 2, GB, HQ, D])
        th = m.sb("th", [128, GT])
        c1g = m.sb("c1g", [128, GB])
        zc = m.sb("zc", [128, GB, NH])
        coh = m.sb("coh", [128, 2, GB, NH])
        nm = m.sb("nm", [128, 2, NH])
        zs = m.sb("zs", [128, 2, NH])
        rz = m.sb("rz", [128, 2, NH])
        p = m.sb("p", [128, 2, NH, T])
        pT = m.sb("pT", [128, NH, T])
        yT = m.sb("yT", [128, GT])
        aT = m.sb("aT", [128, GT])
        sq = m.sb("sq", [128, GT])
        rt = m.sb("rt", [128, GT])
        hT = m.sb("hT", [128, GT])
        ba = m.sb("ba", [128, GROUPS + 1, GB, 2 * GH])
        ex = m.sb("ex", [128, GROUPS, GB, 2 * GH])
        pos = m.sb("pos", [128, GROUPS, GB, GH])
        lo = m.sb("lo", [128, GROUPS, GB, GH])
        beta = m.sb("beta", [128, GROUPS + 1, GB, GH])
        al = m.sb("al", [128, GROUPS, GB, GH])
        alT = m.sb("alT", [GB * GH, GROUPS + 1, T])
        s_ps = [m.ps(f"sp{i}", [128, HQ, T]) for i in range(HQ)]
        pt_ps = m.ps("ptp", [128, HQ, T])
        y_ps = m.ps("yp", [128, GT])
        xa = m.ps("xa", [128, GT])
        tb = m.ps("tb", [128, GT])
        x_in = [m.sem(f"x_in{i}") for i in range(2)]
        fa_in = [m.sem(f"fa_in{i}") for i in range(2)]
        names = ("primed q_made q_kept k_made k_kept v_made v_kept vm_made c1_kept t_made t_kept z_made z_kept z_exp coh_kept "
                 "km_made s_made peak exps rz_made p_made turned pt_kept y_made y_kept o_made a_kept sq_kept ms_made "
                 "ms_root rt_made h_kept ba_made ba_kept z_sized ba_exp one_kept ln_kept g_kept al_exp al_turned al_out "
                 "a_stored h_stored be_stored al_stored chain").split()
        s = {n: m.sem(n) for n in names}
        LINKS_TURN = GB * HQ + 2
        EXP0 = 2 * HQ

        with nc.Block() as block:
            @block.sync
            def _(sp):
                def store_before(u, slot):
                    sp.wait_ge(s["a_kept"], u + 1)
                    sp.dma_start(dram["aT"][slot, :, :].squeeze(0), aT[:]).then_inc(s["a_stored"], 16)
                    sp.wait_ge(s["h_kept"], u + 1)
                    sp.dma_start(dram["hT"][slot, :, :].squeeze(0), hT[:]).then_inc(s["h_stored"], 16)

                for half in range(2):
                    sp.dma_start(xT[:, half, :], dram["x2T"][1 + half, :, :]).then_inc(x_in[half], 16)
                sp.dma_start(fab[:, 0, :], dram["fa"][GB:2 * GB, :].rearrange("(o b) t -> o (b t)", o=1).to_broadcast([128, GT])).then_inc(fa_in[0], 16)
                sp.dma_start(fab[:, 1, :], dram["fa"][0:GB, :].rearrange("(o b) t -> o (b t)", o=1).to_broadcast([128, GT])).then_inc(fa_in[1], 16)
                sp.wait_ge(s["primed"], 1)
                sp.dma_start(dram["aT"][GROUPS + 1, :, :], aT[:]).then_inc(s["a_stored"], 16)
                sp.dma_start(dram["hT"][GROUPS + 1, :, :], hT[:]).then_inc(s["h_stored"], 16)
                with sp.Fori(0, TURNS) as it:
                    for half in range(2):
                        u = it * 2 + half
                        sp.wait_ge(s["t_made"], u + 1)
                        sp.dma_start(xT[:, half, :], dram["x2T"][bass.ds(u + 3, 1), :, :].squeeze(0)).then_inc(x_in[half], 16)
                        sp.wait_ge(s["y_made"], u + 1)
                        sp.dma_start(fab[:, 1 - half, :], dram["fa"][bass.ds((u + 2) * GB, GB), :].rearrange("(o b) t -> o (b t)", o=1)
                                     .to_broadcast([128, GT])).then_inc(fa_in[1 - half], 16)
                        store_before(u, bass.ds(u, 1))
                store_before(GROUPS, bass.ds(GROUPS, 1))
                sp.wait_ge(s["g_kept"], 1)
                sp.dma_start(dram["beta"][1:GROUPS + 2, :, :].rearrange("g p c -> p g c"),
                             beta[:].rearrange("p g b h -> p g (b h)")).then_inc(s["be_stored"], 16)
                sp.wait_ge(s["al_out"], 1)
                sp.dma_start(dram["alpha"][1:GROUPS + 2, :, :].rearrange("g p t -> p g t"), alT[:]).then_inc(s["al_stored"], 16)
                for n in ("a_stored", "h_stored"):
                    sp.wait_ge(s[n], 16 * (GROUPS + 2))
                for n in ("be_stored", "al_stored"):
                    sp.wait_ge(s[n], 16)
                for half in range(2):
                    sp.wait_ge(x_in[half], 16 * (TURNS + 1))
                    sp.wait_ge(fa_in[half], 16 * (TURNS + 1))

            @block.gpsimd
            def _(pool):
                def mask_k(n, kk, h, b, r):
                    pool.wait_ge(s["k_kept"], kk)
                    pool.wait_ge(s["exps"], n * HQ + HQ)
                    nc.gpsimd.tensor_tensor(km[:, r, :, :], kT[:, h, b * T:(b + 1) * T].unsqueeze(1).to_broadcast([128, NH, T]),
                                            w["headmask"][:].unsqueeze(2).to_broadcast([128, NH, T]), ALU.mult).then_inc(s["km_made"], 1)

                def weigh(n, r, i):
                    pool.wait_ge(s["rz_made"], n)
                    nc.gpsimd.tensor_tensor(p[:, r, i * HQ:(i + 1) * HQ, :], p[:, r, i * HQ:(i + 1) * HQ, :],
                                            rz[:, r, i * HQ:(i + 1) * HQ].unsqueeze(2).to_broadcast([128, HQ, T]),
                                            ALU.mult).then_inc(s["p_made"], 1)

                def norm(u):
                    pool.wait_ge(s["rt_made"], u * 2 + 2)
                    pool.wait_ge(s["h_stored"], u * 16 + 16)
                    nc.gpsimd.tensor_tensor(hT[:], aT[:], rt[:], ALU.mult).then_inc(s["h_kept"], 1)

                def mask_v(vv, h, part):
                    pool.wait_ge(s["v_kept"], vv)
                    rows = slice(part * GB // 2, (part + 1) * GB // 2)
                    nc.gpsimd.tensor_tensor(vm[:, h, rows, :, :], v[:, h, rows, :].unsqueeze(2).to_broadcast([128, GB // 2, HQ, D]),
                                            w["quartermask"][:].unsqueeze(1).to_broadcast([128, GB // 2, HQ, D]), ALU.mult).then_inc(s["vm_made"], 1)

                pool.sem_inc(s["p_made"], HQ - 1)
                mask_v(1, 0, 0)
                mask_v(1, 0, 1)
                mask_k(0, 1, 0, 0, 0)
                with pool.Fori(0, TURNS) as it:
                    for half in range(2):
                        u = it * 2 + half
                        for b in range(GB):
                            n = u * GB + b
                            weigh(n * HQ + 1, (b + 1) % 2, HQ - 1)
                            if b < GB - 1:
                                mask_k(n + 1, u + 1, half, b + 1, (b + 1) % 2)
                            else:
                                mask_k(n + 1, u + 2, 1 - half, 0, 0)
                            for i in range(HQ - 1):
                                weigh(n * HQ + i + 2, b % 2, i)
                                if b == 3 and i == 0:
                                    norm(u)
                            if b >= 2:
                                mask_v(u + 2, 1 - half, b - 2)
                weigh(B * HQ + 1, 1, HQ - 1)
                norm(GROUPS)

            @block.tensor
            def _(pe):
                def project_qkv(vv, h, load, part):
                    if part == "q":
                        pe.wait_ge(x_in[h], load)
                        pe.wait_ge(s["z_kept"], vv + 1)
                        nc.tensor.matmul(xa[:], w["WqT1"][:], xT[:, h, :], start=True, stop=True).then_inc(s["q_made"], 1)
                    if part == "k":
                        pe.wait_ge(s["q_kept"], vv + 1)
                        nc.tensor.matmul(xa[:], w["WkT1"][:], xT[:, h, :], start=True, stop=True).then_inc(s["k_made"], 1)
                    if part == "v":
                        pe.wait_ge(s["k_kept"], vv + 1)
                        for b in range(GB):
                            last = nc.tensor.matmul(xa[:, b * T:(b + 1) * T], xT[:, h, b * T:(b + 1) * T], w["WvT1"][:], start=True, stop=True)
                        last.then_inc(s["v_made"], 1)
                    if part == "t":
                        pe.wait_ge(s["v_kept"], vv + 1)
                        nc.tensor.matmul(xa[:], w["Wc1xT"][:], xT[:, h, :], start=True, stop=True).then_inc(s["t_made"], 1)
                    if part == "z":
                        pe.wait_ge(s["t_kept"], vv + 1)
                        for b in range(GB):
                            last = nc.tensor.matmul(xa[:, b * NH:(b + 1) * NH], th[:, b * T:(b + 1) * T], w["Wc2T"][:], start=True, stop=True)
                        last.then_inc(s["z_made"], 1)

                def scores(n, half, b, i):
                    if i == 0:
                        pe.wait_ge(s["km_made"], n + 1)
                    pe.wait_ge(s["exps"], n * HQ + i + 1 + EXP0 - HQ)
                    nc.tensor.matmul(s_ps[i][:].rearrange("p h t -> p (h t)"), qT[:, half, b * T:(b + 1) * T],
                                     km[:, b % 2, i * HQ:(i + 1) * HQ, :].rearrange("p h t -> p (h t)"),
                                     start=True, stop=True).then_inc(s["s_made"], 1)

                def turn_before(n, r, i):
                    pe.wait_ge(s["p_made"], n * HQ + i + 1)
                    pe.wait_ge(s["pt_kept"], n * HQ + i + 1)
                    for k in range(HQ):
                        last = nc.tensor.transpose(pt_ps[:, k, :], p[:, r, i * HQ + k, :], w["ident"][:])
                    last.then_inc(s["turned"], 1)

                def values_before(n, h, b, done, load):
                    pe.wait_ge(fa_in[h], load)
                    pe.wait_ge(s["pt_kept"], n * HQ + HQ + 1)
                    for i in range(HQ):
                        for k in range(HQ):
                            last = nc.tensor.matmul(y_ps[i * 32:(i + 1) * 32, b * T:(b + 1) * T], vm[:, h, b, k, i * 32:(i + 1) * 32],
                                                    pT[:, i * HQ + k, :], start=(k == 0), stop=False, skip_group_check=True)
                    last = nc.tensor.matmul(y_ps[:, b * T:(b + 1) * T], v[:, h, b, :], fab[:, h, b * T:(b + 1) * T],
                                            start=False, stop=True, skip_group_check=True)
                    if done:
                        last.then_inc(s["y_made"], 1)

                def output(u):
                    pe.wait_ge(s["y_kept"], u + 1)
                    nc.tensor.matmul(tb[:], w["WoutT"][:], yT[:], start=True, stop=True).then_inc(s["o_made"], 1)

                def mean_square(u):
                    pe.wait_ge(s["sq_kept"], u + 1)
                    nc.tensor.matmul(tb[:], w["mean"][:], sq[:], start=True, stop=True).then_inc(s["ms_made"], 1)

                def alpha_beta(u):
                    pe.wait_ge(s["h_kept"], u + 1)
                    for b in range(GB):
                        last = nc.tensor.matmul(tb[:, b * 2 * GH:(b + 1) * 2 * GH], hT[:, b * T:(b + 1) * T], w["Wba"][:], start=True, stop=True)
                    last.then_inc(s["ba_made"], 1)

                def alpha_turn():
                    pe.wait_ge(s["al_exp"], 1)
                    for g in range(GROUPS):
                        bank = tb if g < GROUPS // 2 else xa
                        at = g % (GROUPS // 2) * T
                        last = nc.tensor.transpose(bank[0:GB * GH, at:at + T], al[:, g, :, :].rearrange("p b h -> p (b h)"), w["ident"][:])
                    last.then_inc(s["al_turned"], 1)

                for part in "qkvtz":
                    project_qkv(0, 0, 16, part)
                with pe.Fori(0, TURNS) as it:
                    for half in range(2):
                        u = it * 2 + half
                        ahead = lambda part: project_qkv(u + 1, 1 - half, it * 16 + 16 + 16 * half, part)
                        for b in range(GB):
                            n = u * GB + b
                            scores(n, half, b, 0)
                            scores(n, half, b, 1)
                            if b == 2:
                                mean_square(u)
                            if b == 0:
                                values_before(n - 1, 1 - half, GB - 2, False, it * 16 + 16)
                            if b > 1:
                                if b == 2:
                                    pe.wait_ge(s["y_kept"], u + 1)
                                    pe.wait_ge(s["vm_made"], u * 2 + 2)
                                values_before(n - 1, half, b - 2, False, it * 16 + 16 + 16 * half)
                            turn_before(n, (b + 1) % 2, 0)
                            scores(n, half, b, 2)
                            turn_before(n, (b + 1) % 2, 1)
                            [lambda: ahead("q"), lambda: output(u), lambda: ahead("t"), lambda: ahead("z")][b]()
                            scores(n, half, b, 3)
                            turn_before(n, (b + 1) % 2, 2)
                            if b == 1:
                                ahead("v")
                            if b == 0:
                                ahead("k")
                            turn_before(n, (b + 1) % 2, 3)
                            if b == 3:
                                alpha_beta(u)
                            if b == 0:
                                values_before(n, 1 - half, GB - 1, True, it * 16 + 16)
                values_before(B - 1, 1, GB - 2, False, TURNS * 16 + 16)
                for i in range(HQ):
                    turn_before(B, 1, i)
                values_before(B, 1, GB - 1, True, TURNS * 16 + 16)
                output(GROUPS)
                mean_square(GROUPS)
                alpha_beta(GROUPS)
                alpha_turn()

            @block.scalar
            def _(act):
                def keep_q(vv, h):
                    act.wait_ge(s["q_made"], vv + 1)
                    nc.scalar.activation(qT[:, h, :], xa[:], ACT.Identity, bias=c["bqs"][:], scale=SCALE).then_inc(s["q_kept"], 1)

                def keep_k(vv, h):
                    act.wait_ge(s["k_made"], vv + 1)
                    nc.scalar.activation(kT[:, h, :], xa[:], ACT.Identity, bias=w["bk"][:]).then_inc(s["k_kept"], 1)

                def keep_t(vv):
                    act.wait_ge(s["c1_kept"], vv + 1)
                    act.wait_ge(s["t_made"], vv + 1)
                    for b in range(GB):
                        last = nc.scalar.activation(th[:, b * T:(b + 1) * T], xa[:, b * T:(b + 1) * T], ACT.Tanh, bias=c1g[:, b:b + 1])
                    last.then_inc(s["t_kept"], 1)

                def exp_z(vv):
                    act.wait_ge(s["z_kept"], vv + 2)
                    nc.scalar.activation(zc[:], zc[:], ACT.Exp, scale=-1.0).then_inc(s["z_exp"], 1)

                def exp_scores(n, r, i):
                    act.wait_ge(s["peak"], n * HQ + i + 1)
                    for k in range(HQ):
                        h = i * HQ + k
                        last = nc.scalar.activation(p[:, r, h, :], s_ps[i][:, k, :], ACT.Exp, bias=nm[:, r, h:h + 1],
                                                    accum_out=zs[:, r, h:h + 1])
                    last.then_inc(s["exps"], 1)

                def keep_y(u):
                    act.wait_ge(s["y_made"], u + 1)
                    nc.scalar.copy(yT[:], y_ps[:]).then_inc(s["y_kept"], 1)

                def keep_a(u):
                    act.wait_ge(s["o_made"], u + 1)
                    act.wait_ge(s["a_stored"], u * 16 + 16)
                    nc.scalar.activation(aT[:], tb[:], ACT.Identity, bias=w["bout"][:]).then_inc(s["a_kept"], 1)

                def root_ms(u):
                    act.wait_ge(s["ms_made"], u + 1)
                    nc.scalar.activation(rt[:], tb[:], ACT.Sqrt, bias=w["eps6"][:]).then_inc(s["ms_root"], 1)

                def alpha_exp():
                    act.wait_ge(s["z_sized"], 1)
                    nc.scalar.activation(ex[:], ba[:, 1:, :, :], ACT.Exp, scale=-1.0).then_inc(s["ba_exp"], 1)

                def alpha_ln():
                    act.wait_ge(s["one_kept"], 1)
                    nc.scalar.activation(lo[:], lo[:], ACT.Ln).then_inc(s["ln_kept"], 1)

                def alpha_last():
                    act.wait_ge(s["g_kept"], 1)
                    nc.scalar.activation(al[:], pos[:], ACT.Exp, scale=-1.0).then_inc(s["al_exp"], 1)

                act.sem_inc(s["exps"], EXP0)
                keep_q(0, 0)
                keep_k(0, 0)
                keep_t(0)
                exp_z(0)
                with act.Fori(0, TURNS) as it:
                    for half in range(2):
                        u = it * 2 + half
                        for b in range(GB):
                            n = u * GB + b
                            for i in range(HQ):
                                exp_scores(n, b % 2, i)
                                if b == 0 and i == 2:
                                    keep_q(u + 1, 1 - half)
                                if b == 1 and i == 0:
                                    keep_y(u)
                                    keep_k(u + 1, 1 - half)
                                if b == 1 and i == 2:
                                    keep_a(u)
                                if b == 2 and i == 2:
                                    root_ms(u)
                                    keep_t(u + 1)
                                if b == 3 and i == 2:
                                    exp_z(u + 1)
                keep_y(GROUPS)
                keep_a(GROUPS)
                root_ms(GROUPS)
                alpha_exp()
                alpha_ln()
                alpha_last()

            @block.vector
            def _(dve):
                ch = Chain(dve, s["chain"])

                def keep_v(vv, h):
                    dve.wait_ge(s["v_made"], vv + 1)
                    nc.vector.tensor_tensor(v[:, h, :, :], xa[:].rearrange("p (b f) -> p b f", f=D),
                                            w["bvb"][:].unsqueeze(1).to_broadcast([128, GB, D]), ALU.add).then_inc(s["v_kept"], 1)

                def keep_c1(vv):
                    nc.vector.tensor_scalar(c1g[:], c["c1b"][:, bass.ds(vv * GB + GB, GB)], 0.0, None, ALU.add).then_inc(s["c1_kept"], 1)

                def keep_z(vv):
                    dve.wait_ge(s["z_made"], vv + 1)
                    nc.vector.tensor_tensor(zc[:], xa[:, 0:GB * NH].rearrange("p (b h) -> p b h", h=NH),
                                            w["bc2b"][:].unsqueeze(1).to_broadcast([128, GB, NH]), ALU.add).then_inc(s["z_kept"], 1)

                def coherence(vv, h):
                    dve.wait_ge(s["z_exp"], vv + 1)
                    ch.link(nc.vector.tensor_scalar(coh[:, h, :, :], zc[:], 1.0, 1e-8, ALU.add, ALU.mult))
                    ch.link(nc.vector.tensor_scalar(coh[:, h, :, :], coh[:, h, :, :], 1.0, 1.0 / (1.0 - FIELD), ALU.add, ALU.mult))
                    nc.vector.reciprocal(coh[:, h, :, :], coh[:, h, :, :]).then_inc(s["coh_kept"], 1)
                    dve.wait_ge(s["coh_kept"], vv + 1)

                def peaks(n, r, i):
                    dve.wait_ge(s["s_made"], n * HQ + i + 1)
                    hs = slice(i * HQ, (i + 1) * HQ)
                    nc.vector.tensor_reduce(nm[:, r, hs], s_ps[i][:], AX.X, ALU.max, negate=True).then_inc(s["peak"], 1)

                def factors(n, r, i, h, b):
                    dve.wait_ge(s["exps"], n)
                    hs = slice(i * HQ, (i + 1) * HQ)
                    ch.link(nc.vector.reciprocal(rz[:, r, hs], zs[:, r, hs]))
                    nc.vector.tensor_tensor(rz[:, r, hs], rz[:, r, hs], coh[:, h, b, hs], ALU.mult).then_inc(s["rz_made"], 1)

                def keep_turned(n, i):
                    dve.wait_ge(s["turned"], n * HQ + i + 1)
                    nc.vector.tensor_copy(pT[:, i * HQ:(i + 1) * HQ, :], pt_ps[:]).then_inc(s["pt_kept"], 1)

                def square(u):
                    dve.wait_ge(s["a_kept"], u + 1)
                    nc.vector.tensor_tensor(sq[:], aT[:], aT[:], ALU.mult).then_inc(s["sq_kept"], 1)

                def turn_root(u, part):
                    dve.wait_ge(s["ms_root"], u + 1)
                    cols = slice(part * GT // 2, (part + 1) * GT // 2)
                    nc.vector.reciprocal(rt[:, cols], rt[:, cols]).then_inc(s["rt_made"], 1)

                def alpha_in(u):
                    dve.wait_ge(s["ba_made"], u + 1)
                    nc.vector.tensor_copy(ba[:, bass.ds(u, 1), :, :].squeeze(1), tb[:, 0:GB * 2 * GH].rearrange("p (b h) -> p b h", h=2 * GH)).then_inc(s["ba_kept"], 1)

                def alpha_size():
                    dve.wait_ge(s["ba_kept"], GROUPS + 1)
                    logits = ba[:, 1:, :, :].rearrange("p g b h -> p (g b) h")[:, :, GH:]
                    flat = pos[:].rearrange("p g b h -> p (g b) h")
                    ch.link(nc.vector.tensor_tensor(flat, logits, w["dtb"][:].unsqueeze(1).to_broadcast([128, B, GH]), ALU.add))
                    ch.link(nc.vector.tensor_scalar(logits, flat, -1.0, None, ALU.mult))
                    nc.vector.tensor_tensor(logits, logits, flat, ALU.max).then_inc(s["z_sized"], 1)

                def alpha_one():
                    dve.wait_ge(s["ba_exp"], 1)
                    nc.vector.tensor_scalar(lo[:], ex[:, :, :, GH:], 1.0, None, ALU.add).then_inc(s["one_kept"], 1)
                    ch.link(nc.vector.tensor_scalar(beta[:, 0:GROUPS, :, :], ex[:, :, :, 0:GH], 1.0, None, ALU.add))
                    ch.link(nc.vector.reciprocal(beta[:, 0:GROUPS, :, :], beta[:, 0:GROUPS, :, :]))

                def alpha_sum():
                    dve.wait_ge(s["ln_kept"], 1)
                    flat = pos[:].rearrange("p g b h -> p (g b) h")
                    ch.link(nc.vector.scalar_tensor_tensor(pos[:], pos[:], 0.0, lo[:], ALU.max, ALU.add))
                    nc.vector.tensor_tensor(flat, flat, c["expA"][:].unsqueeze(1).to_broadcast([128, B, GH]), ALU.mult).then_inc(s["g_kept"], 1)

                def alpha_out():
                    dve.wait_ge(s["al_turned"], 1)
                    for k, bank in enumerate((tb, xa)):
                        gs = slice(k * GROUPS // 2, (k + 1) * GROUPS // 2)
                        last = nc.vector.tensor_copy(alT[:, gs, 1:], bank[0:GB * GH, :].rearrange("p (g t) -> p g t", t=T)[:, :, 1:])
                    last.then_inc(s["al_out"], 1)

                for t in (p, pT, vm, v, coh, rz, aT, hT, beta):
                    nc.vector.memset(t[:], 0.0)
                nc.vector.memset(zs[:], 1.0)
                nc.vector.memset(y_ps[:], 0.0)
                nc.vector.memset(alT[:], 0.0).then_inc(s["primed"], 1)
                dve.wait_ge(s["primed"], 1)
                dve.sem_inc(s["z_kept"], 1)
                dve.sem_inc(s["pt_kept"], 1)
                keep_c1(0)
                keep_v(0, 0)
                keep_z(0)
                coherence(0, 0)
                before = ch.n
                with dve.Fori(0, TURNS) as it:
                    ch.turn(it, 2 * LINKS_TURN, before)
                    for half in range(2):
                        u = it * 2 + half
                        for b in range(GB):
                            n = u * GB + b
                            for i in range(HQ):
                                peaks(n, b % 2, i)
                                if i:
                                    keep_turned(n, i - 1)
                                if i == 0:
                                    factors(n * HQ + EXP0, (b + 1) % 2, HQ - 1, half if b else 1 - half, (b - 1) % GB)
                                else:
                                    factors(n * HQ + i + EXP0, b % 2, i - 1, half, b)
                                if i == HQ - 1:
                                    keep_turned(n, i)
                                if b == 0 and i == 0:
                                    keep_c1(u + 1)
                                if b == 1 and i == 3:
                                    square(u)
                                    keep_v(u + 1, 1 - half)
                                if b == 2 and i == 3:
                                    turn_root(u, 0)
                                if b == 3 and i == 0:
                                    turn_root(u, 1)
                                if b == 3 and i == 2:
                                    keep_z(u + 1)
                                if b == 3 and i == 3:
                                    coherence(u + 1, 1 - half)
                                    alpha_in(u)
                assert ch.n == 2 * LINKS_TURN, ch.n
                ch.turn(0, 0, before + GROUPS * LINKS_TURN)
                factors(B * HQ + EXP0, 1, HQ - 1, 1, GB - 1)
                for i in range(HQ):
                    keep_turned(B, i)
                square(GROUPS)
                turn_root(GROUPS, 0)
                turn_root(GROUPS, 1)
                alpha_in(GROUPS)
                alpha_size()
                alpha_one()
                alpha_sum()
                alpha_out()


def delta_rule(nc, w, dram):
    H, HH = 8, 4
    BL, NB = 32, 4
    AHEAD = RING = 8
    EPS = 1e-6
    ROW_TURNS = B // RING
    ROWS = {(0, 0): (1, 8), (0, 1): (8, 12), (0, 2): (12, 15), (0, 3): (15, 17), (1, 0): (17, 19), (1, 1): (19, 21),
            (1, 2): (21, 23), (1, 3): (23, 24), (2, 0): (24, 25), (2, 1): (25, 27), (2, 2): (27, 28), (2, 3): (28, 29),
            (3, 0): (29, 30), (3, 1): (30, BL)}
    with ExitStack() as ctx:
        m = Memory(nc, ctx, "delta")
        hk = m.sb("hk", [128, 2, T])
        hv = m.sb("hv", [128, 2, T])
        aT = m.sb("aT", [128, 2, T])
        xo = m.sb("xo", [128, 2, T])
        al = m.sb("al", [128, 2, H * T])
        ball = m.sb("ball", [128, GROUPS + 1, GB * H])
        bt = m.sb("bt", [128, H])
        kq = m.sb("kq", [128, 2, H, 2 * T])
        sq = m.sb("sq", [128, H, 2 * T])
        nrow = m.sb("nrow", [128, 2 * T])
        arg = m.sb("arg", [128, 2 * H])
        rt = m.sb("rt", [128, 2 * H])
        qe = m.sb("qe", [128, RING, H])
        qn = m.sb("qn", [128, H])
        kn = m.sb("kn", [128, RING, H])
        ck = m.sb("ck", [128, H])
        dc = m.sb("dc", [128, 2, H, T])
        la = m.sb("la", [128, RING, H, 2 * T])
        ll = m.sb("ll", [128, BL, BL])
        dd = m.sb("dd", [128, BL, BL])
        prod = m.sb("prod", [128, BL * BL])
        di = m.sb("di", [128, 2, GB * H, T])
        ct = m.sb("ct", [128, H, T])
        ad = m.sb("ad", [128, H, T])
        sv = m.sb("sv", [128, H, T])
        z = m.sb("z", [128, H, T])
        gw = m.sb("gw", [128, H, T])
        og = m.sb("og", [128, H, T])
        oT = m.sb("oT", [128, H, T])
        carry = m.sb("carry", [128, 2])
        ms = m.sb("ms", [128, H])
        x_ps = [m.ps(f"xp{i}", [128, HH, 2 * T]) for i in range(2)]
        z_ps = [m.ps(f"zp{i}", [128, HH, T]) for i in range(2)]
        n_ps = m.ps("np", [128, GT])
        w_ps = m.ps("wp", [128, HH, T])
        k_rows, k_cols, q_cols = n_ps[:, 0:2 * T], n_ps[:, 256:256 + H], n_ps[:, 256 + H:256 + 2 * H]
        ring2 = lambda name: [m.sem(f"{name}{i}") for i in range(2)]
        hk_in, hv_in, at_in, al_in, x_stored, lanes_out, inv_in = (ring2(n) for n in (
            "hk_in", "hv_in", "at_in", "al_in", "x_stored", "lanes_out", "inv_in"))
        names = ("beta_in ll_in pre_made pre_kept pre_root inv_out primed kq_made kq_kept sq_kept n_made nrow_kept ncol_made ck_made diag_made kkq_made la_kept "
                 "ca_made c_kept ad_kept g_made g_kept gw_made v_made v_kept r_made z_made z_kept o_made osq_kept og_kept "
                 "arg_made root_made rs_made o_done ot_made ot_kept wo_made x_kept dd_made chain").split()
        s = {n: m.sem(n) for n in names}

        class Row:

            def __init__(self, t, k):
                self.n, self.two, self.four = t * RING + k, t * (RING // 2) + k // 2, t * (RING // GB) + k // GB
                self.half, self.pair, self.b, self.slot = k % 2, k // GB % 2, k % GB, k % RING
                self.group = bass.ds(self.four + 1, 1)
                self.group_v = bass.ds((t + 1) * (RING // GB) + (k // GB - 1), 1)

        def turns(eng, step, begin=lambda t: None):
            with eng.Fori(0, ROW_TURNS - 1) as t:
                begin(t)
                for k in range(RING):
                    step(t, k)
            begin(ROW_TURNS - 1)
            for k in range(RING):
                step(ROW_TURNS - 1, k)

        def looped(t):
            return not isinstance(t, int)

        heads = [slice(i * HH, (i + 1) * HH) for i in range(2)]

        with nc.Block() as block:
            @block.sync
            def _(sp):
                def load_tokens(buf, src, r, sem):
                    sp.dma_start(buf[:, r.half, :], dram[src][r.group_v if buf is hv else r.group, :, r.b * T:(r.b + 1) * T].squeeze(0)).then_inc(sem[r.half], 16)

                def load_alpha(r):
                    sp.dma_start(al[:, r.half, :], dram["alpha"][r.group, r.b * H:(r.b + 1) * H, :].rearrange("u h t -> u (h t)")
                                 .to_broadcast([128, H * T])).then_inc(al_in[r.half], 16)

                def store_lanes(p):
                    sp.wait_ge(s["la_kept"], p.n * 2 + 2)
                    for g in range(NB):
                        sp.dma_start(dram["lanes"][p.pair, g, p.b * H:(p.b + 1) * H, :, :].rearrange("h j i -> j h i"),
                                     la[g * BL:(g + 1) * BL, p.slot, :, g * BL:(g + 1) * BL]).then_inc(lanes_out[p.half], 16)

                def load_lanes(p, before):
                    for half in range(2):
                        sp.wait_ge(lanes_out[half], p.four * 128 + 128)
                    if before:
                        sp.wait_ge(s["dd_made"], p.four)
                    sp.dma_start(ll[:].rearrange("p j i -> p (j i)"),
                                 dram["lanes"][p.pair, :, :, :, :].rearrange("g h j i -> (g h) (j i)")).then_inc(s["ll_in"], 16)

                def move_inverses(p):
                    sp.wait_ge(s["dd_made"], p.four + 1)
                    sp.dma_start(dram["inverses"][p.pair, :, :, :, :].rearrange("g h i j -> (g h) (i j)"),
                                 dd[:].rearrange("p i j -> p (i j)")).then_inc(s["inv_out"], 16)
                    sp.wait_ge(s["inv_out"], p.four * 16 + 16)
                    for g in range(NB):
                        sp.dma_start(di[g * BL:(g + 1) * BL, p.pair, :, g * BL:(g + 1) * BL],
                                     dram["inverses"][p.pair, g, :, :, :].rearrange("h i j -> i h j")).then_inc(inv_in[p.pair], 16)

                def store_x(r):
                    sp.wait_ge(s["x_kept"], r.n + 2)
                    sp.dma_start(dram["xpT"][r.group, :, r.b * T:(r.b + 1) * T].squeeze(0), xo[:, r.half, :]).then_inc(x_stored[r.half], 16)

                def step(t, k):
                    r = Row(t, k)
                    load_tokens(aT, "aT", r, at_in)
                    if looped(t):
                        sp.wait_ge(s["la_kept"], r.n * 2 + 2 * AHEAD)
                        load_alpha(Row(t, k + AHEAD + 1))
                    if k % GB == GB - 1 and (looped(t) or k + 1 < RING):
                        move_inverses(Row(t, k + 1))
                    if looped(t):
                        sp.wait_ge(s["n_made"], r.n + AHEAD + 1)
                        load_tokens(hk, "hT", Row(t, k + AHEAD + 2), hk_in)
                    store_x(Row(t, k - 1))
                    if looped(t) or k + 2 < RING:
                        sp.wait_ge(s["g_made"], r.n * 2 + 2)
                        load_tokens(hv, "hT", Row(t, k + 2), hv_in)
                    if looped(t):
                        p = Row(t, k + AHEAD)
                        store_lanes(p)
                        if p.b == GB - 1:
                            load_lanes(p, True)

                sp.dma_start(ball[:], dram["beta"][1:GROUPS + 2, :, :].rearrange("g t h -> t g h")).then_inc(s["beta_in"], 16)
                for k in range(2):
                    load_tokens(hk, "hT", Row(0, k), hk_in)
                    load_alpha(Row(0, k))
                for k in range(2):
                    load_tokens(hv, "hT", Row(0, k), hv_in)
                load_tokens(aT, "aT", Row(0, -1), at_in)
                sp.wait_ge(s["primed"], 1)
                for half in range(2):
                    sp.dma_start(dram["xpT"][GROUPS + 1, :, half * T:(half + 1) * T], xo[:, half, :]).then_inc(x_stored[half], 16)
                for k in range(AHEAD):
                    sp.wait_ge(s["n_made"], k + 1)
                    load_tokens(hk, "hT", Row(0, k + 2), hk_in)
                    store_lanes(Row(0, k))
                    if k + 2 <= AHEAD:
                        load_alpha(Row(0, k + 2))
                    if k == GB - 1:
                        load_lanes(Row(0, k), False)
                move_inverses(Row(0, 0))
                load_lanes(Row(0, RING - 1), True)
                turns(sp, step)
                store_x(Row(ROW_TURNS - 1, RING - 1))
                for half in range(2):
                    sp.wait_ge(x_stored[half], 16 * (B // 2 + 1 + half))
                    sp.wait_ge(hk_in[half], 16 * (B // 2 + 1))
                sp.wait_ge(al_in[0], 16 * (B // 2 + 1))

            @block.tensor
            def _(pe):
                def project(ps, p, heads):
                    for j, h in enumerate(heads):
                        nc.tensor.matmul(ps[:, j, 0:T], w["dWk"][:, h * T:(h + 1) * T], hk[:, p.half, :], start=True, stop=True)
                        last = nc.tensor.matmul(ps[:, j, T:], w["dWq"][:, h * T:(h + 1) * T], hk[:, p.half, :], start=True, stop=True)
                    return last

                def project_kq(p, i):
                    if i == 0:
                        pe.wait_ge(hk_in[p.half], p.two * 16 + 16)
                    project(x_ps[i], p, range(i * HH, (i + 1) * HH)).then_inc(s["kq_made"], 1)

                def project_ahead(p):
                    pe.wait_ge(hk_in[p.half], p.two * 16 + 16)
                    for i in range(4):
                        if p.n * 4 + i > 1:
                            pe.wait_ge(s["pre_kept"], p.n * 4 + i - 1)
                        project(z_ps[i % 2][:].rearrange("p (h a) t -> p h (a t)", a=2), p, range(2 * i, 2 * i + 2)).then_inc(s["pre_made"], 1)

                def norms(p, before=True):
                    pe.wait_ge(s["sq_kept"], p.n + 1)
                    if before:
                        pe.wait_ge(s["ck_made"], p.n)
                    for a in range(2):
                        for g in range(4):
                            last = nc.tensor.matmul(k_rows[g * 32:(g + 1) * 32, :], w["headrow"][:, a, :], sq[:, g + 4 * a, :],
                                                    start=(a == 0), stop=(a == 1))
                    last.then_inc(s["n_made"], 1)

                def norm_columns(p):
                    pe.wait_ge(s["nrow_kept"], p.n + 1)
                    nc.tensor.matmul(k_cols, nrow[:, 0:T], w["headpick"][:], start=True, stop=True)
                    nc.tensor.matmul(q_cols, nrow[:, T:], w["headpick"][:], start=True, stop=True).then_inc(s["ncol_made"], 1)

                def key_products(p, i):
                    for j, h in enumerate(range(i * HH, (i + 1) * HH)):
                        last = nc.tensor.matmul(x_ps[i][:, j, :], kq[:, p.half, h, 0:T], kq[:, p.half, h, :], start=True, stop=True)
                    last.then_inc(s["kkq_made"], 1)

                def invert(r, i):
                    for j, h in enumerate(range(i * HH, (i + 1) * HH)):
                        last = nc.tensor.matmul(x_ps[i][:, j, :], di[:, r.pair, r.b * H + h, :], la[:, r.slot, h, :], start=True, stop=True)
                    last.then_inc(s["ca_made"], 1)

                def project_gate(r, i):
                    pe.wait_ge(s["v_kept"], r.n * 2 + i + 1)
                    nc.tensor.matmul(z_ps[i][:].rearrange("p h t -> p (h t)"), hv[:, r.half, :], w["dWg"][:, i * GT:(i + 1) * GT],
                                     start=True, stop=True).then_inc(s["g_made"], 1)

                def project_v(r, i):
                    if i == 0:
                        pe.wait_ge(hv_in[r.half], r.two * 16 + 16)
                    pe.wait_ge(s["og_kept"], r.n * 2 + i + 1)
                    nc.tensor.matmul(z_ps[i][:].rearrange("p h t -> p (h t)"), hv[:, r.half, :], w["dWv"][:, i * GT:(i + 1) * GT],
                                     start=True, stop=True).then_inc(s["v_made"], 1)

                def correct(r, round, i):
                    if round == 0:
                        pe.wait_ge(s["c_kept"], r.n * 2 + i + 1)
                        pe.wait_ge(s["g_kept"], r.n * 2 + i + 1)
                        pe.wait_ge(s["r_made"], r.n + 1)
                    else:
                        pe.wait_ge(s["z_kept"], r.n * 6 + 2 * round + i - 1)
                    for j, h in enumerate(range(i * HH, (i + 1) * HH)):
                        last = nc.tensor.matmul(z_ps[i][:, j, :], ct[:, h, :], (z if round else sv)[:, h, :], start=True, stop=True)
                    last.then_inc(s["z_made"], 1)

                def attend(r, i):
                    pe.wait_ge(s["z_kept"], r.n * 6 + i + 5)
                    pe.wait_ge(s["ad_kept"], r.n * 2 + i + 1)
                    for j, h in enumerate(range(i * HH, (i + 1) * HH)):
                        last = nc.tensor.matmul(z_ps[i][:, j, :], ad[:, h, :], z[:, h, :], start=True, stop=True)
                    last.then_inc(s["o_made"], 1)

                def turn_output(r, i):
                    if i == 0:
                        pe.wait_ge(s["o_done"], r.n + 2)
                    else:
                        pe.wait_ge(s["ot_kept"], r.n * 2 + 3)
                    for j, h in enumerate(range(i * HH, (i + 1) * HH)):
                        last = nc.tensor.transpose(w_ps[:, j, :], og[:, h, :], w["ident"][:])
                    last.then_inc(s["ot_made"], 1)

                def output(r):
                    pe.wait_ge(s["ot_kept"], r.n * 2 + 4)
                    for h in range(H):
                        last = nc.tensor.matmul(w_ps[:, 0, :], w["dWo"][:, h, :], oT[:, h, :], start=(h == 0), stop=(h == H - 1))
                    last.then_inc(s["wo_made"], 1)

                def step(t, k):
                    r, q, p, before = Row(t, k), Row(t, k + AHEAD), Row(t, k + AHEAD + 1), Row(t, k - 1)
                    if r.b == 0:
                        pe.wait_ge(inv_in[r.pair], (t + 1) * 16 * NB)
                    for i in range(2):
                        if looped(t) or k == 0:
                            pe.wait_ge(s["sq_kept"], r.n + AHEAD + 1)
                        else:
                            pe.wait_ge(s["ad_kept"], (r.n - 1) * 2 + i + 1)
                        invert(r, i)
                    for i in range(2):
                        project_v(r, i)
                    for i in range(2):
                        if looped(t):
                            pe.wait_ge(s["ad_kept"], r.n * 2 + i + 1)
                            key_products(q, i)
                        if i == 0:
                            project_gate(r, 0)
                            project_gate(r, 1)
                    for i in range(2):
                        correct(r, 0, i)
                    if looped(t):
                        pe.wait_ge(s["la_kept"], q.n * 2 + 1)
                        project_kq(p, 0)
                    turn_output(before, 0)
                    for i in range(2):
                        correct(r, 1, i)
                    if looped(t):
                        pe.wait_ge(s["la_kept"], q.n * 2 + 2)
                        project_kq(p, 1)
                    turn_output(before, 1)
                    for i in range(2):
                        correct(r, 2, i)
                    output(before)
                    if looped(t):
                        norms(p)
                    for i in range(2):
                        attend(r, i)
                    if looped(t):
                        norm_columns(p)

                project_ahead(Row(0, 0))
                for k in range(AHEAD + 1):
                    p = Row(0, k)
                    norms(p, k > 0)
                    if k < AHEAD:
                        project_ahead(Row(0, k + 1))
                    norm_columns(p)
                    if k < AHEAD:
                        for i in range(2):
                            if k:
                                pe.wait_ge(s["la_kept"], 2 * k + i - 1)
                            key_products(p, i)
                pe.wait_ge(s["la_kept"], 2 * AHEAD)
                pe.wait_ge(s["pre_kept"], 4 * AHEAD + 4)
                pe.wait_ge(s["primed"], 1)
                turns(pe, step)
                last = Row(ROW_TURNS - 1, RING - 1)
                for i in range(2):
                    turn_output(last, i)
                output(last)

            @block.scalar
            def _(act):
                def square(p):
                    nc.scalar.activation(sq[:], kq[:, p.half, :, :], ACT.Square).then_inc(s["sq_kept"], 1)

                def keep_ahead(p):
                    for i in range(4):
                        act.wait_ge(s["pre_made"], p.n * 4 + i + 1)
                        nc.scalar.activation(kq[:, p.half, 2 * i:2 * i + 2, :].rearrange("p h t -> p (h t)"),
                                             z_ps[i % 2][:].rearrange("p h t -> p (h t)"), ACT.Silu).then_inc(s["pre_kept"], 1)
                    act.wait_ge(s["pre_kept"], p.n * 4 + 4)
                    square(p)

                def keep_kq(p, i):
                    act.wait_ge(s["kq_made"], (p.n - AHEAD - 1) * 2 + i + 1)
                    nc.scalar.activation(kq[:, p.half, heads[i], :], x_ps[i][:], ACT.Silu).then_inc(s["kq_kept"], 1)

                def keep_v(r):
                    for i in range(2):
                        act.wait_ge(s["v_made"], r.n * 2 + i + 1)
                        nc.scalar.activation(sv[:, heads[i], :], z_ps[i][:], ACT.Silu).then_inc(s["v_kept"], 1)

                def turn_kept(r, i):
                    act.wait_ge(s["ot_made"], r.n * 2 + i + 3)
                    nc.scalar.copy(oT[:, heads[i], :], w_ps[:]).then_inc(s["ot_kept"], 1)

                def step(t, k):
                    r, p, before = Row(t, k), Row(t, k + AHEAD + 1), Row(t, k - 1)
                    for i in range(2):
                        act.wait_ge(s["c_kept"], r.n * 2 + i + 1)
                        nc.scalar.copy(ad[:, heads[i], :], x_ps[i][:, :, T:]).then_inc(s["ad_kept"], 1)
                    keep_v(r)
                    for i in range(2):
                        act.wait_ge(s["g_made"], r.n * 2 + i + 1)
                        nc.scalar.activation(gw[:, heads[i], :], z_ps[i][:], ACT.Silu).then_inc(s["g_kept"], 1)
                    if looped(t):
                        keep_kq(p, 0)
                    turn_kept(before, 0)
                    if looped(t):
                        keep_kq(p, 1)
                    turn_kept(before, 1)
                    if looped(t):
                        act.wait_ge(s["kq_kept"], (p.n - AHEAD - 1) * 2 + 2)
                        square(p)
                    for i in range(2):
                        act.wait_ge(s["o_made"], r.n * 2 + i + 1)
                        for j in range(HH):
                            last = nc.scalar.activation(sq[:, i * HH + j, 0:T], z_ps[i][:, j, :], ACT.Square, scale=T ** -0.5,
                                                        accum_out=ms[:, i * HH + j:i * HH + j + 1])
                        last.then_inc(s["osq_kept"], 1)
                    act.wait_ge(s["arg_made"], r.n + 2)
                    nc.scalar.activation(rt[:], arg[:], ACT.Sqrt).then_inc(s["root_made"], 1)

                for k in range(AHEAD + 1):
                    keep_ahead(Row(0, k))
                act.wait_ge(s["arg_made"], 1)
                nc.scalar.activation(kn[:], kn[:], ACT.Sqrt).then_inc(s["pre_root"], 1)
                nc.scalar.activation(rt[:, 0:H], arg[:, 0:H], ACT.Sqrt).then_inc(s["root_made"], 1)
                turns(act, step)
                for i in range(2):
                    turn_kept(Row(ROW_TURNS - 1, RING - 1), i)

            @block.gpsimd
            def _(pool):
                def diagonal(p):
                    pool.wait_ge(s["ck_made"], p.n + 1)
                    nc.gpsimd.tensor_tensor(dc[:, p.half, :, :], w["ident"][:].unsqueeze(1).to_broadcast([128, H, T]),
                                            ck[:].unsqueeze(2).to_broadcast([128, H, T]), ALU.mult).then_inc(s["diag_made"], 1)

                def scale_v(r):
                    pool.wait_ge(s["v_kept"], r.n * 2 + 2)
                    nc.gpsimd.tensor_tensor(sv[:], sv[:], kn[:, r.slot, :].unsqueeze(2).to_broadcast([128, H, T]),
                                            ALU.mult).then_inc(s["r_made"], 1)

                def step(t, k):
                    r, p = Row(t, k), Row(t, k + AHEAD + 1)
                    scale_v(r)
                    pool.wait_ge(s["g_kept"], r.n * 2 + 2)
                    nc.gpsimd.tensor_tensor(gw[:], gw[:], w["onw"][:].unsqueeze(1).to_broadcast([128, H, T]),
                                            ALU.mult).then_inc(s["gw_made"], 1)
                    pool.wait_ge(s["og_kept"], r.n * 2 + 4)
                    pool.wait_ge(s["rs_made"], r.n + 1)
                    nc.gpsimd.tensor_tensor(og[:], og[:], rt[:, H:].unsqueeze(2).to_broadcast([128, H, T]),
                                            ALU.mult).then_inc(s["o_done"], 1)
                    if looped(t):
                        diagonal(p)

                nc.gpsimd.memset(di[:], 0.0)
                nc.gpsimd.memset(xo[:], 0.0)
                nc.gpsimd.memset(og[:], 0.0).then_inc(s["primed"], 1)
                pool.wait_ge(s["primed"], 1)
                pool.sem_inc(s["o_done"], 1)
                for k in range(AHEAD + 1):
                    diagonal(Row(0, k))
                pool.wait_ge(s["pre_root"], 1)
                turns(pool, step)

            @block.vector
            def _(dve):
                ch = Chain(dve, s["chain"])

                def keep_rows(p):
                    ch.link(nc.vector.tensor_scalar(bt[:], ball[:].rearrange("p g h -> p (g h)")[:, bass.ds(p.n * H, H)], 0.0, None, ALU.add))
                    dve.wait_ge(s["n_made"], p.n + 1)
                    nc.vector.tensor_copy(nrow[:], k_rows).then_inc(s["nrow_kept"], 1)

                def keep_columns(p, squares, eps_q):
                    dve.wait_ge(s["ncol_made"], p.n + 1)
                    ch.link(nc.vector.tensor_scalar(squares, k_cols, EPS, None, ALU.add))
                    nc.vector.tensor_scalar(eps_q, q_cols, EPS, EPS * T, ALU.add, ALU.mult)
                    ch.link(nc.vector.reciprocal(ck[:], squares))
                    nc.vector.tensor_tensor(ck[:], ck[:], bt[:], ALU.mult).then_inc(s["ck_made"], 1)

                def decays(p):
                    dve.wait_ge(s["diag_made"], p.n + 1)
                    dve.wait_ge(al_in[p.half], p.two * 16 + 16)
                    dcf = dc[:, p.half, :, :].rearrange("p h t -> p (h t)")
                    ch.link(nc.vector.tensor_tensor_scan(dcf, al[:, p.half, :], dcf, 0.0, ALU.mult, ALU.add))

                def keep_la(p):
                    for i in range(2):
                        dve.wait_ge(s["kkq_made"], p.n * 2 + i + 1)
                        nc.vector.tensor_tensor(la[:, p.slot, heads[i], :].rearrange("p h (a t) -> p h a t", t=T),
                                                x_ps[i][:].rearrange("p h (a t) -> p h a t", t=T),
                                                dc[:, p.half, heads[i], :].unsqueeze(2).to_broadcast([128, HH, 2, T]), ALU.mult).then_inc(s["la_kept"], 1)

                def inverses(p, first, end, before):
                    if first == 1:
                        dve.wait_ge(s["ll_in"], p.four * 16 + 16)
                        if before:
                            dve.wait_ge(s["inv_out"], p.four * 16)
                    for i in range(first, end):
                        pr = prod[:, 0:i * i].rearrange("p (j a) -> p j a", a=i)
                        ch.link(nc.vector.tensor_tensor(pr, dd[:, 0:i, 0:i].rearrange("p a j -> p j a"),
                                                        ll[:, 0:i, i].unsqueeze(1).to_broadcast([128, i, i]), ALU.mult))
                        last = nc.vector.tensor_reduce(dd[:, i, 0:i], pr, AX.X, ALU.add, negate=True)
                        if i < BL - 1:
                            ch.link(last)
                        else:
                            last.then_inc(s["dd_made"], 1)

                def residual(r):
                    dve.wait_ge(s["wo_made"], r.n + 2)
                    dve.wait_ge(at_in[r.half], (r.two + 1 + r.half) * 16)
                    dve.wait_ge(x_stored[r.half], (r.two + 1 + r.half) * 16)
                    nc.vector.tensor_tensor(xo[:, r.half, :], aT[:, r.half, :], w_ps[:, 0, :], ALU.add).then_inc(s["x_kept"], 1)

                def step(t, k):
                    r, q, p, before = Row(t, k), Row(t, k + AHEAD), Row(t, k + AHEAD + 1), Row(t, k - 1)
                    group = Row(t, (k // GB + 1) * GB)

                    def part(place):
                        if (k % GB, place) in ROWS and (looped(t) or k < GB):
                            inverses(group, *ROWS[k % GB, place], True)

                    def correct(round):
                        for i in range(2):
                            dve.wait_ge(s["z_made"], r.n * 6 + 2 * round + i + 1)
                            nc.vector.tensor_tensor(z[:, heads[i], :], sv[:, heads[i], :], z_ps[i][:], ALU.subtract).then_inc(s["z_kept"], 1)

                    for i in range(2):
                        dve.wait_ge(s["ca_made"], r.n * 2 + i + 1)
                        nc.vector.tensor_tensor(ct[:, heads[i], :], x_ps[i][:, :, 0:T],
                                                w["offblock"][:].unsqueeze(1).to_broadcast([128, HH, T]), ALU.mult).then_inc(s["c_kept"], 1)
                    if looped(t):
                        decays(q)
                    part(0)
                    if looped(t):
                        keep_la(q)
                    correct(0)
                    part(1)
                    correct(1)
                    part(2)
                    correct(2)
                    residual(before)
                    part(3)
                    if looped(t):
                        keep_rows(p)
                    for i in range(2):
                        dve.wait_ge(s["osq_kept"], r.n * 2 + i + 1)
                        if i == 0:
                            dve.wait_ge(s["gw_made"], r.n + 1)
                        nc.vector.tensor_tensor(og[:, heads[i], :], z_ps[i][:], gw[:, heads[i], :], ALU.mult).then_inc(s["og_kept"], 1)
                    last = nc.vector.tensor_tensor(arg[:, H:], ms[:], qe[:, r.slot, :], ALU.add)
                    if looped(t):
                        ch.link(last)
                        nc.vector.tensor_copy(kn[:, r.slot, :], rt[:, 0:H])
                        nc.vector.tensor_copy(qe[:, r.slot, :], qn[:])
                        keep_columns(p, arg[:, 0:H], qn[:])
                        last = nc.vector.memset(carry[:, r.half:r.half + 1], 0.0)
                    last.then_inc(s["arg_made"], 1)
                    dve.wait_ge(s["root_made"], r.n + 2)
                    nc.vector.reciprocal(rt[:, H:], rt[:, H:]).then_inc(s["rs_made"], 1)

                nc.vector.memset(arg[:], 1.0)
                ch.link(nc.vector.memset(dd[:], 0.0))
                ch.link(nc.vector.memset(dd[:].rearrange("p i j -> p (i j)")[:, 0:BL * BL:BL + 1], 1.0))
                dve.sem_inc(s["og_kept"], 2)
                dve.wait_ge(s["beta_in"], 16)
                for k in range(AHEAD + 1):
                    p = Row(0, k)

                    def part(place):
                        n = (k - GB) * 3 + place
                        if 0 <= n < len(ROWS):
                            inverses(Row(0, 0), *list(ROWS.values())[n], False)

                    keep_rows(p)
                    part(0)
                    if k == AHEAD:
                        keep_columns(p, arg[:, 0:H], qn[:])
                    else:
                        keep_columns(p, kn[:, p.slot, :], qe[:, p.slot, :])
                        part(1)
                        decays(p)
                        keep_la(p)
                        part(2)
                for n in range((AHEAD - GB) * 3 + 1, len(ROWS)):
                    inverses(Row(0, 0), *list(ROWS.values())[n], False)
                nc.vector.memset(carry[:, 1:2], 0.0).then_inc(s["arg_made"], 1)
                before = ch.n
                links = RING * 5 + RING // GB * (2 * BL - 3)
                turns(dve, step, lambda t: ch.turn(t, links, before))
                residual(Row(ROW_TURNS - 1, RING - 1))


def last_layer(nc, w, dram):
    HT = 4
    Q = 32
    A16, W8 = 32767.0, 127.0
    ROUND = 1.5 * 2.0 ** 23
    EPS, TINY = 1e-6, 1e-8
    with ExitStack() as ctx:
        m = Memory(nc, ctx, "last")
        xp = m.sb("xp", [128, 2, GT])
        x2 = m.sb("x2", [128, 2, GT])
        xs = m.sb("xs", [128, 2, GT])
        sq = m.sb("sq", [128, GT])
        r2 = m.sb("r2", [128, 2, GT])
        rl = m.sb("rl", [128, HT, GT])
        f2 = m.sb("f2", [128, 2, HT, GT])
        x3 = m.sb("x3", [128, 2, GT])
        x3b = m.sb("x3b", [128, GROUPS * GT])
        xr = m.sb("xr", [128, GROUPS * GT])
        hid = m.sb("hid", [128, GROUPS * HT * GT])
        out = m.sb("out", [128, 2, GT])
        rotT = m.sb("rotT", [128, D])
        side = m.sb("side", [128, 2, 4, Q])
        qsq = m.sb("qsq", [128, B + 4])
        qn = m.sb("qn", [128, 2])
        qc = m.sb("qc", [128, 2, 4])
        win = m.sb("win", [128, HT, D])
        wq = m.sb("wq", [128, 2, HT, D])
        wsc = m.sb("wsc", [128, 2, HT])
        gsc = m.sb("gsc", [128, HT])
        osc = m.sb("osc", [128, HT])
        am = m.sb("am", [128, GROUPS])
        peak = m.sb("peak", [128, 1])
        one = m.sb("one", [1, 1])
        sc = m.sb("sc", [128, 2])
        isc = m.sb("isc", [128, 1])
        shift = m.sb("shift", [128, 1])
        carry = m.sb("carry", [128, 2])
        carry_a = m.sb("carry_a", [128, 2])
        f_ps = [m.ps(f"fp{j}", [128, GT]) for j in range(HT)]
        ms_ps, y_ps, r_ps, s_ps = (m.ps(n, [128, GT]) for n in ("msp", "yp", "rp", "sp"))
        h_ps = [f_ps, [ms_ps, y_ps, r_ps, s_ps]]
        o_ps = [y_ps, r_ps]
        x_in = [m.sem(f"x_in{i}") for i in range(2)]
        out_stored = [m.sem(f"out_stored{i}") for i in range(2)]
        names = ("primed q_made q_root sides_made rot_made rot_kept win_made win_turned win_kept sq_kept fc_made rl_kept "
                 "f2_low f2_high ms_made r2_kept xs_made y_made y_kept x3_kept x3b_kept xr_made xr_kept am_made peak_made peak_turned "
                 "one_made one_spread scaled xi_rounded xi_made h_made h_kept t_made t_low t_high o_made o_kept chain").split()
        s = {n: m.sem(n) for n in names}

        class Group:

            def __init__(self, it, k):
                self.n, self.half = it * 2 + k, k % 2
                self.loads, self.stores = it * 32 + k // 2 * 32 + 32, it * 16 + k // 2 * 16 + 16

            def of(self, size):
                return bass.ds(self.n * size, size)

        def all_groups(eng, step):
            with eng.Fori(0, TURNS) as it:
                for k in range(2):
                    step(Group(it, k))

        def groups(eng, first, second, third=lambda g: None):
            first(Group(0, 0))
            first(Group(0, 1))
            second(Group(0, 0))
            with eng.Fori(0, TURNS - 1) as it:
                for k in range(2):
                    first(Group(it, k + 2))
                    third(Group(it, k))
                    second(Group(it, k + 1))
            third(Group(TURNS - 1, 0))
            second(Group(TURNS - 1, 1))
            third(Group(TURNS - 1, 1))

        with nc.Block() as block:
            @block.sync
            def _(sp):
                def load(g):
                    slot = bass.ds(g.n + 1, 1)
                    sp.dma_start(xp[:, g.half, :], dram["xpT"][slot, :, :].squeeze(0)).then_inc(x_in[g.half], 16)
                    sp.dma_start(x2[:, g.half, :], dram["x2T"][slot, :, :].squeeze(0)).then_inc(x_in[g.half], 16)

                def store(g):
                    sp.wait_ge(s["o_kept"], g.n + 1)
                    sp.dma_start(dram["outT"][bass.ds(g.n, 1), :, :].squeeze(0), out[:, g.half, :]).then_inc(out_stored[g.half], 16)

                load(Group(0, 0))
                load(Group(0, 1))
                sp.wait_ge(s["primed"], 1)
                for half in range(2):
                    sp.dma_start(dram["xpT"][GROUPS + 1, :, :], out[:, half, :]).then_inc(out_stored[half], 16)
                    sp.wait_ge(out_stored[half], 16)
                with sp.Fori(0, TURNS - 1) as it:
                    for k in range(2):
                        sp.wait_ge(s["xs_made"], it * 2 + k + 1)
                        sp.wait_ge(s["sq_kept"], it * 2 + k + 1)
                        sp.wait_ge(s["fc_made"], (it * 2 + k) * HT + HT)
                        load(Group(it, k + 2))
                with sp.Fori(0, TURNS) as it:
                    for k in range(2):
                        store(Group(it, k))
                for half in range(2):
                    sp.wait_ge(out_stored[half], 16 * (TURNS + 1))

            @block.tensor
            def _(pe):
                def feed(g):
                    pe.wait_ge(x_in[g.half], g.loads)
                    for j in range(HT):
                        pe.wait_ge(s["rl_kept"], g.n * HT + j + 1)
                        nc.tensor.matmul(f_ps[j][:], w["Wfc"][:, j * D:(j + 1) * D], xp[:, g.half, :], start=True, stop=True).then_inc(s["fc_made"], 1)
                    pe.wait_ge(s["sq_kept"], g.n + 1)
                    pe.wait_ge(s["r2_kept"], g.n + 1)
                    nc.tensor.matmul(ms_ps[:], w["mean"][:], sq[:], start=True, stop=True).then_inc(s["ms_made"], 1)

                def project(g):
                    pe.wait_ge(s["f2_low"], g.n + 2)
                    pe.wait_ge(s["f2_high"], g.n + 2)
                    pe.wait_ge(s["y_kept"], g.n + 1)
                    for j in range(HT):
                        last = nc.tensor.matmul(y_ps[:], w["Wproj"][:, j, :], f2[:, g.half, j, :], start=(j == 0), stop=(j == HT - 1))
                    last.then_inc(s["y_made"], 1)

                def turn_x3(g):
                    pe.wait_ge(s["x3_kept"], g.n + 3)
                    pe.wait_ge(s["xr_kept"], g.n + 1)
                    nc.tensor.matmul(r_ps[:], rotT[:], x3[:, g.half, :], start=True, stop=True).then_inc(s["xr_made"], 1)

                def spread(k):
                    pe.wait_ge(s["peak_made"], k + 1)
                    nc.tensor.matmul(s_ps[0:1, 0:128], peak[:], w["ident"][:], start=True, stop=True).then_inc(s["peak_turned"], 1)
                    pe.wait_ge(s["one_made"], k + 1)
                    nc.tensor.matmul(s_ps[:, 128:129], w["ones"][0:1, :], one[:], start=True, stop=True).then_inc(s["one_spread"], 1)

                def hidden(g):
                    pe.wait_ge(s["xi_made"], g.n + 1)
                    pe.wait_ge(s["h_kept"], g.n + 1)
                    for j in range(HT):
                        last = nc.tensor.matmul(h_ps[g.half][j][:], win[:, j, :], xr[:, g.of(GT)], start=True, stop=True)
                    last.then_inc(s["h_made"], 1)

                def output(g):
                    pe.wait_ge(s["t_low"], g.n + 1)
                    pe.wait_ge(s["t_high"], g.n + 1)
                    for j in range(HT):
                        last = nc.tensor.matmul(o_ps[g.half][:], wq[:, 1, j, :], f2[:, g.half, j, :], start=(j == 0), stop=(j == HT - 1))
                    last.then_inc(s["o_made"], 1)

                pe.wait_ge(s["sides_made"], 1)
                nc.tensor.matmul(s_ps[:, 0:D], side[:, 0, :, :].rearrange("p c d -> p (c d)"), side[:, 1, :, :].rearrange("p c d -> p (c d)"),
                                 start=True, stop=True).then_inc(s["rot_made"], 1)
                pe.wait_ge(s["win_made"], 1)
                for j in range(HT):
                    last = nc.tensor.transpose(ms_ps[:, j * D:(j + 1) * D], wq[:, 0, j, :], w["ident"][:])
                last.then_inc(s["win_turned"], 1)
                pe.wait_ge(s["win_kept"], 1)
                pe.wait_ge(s["rot_kept"], 1)
                groups(pe, feed, project, turn_x3)
                spread(0)
                all_groups(pe, hidden)
                spread(1)
                all_groups(pe, output)

            @block.scalar
            def _(act):
                def feed(g):
                    for j in range(HT):
                        act.wait_ge(s["fc_made"], g.n * HT + j + 1)
                        act.wait_ge(s["f2_low" if j < 2 else "f2_high"], g.n + 1)
                        nc.scalar.activation(rl[:, j, :], f_ps[j][:], ACT.Relu).then_inc(s["rl_kept"], 1)
                        if j == 0:
                            nc.scalar.activation(sq[:], xp[:, g.half, :], ACT.Square).then_inc(s["sq_kept"], 1)

                def keep_x3(g):
                    act.wait_ge(s["x3_kept"], g.n + 3)
                    nc.scalar.copy(carry_a[:, g.half:g.half + 1], shift[:])
                    nc.scalar.activation(x3b[:, g.of(GT)], x3[:, g.half, :], ACT.Identity, bias=w["bout2"][:]).then_inc(s["x3b_kept"], 1)

                def keep_hidden(g):
                    act.wait_ge(s["h_made"], g.n + 1)
                    nc.scalar.copy(carry_a[:, g.half:g.half + 1], shift[:])
                    for j in range(HT):
                        last = nc.scalar.activation(hid[:, bass.ds(g.n * (HT * GT) + j * GT, GT)], h_ps[g.half][j][:], ACT.Gelu,
                                                    bias=w["bin"][:, j:j + 1], scale=gsc[:, j:j + 1])
                    last.then_inc(s["h_kept"], 1)

                def round_high(g):
                    act.wait_ge(s["t_made"], g.n + 1)
                    nc.scalar.activation(f2[:, g.half, 2:, :], f2[:, g.half, 2:, :], ACT.Identity, bias=shift[:]).then_inc(s["t_high"], 1)

                act.sem_inc(s["rl_kept"], HT)
                act.sem_inc(s["x3b_kept"], 2)
                act.wait_ge(s["q_made"], 1)
                nc.scalar.activation(qn[:], qn[:], ACT.Sqrt).then_inc(s["q_root"], 1)
                groups(act, feed, lambda g: None, keep_x3)
                act.wait_ge(s["x3b_kept"], GROUPS + 2)
                act.wait_ge(s["scaled"], 1)
                act.sem_inc(s["h_kept"], 2)
                all_groups(act, keep_hidden)
                all_groups(act, round_high)

            @block.gpsimd
            def _(pool):
                def feed(g):
                    pool.wait_ge(x_in[g.half], g.loads)
                    pool.wait_ge(s["x3_kept"], g.n + 1)
                    nc.gpsimd.tensor_tensor(xs[:, g.half, :], xp[:, g.half, :], x2[:, g.half, :], ALU.add).then_inc(s["xs_made"], 1)
                    pool.wait_ge(s["rl_kept"], g.n * HT + 2 * HT)
                    nc.gpsimd.tensor_tensor(f2[:, g.half, 2:, :], rl[:, 2:, :], rl[:, 2:, :], ALU.mult).then_inc(s["f2_high"], 1)

                pool.sem_inc(s["f2_high"], 1)
                nc.gpsimd.memset(out[:], 0.0).then_inc(s["primed"], 1)
                def round_xr(g):
                    pool.wait_ge(s["xi_rounded"], g.n + 1)
                    nc.gpsimd.tensor_tensor(xr[:, g.of(GT)], xr[:, g.of(GT)], shift[:].to_broadcast([128, GT]), ALU.add).then_inc(s["xi_made"], 1)

                def round_low(g):
                    pool.wait_ge(s["t_made"], g.n + 1)
                    nc.gpsimd.tensor_tensor(f2[:, g.half, 0:2, :], f2[:, g.half, 0:2, :], shift[:].unsqueeze(2).to_broadcast([128, 2, GT]),
                                            ALU.add).then_inc(s["t_low"], 1)

                all_groups(pool, feed)
                all_groups(pool, round_xr)
                all_groups(pool, round_low)

            @block.vector
            def _(dve):
                ch = Chain(dve, s["chain"])

                def quaternions():
                    ch.link(nc.vector.tensor_tensor(qsq[:, 0:B], w["qleft_all"][:], w["qleft_all"][:], ALU.mult))
                    ch.link(nc.vector.tensor_tensor(qsq[:, B:], w["qright"][:], w["qright"][:], ALU.mult))
                    nc.vector.tensor_reduce(qn[:, 0:1], qsq[:, B:], AX.X, ALU.add)
                    ch.link(nc.vector.tensor_reduce(qn[:, 1:2], qsq[:, 0:B], AX.X, ALU.add))
                    nc.vector.tensor_scalar(qn[:], qn[:], TINY, None, ALU.add).then_inc(s["q_made"], 1)
                    nc.vector.tensor_tensor(qc[:, 0, :], w["qright"][:], w["right_sign"][:], ALU.mult)
                    ch.link(nc.vector.tensor_tensor(qc[:, 1, :], w["qleft"][:], w["left_sign"][:], ALU.mult))
                    ch.link(nc.vector.tensor_scalar(qc[:, 0, :], qc[:, 0, :], w["sgate"][:], None, ALU.mult))
                    dve.wait_ge(s["q_root"], 1)
                    ch.link(nc.vector.reciprocal(qn[:], qn[:]))
                    ch.link(nc.vector.tensor_tensor(qc[:], qc[:], qn[:].unsqueeze(2).to_broadcast([128, 2, 4]), ALU.mult))
                    for i in range(2):
                        last = nc.vector.tensor_tensor(side[:, i, :, :], w["same"][:].rearrange("p (c d) -> p c d", d=Q),
                                                       qc[:, i, :].unsqueeze(2).to_broadcast([128, 4, Q]), ALU.mult)
                    last.then_inc(s["sides_made"], 1)
                    dve.wait_ge(s["rot_made"], 1)
                    nc.vector.tensor_copy(rotT[:], s_ps[:, 0:D]).then_inc(s["rot_kept"], 1)

                def integers(i, name):
                    wide = wsc[:, i, :].unsqueeze(2).to_broadcast([128, HT, D])
                    ch.link(nc.vector.tensor_reduce(wsc[:, i, :], w[name][:], AX.X, ALU.max, apply_absolute_value=True))
                    ch.link(nc.vector.tensor_scalar(wsc[:, i, :], wsc[:, i, :], TINY, None, ALU.max))
                    ch.link(nc.vector.reciprocal(wsc[:, i, :], wsc[:, i, :]))
                    ch.link(nc.vector.tensor_scalar(wsc[:, i, :], wsc[:, i, :], W8, None, ALU.mult))
                    ch.link(nc.vector.tensor_tensor(wq[:, i, :, :], w[name][:], wide, ALU.mult))
                    ch.link(nc.vector.tensor_scalar(wq[:, i, :, :], wq[:, i, :, :], ROUND, None, ALU.add))
                    return nc.vector.tensor_scalar(wq[:, i, :, :], wq[:, i, :, :], ROUND, None, ALU.subtract)

                def output_weights():
                    ch.link(integers(1, "Wout2"))
                    ch.link(nc.vector.reciprocal(osc[:], wsc[:, 1, :]))
                    ch.link(nc.vector.tensor_tensor(wq[:, 1, :, :], wq[:, 1, :, :], osc[:].unsqueeze(2).to_broadcast([128, HT, D]), ALU.mult))

                def input_weights():
                    integers(0, "WinT").then_inc(s["win_made"], 1)
                    dve.wait_ge(s["win_turned"], 1)
                    nc.vector.tensor_copy(win[:].rearrange("p j h -> p (j h)"), ms_ps[:]).then_inc(s["win_kept"], 1)

                def feed(g):
                    dve.wait_ge(s["rl_kept"], g.n * HT + HT + 2)
                    nc.vector.tensor_tensor(f2[:, g.half, 0:2, :], rl[:, 0:2, :], rl[:, 0:2, :], ALU.mult).then_inc(s["f2_low"], 1)
                    dve.wait_ge(s["ms_made"], g.n + 1)
                    nc.vector.tensor_scalar(r2[:, g.half, :], ms_ps[:], EPS, None, ALU.add).then_inc(s["r2_kept"], 1)
                    dve.wait_ge(s["r2_kept"], g.n + 2)
                    nc.vector.reciprocal(r2[:, g.half, :], r2[:, g.half, :])

                def residual(g):
                    dve.wait_ge(s["x3b_kept"], g.n + 1)
                    dve.wait_ge(s["y_made"], g.n + 1)
                    nc.vector.tensor_tensor(x3[:, g.half, :], y_ps[:], r2[:, g.half, :], ALU.mult).then_inc(s["y_kept"], 1)
                    dve.wait_ge(s["y_kept"], g.n + 2)
                    dve.wait_ge(s["xs_made"], g.n + 1)
                    nc.vector.tensor_tensor(x3[:, g.half, :], x3[:, g.half, :], xs[:, g.half, :], ALU.add).then_inc(s["x3_kept"], 1)

                def keep_xr(g):
                    dve.wait_ge(s["xr_made"], g.n + 1)
                    nc.vector.memset(carry[:, g.half:g.half + 1], 0.0)
                    nc.vector.tensor_reduce(am[:, g.of(1)], r_ps[:], AX.X, ALU.max, apply_absolute_value=True)
                    nc.vector.tensor_copy(xr[:, g.of(GT)], r_ps[:]).then_inc(s["xr_kept"], 1)

                def scale(k):
                    if k == 0:
                        dve.wait_ge(s["xr_kept"], GROUPS + 1)
                    else:
                        dve.wait_ge(s["am_made"], GROUPS)
                    ch.link(nc.vector.tensor_reduce(peak[:], am[:], AX.X, ALU.max))
                    nc.vector.tensor_scalar(peak[:], peak[:], TINY, None, ALU.max).then_inc(s["peak_made"], 1)
                    dve.wait_ge(s["peak_turned"], k + 1)
                    nc.vector.tensor_reduce(one[:], s_ps[0:1, 0:128], AX.X, ALU.max).then_inc(s["one_made"], 1)
                    dve.wait_ge(s["one_spread"], k + 1)
                    ch.link(nc.vector.reciprocal(sc[:, k:k + 1], s_ps[:, 128:129]))
                    ch.link(nc.vector.tensor_scalar(sc[:, k:k + 1], sc[:, k:k + 1], A16, None, ALU.mult))

                def round_xr(g):
                    nc.vector.tensor_scalar(xr[:, g.of(GT)], xr[:, g.of(GT)], sc[:, 0:1], ROUND, ALU.mult, ALU.add).then_inc(s["xi_rounded"], 1)

                def hidden_peak(g):
                    dve.wait_ge(s["h_kept"], g.n + 3)
                    nc.vector.tensor_reduce(am[:, g.of(1)], hid[:, g.of(HT * GT)], AX.X, ALU.max, apply_absolute_value=True).then_inc(s["am_made"], 1)

                def round_hidden(g):
                    nc.vector.tensor_scalar(f2[:, g.half, :, :].rearrange("p j t -> p (j t)"), hid[:, g.of(HT * GT)], sc[:, 1:2], ROUND,
                                            ALU.mult, ALU.add).then_inc(s["t_made"], 1)

                def output(g):
                    dve.wait_ge(out_stored[g.half], g.stores)
                    dve.wait_ge(s["o_made"], g.n + 1)
                    nc.vector.memset(carry[:, g.half:g.half + 1], 0.0)
                    nc.vector.scalar_tensor_tensor(out[:, g.half, :], o_ps[g.half][:], isc[:], x3b[:, g.of(GT)], ALU.mult, ALU.add).then_inc(s["o_kept"], 1)

                nc.vector.memset(shift[:], -ROUND)
                quaternions()
                input_weights()
                for n in ("f2_low", "r2_kept", "y_kept", "xr_kept", "x3_kept", "x3_kept"):
                    dve.sem_inc(s[n], 1)
                groups(dve, feed, residual, keep_xr)
                scale(0)
                ch.link(nc.vector.tensor_scalar(gsc[:], wsc[:, 0, :], sc[:, 0:1], None, ALU.mult))
                nc.vector.reciprocal(gsc[:], gsc[:]).then_inc(s["scaled"], 1)
                all_groups(dve, round_xr)
                output_weights()
                all_groups(dve, hidden_peak)
                scale(1)
                ch.link(nc.vector.reciprocal(isc[:], sc[:, 1:2]))
                dve.wait_ge(s["x3b_kept"], GROUPS + 2)
                groups(dve, round_hidden, output)


SHARED = {"ident": (128, 128), "ones": (128, 128), "mean": (128, 128)}
HEADS = {"headmask": (128, 16), "quartermask": (128, 4, 128), "condT": (32, 32)}
MIXING = {"raw": (32, 64), "OBT": (128, 64), "WqkvT": (128, 384), "wg1": (128, 8), "rms_w": (128, 1), "wgb": (1, 8),
          "ggb": (1, 8), "ggW": (32, 8), "ibT": (128, 32), "by8": (128, 128), "WoT": (128, 128),
          "gnw": (128, 1), "gnb": (128, 1), "decay": (128, 16, 128), "condTp": (32, 36), "rankTp": (64, 36)}
EXPERTS = {"W1": (128, 8, 256), "W2": (128, 8, 2, 256), "W3": (128, 8, 2, 128), "b1": (128, 8, 2), "b2": (128, 8, 2),
           "b3": (8, 128), "wg2": (128, 8), "F1": (128, 8, 512), "F2": (128, 8, 4, 128), "fb1": (128, 8, 4), "fb2": (8, 128)}
FIELDS = {"Wc1cT": (32, 128), "Wc1xT": (128, 128), "We1T": (32, 128), "We2T": (128, 128), "be2": (1, 128), "be1": (128, 1),
          "bc1": (128, 1), "lng": (32, 128), "lnb": (32, 128), "peT": (128, 128), "Alog": (128, 8), "WqT1": (128, 128),
          "WkT1": (128, 128), "WvT1": (128, 128), "bq": (128, 1), "bk": (128, 1), "bvb": (128, 128), "Wc2T": (128, 16),
          "bc2b": (128, 16), "WoutT": (128, 128), "bout": (128, 1), "eps6": (128, 1), "Wba": (128, 16), "dtb": (128, 8)}
DELTA = {"dWq": (128, 1024), "dWk": (128, 1024), "dWv": (128, 1024), "dWg": (128, 1024), "dWo": (128, 8, 128),
         "onw": (128, 128), "offblock": (128, 128), "headrow": (128, 2, 32), "headpick": (128, 8)}
LAST = {"Wfc": (128, 512), "Wproj": (128, 4, 128), "qleft_all": (128, 32), "qright": (128, 4), "qleft": (128, 4),
        "right_sign": (128, 4), "left_sign": (128, 4), "sgate": (128, 1), "same": (128, 128), "WinT": (128, 4, 128),
        "Wout2": (128, 4, 128), "bin": (128, 4), "bout2": (128, 1)}
BASIS = ("raw", "OBT", "WqkvT", "ones", "wg1", "rms_w", "wgb", "ggb", "condT", "ggW", "ident")
KEPT = {"wg1": (128, 8), "obw": (64, 384), "gball": (128, GB + B, 8), "mtr": (32, 64), "c1b": (128, 2 * GB + B), "expA": (128, 8), "bqs": (128, 1)}
INPUTS = {"xT": (GROUPS + 2, 128, GT), **SHARED, **HEADS, **MIXING, **EXPERTS, **FIELDS, **DELTA, **LAST}


def program(nc, I, outT):
    dram = {"xT": I["xT"], "outT": outT}
    for name, shape in (("x1T", (GROUPS + 3, 128, GT)), ("x2T", (GROUPS + 3, 128, GT)), ("mT", (GROUPS + 2, 128, GT)),
                        ("cw1", (GROUPS + 2, NE, GT)), ("cw2", (GROUPS + 2, NE, GT)), ("fa", (2 * GB + B, T)),
                        ("aT", (GROUPS + 2, 128, GT)), ("hT", (GROUPS + 2, 128, GT)), ("beta", (GROUPS + 2, T, 32)),
                        ("alpha", (GROUPS + 2, 32, T)), ("lanes", (2, 4, 32, 32, 32)), ("inverses", (2, 4, 32, 32, 32)),
                        ("xpT", (GROUPS + 2, 128, GT))):
        dram[name] = nc.dram_tensor(name, shape, F32, kind="Internal").ap()
    w, c = {"raw_dram": I["raw"]}, {}

    def place(ctx, names):
        for name, shape in names.items():
            w[name] = ctx.enter_context(nc.sbuf_tensor(f"w_{name}", shape, F32))

    first = {**MIXING, **SHARED, **HEADS}
    sets = {"basis": {name: first.pop(name) for name in BASIS}, "mixing": first, "experts": EXPERTS, "fields": FIELDS, "delta": DELTA, "last": LAST}
    loaded = {k: nc.alloc_semaphore(f"{k}_loaded") for k in sets}

    def start(sp, *names):
        for k in names:
            for name in sets[k]:
                sp.dma_start(w[name][:], I[name]).then_inc(loaded[k], 16)

    def arrived(k, started=True):
        with nc.Block() as block:
            @block.sync
            def _(sp):
                if not started:
                    start(sp, k)
                sp.wait_ge(loaded[k], 16 * len(sets[k]))

    with ExitStack() as layer1:
        place(layer1, SHARED)
        place(layer1, DELTA)
        with ExitStack() as field:
            for name, shape in KEPT.items():
                c[name] = field.enter_context(nc.sbuf_tensor(f"c_{name}", shape, F32))
            place(field, HEADS)
            place(field, FIELDS)
            with ExitStack() as layer0:
                place(layer0, EXPERTS)
                with ExitStack() as mixing:
                    place(mixing, MIXING)
                    arrived("basis", started=False)
                    mixing_basis(nc, w, c, lambda sp: start(sp, "mixing", "experts", "fields", "delta"))
                    arrived("mixing")
                    retention(nc, w, c, dram)
                arrived("experts")
                moe_first(nc, w, dram)
                moe_second(nc, w, dram)
            arrived("fields")
            field_basis(nc, w, c, dram)
            field_attention(nc, w, c, dram)
        arrived("delta")
        delta_rule(nc, w, dram)
        place(layer1, LAST)
        arrived("last", started=False)
        last_layer(nc, w, dram)


def laid_out(i):
    f = np.float32
    turned = lambda z: np.ascontiguousarray(z.T)
    column = lambda z: z[:, None]
    tiles = lambda z, n: z.reshape(n, 128, -1).transpose(1, 0, 2)
    rows = lambda z, n=128: np.broadcast_to(z[None], (n, z.shape[0]))
    behind = lambda z: np.concatenate([z, np.zeros((z.shape[0], GB), f)], 1)
    eye = np.eye(128, dtype=f)
    head, pos, block = np.arange(128) // 8, np.arange(T), np.arange(T) // 32
    a = {}
    xT = i["x"].reshape(GROUPS, GT, D).transpose(0, 2, 1)
    a["xT"] = np.concatenate([xT, np.zeros((2, D, GT), f)])
    a["ident"], a["ones"], a["mean"] = eye, np.ones((128, 128), f), np.full((128, 128), 1 / D, f)
    a["headmask"] = (head[:, None] == np.arange(16)[None]).astype(f)
    a["quartermask"] = np.broadcast_to((head[None] % 4 == np.arange(4)[:, None]).astype(f), (128, 4, 128))
    a["condT"] = turned(i["cond_256"])
    a["raw"], a["OBT"], a["ibT"] = i["L0_cond_mode_to_rank"], turned(i["L0_cond_output_basis"]), turned(i["L0_cond_input_basis"])
    a["WqkvT"] = np.concatenate([i["L0_attn_W_" + k].T for k in "qkv"], 1)
    a["wg1"], a["rms_w"], a["ggW"] = i["L0_cond2_wg_W"], column(i["L0_cond2_rms_w"]), i["L0_cond2_gg_W"]
    a["wgb"], a["ggb"] = i["L0_cond2_wg_b"][None], i["L0_cond2_gg_b"][None]
    a["by8"] = ((head[:, None] == head[None]) / 8).astype(f)
    a["WoT"], a["gnw"], a["gnb"] = turned(i["L0_attn_W_o"]), column(i["L0_attn_gn_weight"]), column(i["L0_attn_gn_bias"])
    gamma = (1 - 2.0 ** (-5.0 - np.arange(16)))[None, :, None]
    ahead = (pos[None] - pos[:, None])[:, None, :]
    a["decay"] = np.where(ahead >= 0, gamma ** np.maximum(ahead, 0) / np.sqrt(8.0), 0.0).astype(f)
    a["condTp"], a["rankTp"] = behind(i["cond_256"].T), behind(i["cond_64"].T)
    a["W1"], a["b3"] = i["L0_cond2_W1"].transpose(1, 0, 2), i["L0_cond2_b3"]
    a["W2"] = i["L0_cond2_W2"].reshape(NE, 2, 128, 256).transpose(2, 0, 1, 3)
    a["W3"] = i["L0_cond2_W3"].reshape(NE, 2, 128, D).transpose(2, 0, 1, 3)
    a["b1"], a["b2"] = (i["L0_cond2_" + k].reshape(NE, 2, 128).transpose(2, 0, 1) for k in ("b1", "b2"))
    a["wg2"], a["fb2"] = turned(i["L0_ffn_w_gate"]), i["L0_ffn_b2"]
    a["F1"] = i["L0_ffn_W1"].transpose(1, 0, 2)
    a["F2"] = i["L0_ffn_W2"].reshape(NE, 4, 128, D).transpose(2, 0, 1, 3)
    a["fb1"] = i["L0_ffn_b1"].reshape(NE, 4, 128).transpose(2, 0, 1)
    Wc1, Wqkv, bqkv = i["L1_cond_Wc1"], i["L1_cond_Wqkv"], i["L1_cond_bqkv"]
    a["Wc1xT"], a["Wc1cT"] = turned(Wc1[:, :D]), turned(Wc1[:, D:])
    a["We1T"], a["We2T"], a["Wc2T"], a["WoutT"] = (turned(i["L1_cond_" + k]) for k in ("We1", "We2", "Wc2", "Wout"))
    a["be2"], a["be1"], a["bc1"] = i["L1_cond_be2"][None], column(i["L1_cond_be1"]), column(i["L1_cond_bc1"])
    a["lng"], a["lnb"] = rows(i["L1_cond_ln_g"], B), rows(i["L1_cond_ln_b"], B)
    inv = f(10000.0) ** np.repeat(np.arange(0, D, 2, dtype=f) / f(D), 2)
    a["peT"] = turned(np.sin((pos.astype(f)[:, None] / inv[None]).astype(f)).astype(f))
    a["WqT1"], a["WkT1"], a["WvT1"] = (turned(Wqkv[k * D:(k + 1) * D]) for k in range(3))
    a["bq"], a["bk"], a["bvb"] = column(bqkv[:D]), column(bqkv[D:2 * D]), rows(bqkv[2 * D:])
    a["bc2b"], a["bout"] = rows(i["L1_cond_bc2"]), column(i["L1_cond_bout"])
    a["eps6"], a["Alog"], a["dtb"] = np.full((128, 1), 1e-6, f), rows(i["L1_attn_A_log"]), rows(i["L1_attn_dt_bias"])
    a["Wba"] = np.concatenate([i["L1_attn_Wb"], i["L1_attn_Wa"]], 1)
    for k in "qkvg":
        a["dW" + k] = i["L1_attn_W" + k]
    a["dWo"], a["onw"] = tiles(i["L1_attn_Wo"], 8), rows(i["L1_attn_o_norm_w"])
    a["offblock"] = (block[None] > block[:, None]).astype(f)
    a["headrow"] = np.broadcast_to(np.eye(32, dtype=f)[:2][None], (128, 2, 32))
    quarter, place, heads = np.arange(128)[:, None] // 32, np.arange(128)[:, None] % 32, np.arange(8)[None]
    a["headpick"] = ((quarter == heads % 4) & (place == heads // 4)).astype(f)
    a["Wfc"], a["Wproj"] = i["L1_attn_W_fc"], tiles(i["L1_attn_W_proj"], 4)
    part = np.arange(4)[:, None] ^ np.arange(4)[None]
    spread = lambda q: q[part].transpose(0, 2, 1).reshape(128, 4)
    right = np.array([[1, -1, -1, -1], [1, 1, 1, -1], [1, -1, 1, 1], [1, 1, -1, 1]], f) * np.where(part > 0, -1, 1)
    left = np.array([[1, 1, 1, 1], [-1, 1, 1, -1], [-1, -1, 1, 1], [-1, 1, -1, 1]], f)
    a["right_sign"], a["left_sign"] = np.repeat(right, 32, 0).astype(f), np.repeat(left, 32, 0)
    a["qright"], a["qleft"] = spread(i["L1_cond2_q_right"]), spread(i["cond_256"][:4])
    a["qleft_all"] = np.tile(i["cond_256"].T, (4, 1))
    a["sgate"] = np.tile(i["L1_cond2_spectral_gate"].reshape(32), 4)[:, None]
    a["same"] = np.tile(np.eye(32, dtype=f), (4, 4))
    a["WinT"], a["Wout2"] = tiles(i["L1_ffn_W_in"].T, 4), tiles(i["L1_ffn_W_out"], 4)
    a["bin"], a["bout2"] = turned(i["L1_ffn_b_in"].reshape(4, 128)), column(i["L1_ffn_b_out"])
    return a


def kernel(**inputs):
    import concourse.bacc as bacc
    from concourse.bass_utils import run_bass_kernel_spmd

    a = laid_out({k: np.asarray(v) for k, v in inputs.items()})
    arrays = {f"in_{k}_dram": np.ascontiguousarray(a[k]) for k in INPUTS}
    nc = bacc.Bacc("TRN2", target_bir_lowering=False, num_devices=1)
    I = {k: nc.dram_tensor(f"in_{k}_dram", shape, F32, kind="ExternalInput").ap() for k, shape in INPUTS.items()}
    outT = nc.dram_tensor("out_0_dram", (GROUPS, D, GT), F32, kind="ExternalOutput").ap()
    program(nc, I, outT)
    r = run_bass_kernel_spmd(nc, [arrays], core_ids=[0])
    return np.ascontiguousarray(r.results[0]["out_0_dram"].transpose(0, 2, 1)).reshape(B, T, D)
```
